# Optimizing a Trainium2 kernel written in Bass

```python
import numpy as np
import jax
import jax.numpy as jnp

def _softmax(x, axis=-1):
    return jax.nn.softmax(x, axis=axis)

def _gelu(x):
    return jax.nn.gelu(x, approximate=True)

def _silu(x):
    return jax.nn.silu(x)

def _sigmoid(x):
    return jax.nn.sigmoid(x)

def _layernorm(x, axis=-1, eps=1e-05):
    m = jnp.mean(x, axis=axis, keepdims=True)
    v = jnp.var(x, axis=axis, keepdims=True)
    return (x - m) / jnp.sqrt(v + eps)

def _scatter_add(tgt, idx, src, axis=0):
    return tgt.at[idx].add(src)

def _segment_sum(src, seg, n):
    return jax.ops.segment_sum(src, seg, n)
kernel_name = 'mk_decoder_postln_d1_seqx_r8_e4369f'

def setup_inputs(seed: int=0):
    np.random.seed(seed)
    _w = jnp.asarray

    def _rec_inputs():
        import jax
        import jax.numpy as jnp
        _rk = jax.random.key(seed)
        x = -0.0002928 + 1 * jax.random.normal(jax.random.fold_in(_rk, 1), (16, 256, 128), jnp.float32)
        _lenS = 256 - jax.random.randint(jax.random.fold_in(_rk, 7), (16,), 0, max(1, 256 // 4) + 1, jnp.int32)
        _lenS2 = 64 - jax.random.randint(jax.random.fold_in(_rk, 8), (16,), 0, max(1, 64 // 4) + 1, jnp.int32)
        _ctx_512P = jax.random.normal(jax.random.fold_in(_rk, 11), (16, 16, 64), jnp.float32)
        _ctx_512c = jax.random.dirichlet(jax.random.fold_in(_rk, 511), 0.3 * jnp.ones((16,), jnp.float32), (16, 64))
        _ctx_512t = jnp.einsum('bsk,bkd->bsd', _ctx_512c, _ctx_512P)
        _ctx_512t = _ctx_512t * jax.lax.rsqrt(jnp.mean(jnp.square(_ctx_512t)) + 1e-12) * 0.953939
        ctx_512 = 0.00222621 + 0.99962 * (_ctx_512t + 0.3 * jax.random.normal(jax.random.fold_in(_rk, 611), (16, 64, 64), jnp.float32))
        return (x, ctx_512)
    x, ctx_512 = _rec_inputs()

    def _L0_attn_setup():
        import jax, jax.numpy as jnp
        import numpy as np
        E = 128
        H = 16
        D = E // H
        LOCAL_WINDOW = 5
        GATING_THRESHOLD = 0.0
        GAUSS_SIGMA = 2.0
        PERIODIC_STRENGTH = 1.0
        PERIOD = 401.0
        NEG = -1000000000.0
        key = jax.random.key(seed)
        ks = jax.random.split(key, 9)
        B, S = (2, 256)
        sc = 1.0 / np.sqrt(E)
        inp = {'x': jax.random.normal(ks[0], (B, S, E), dtype=jnp.float32), 'wq': jax.random.normal(ks[1], (E, E), dtype=jnp.float32) * sc, 'bq': jnp.zeros((E,), dtype=jnp.float32), 'wk': jax.random.normal(ks[2], (E, E), dtype=jnp.float32) * sc, 'bk': jnp.zeros((E,), dtype=jnp.float32), 'wv': jax.random.normal(ks[3], (E, E), dtype=jnp.float32) * sc, 'bv': jnp.zeros((E,), dtype=jnp.float32), 'wo': jax.random.normal(ks[4], (E, E), dtype=jnp.float32) * sc, 'bo': jnp.zeros((E,), dtype=jnp.float32)}
        return inp
    _L0_attn_all = _L0_attn_setup()
    _L0_attn_in = {k: v for k, v in _L0_attn_all.items() if k in ('wq', 'bq', 'wk', 'bk', 'wv', 'bv', 'wo', 'bo')}
    del _L0_attn_all

    def _L0_xattn_setup():
        import jax, jax.numpy as jnp
        import numpy as np
        B, T, TC, C, CC, H = (2, 256, 64, 128, 64, 16)
        D = C // H

        def _heads(t):
            b, l, _ = t.shape
            return t.reshape(b, l, H, D).transpose(0, 2, 1, 3)
        key = jax.random.key(seed)
        ks = jax.random.split(key, 18)
        w = lambda k, i, o: jax.random.normal(k, (i, o), jnp.float32) / np.sqrt(i).astype(np.float32)
        return {'x': jax.random.normal(ks[0], (B, T, C), jnp.float32), 'cross_input': jax.random.normal(ks[1], (B, TC, CC), jnp.float32), 'Wk': w(ks[2], C, C), 'bk': jnp.zeros((C,), jnp.float32), 'Wq': w(ks[3], C, C), 'bq': jnp.zeros((C,), jnp.float32), 'Wv': w(ks[4], C, C), 'bv': jnp.zeros((C,), jnp.float32), 'Wck': w(ks[5], CC, C), 'bck': jnp.zeros((C,), jnp.float32), 'Wcq': w(ks[6], C, C), 'bcq': jnp.zeros((C,), jnp.float32), 'Wcv': w(ks[7], CC, C), 'bcv': jnp.zeros((C,), jnp.float32), 'Wp': w(ks[8], C, C), 'bp': jnp.zeros((C,), jnp.float32)}
    _L0_xattn_all = _L0_xattn_setup()
    _L0_xattn_in = {k: v for k, v in _L0_xattn_all.items() if k in ('Wk', 'bk', 'Wq', 'bq', 'Wv', 'bv', 'Wck', 'bck', 'Wcq', 'bcq', 'Wcv', 'bcv', 'Wp', 'bp')}
    del _L0_xattn_all

    def _L0_ffn_setup():
        import jax, jax.numpy as jnp
        import numpy as np
        DIM = 128
        HIDDEN = 384
        SCALE = 1.0 / 127.0

        def _dequant(w_int, dtype):
            return w_int.astype(dtype) * jnp.asarray(SCALE, dtype)
        key = jax.random.key(seed)
        k_x, k_g, k_u, k_d = jax.random.split(key, 4)
        x = jax.random.normal(k_x, (4, 256, DIM), dtype=jnp.float32)
        w_gate = jax.random.randint(k_g, (HIDDEN, DIM), -127, 128, dtype=jnp.int32)
        w_up = jax.random.randint(k_u, (HIDDEN, DIM), -127, 128, dtype=jnp.int32)
        w_down = jax.random.randint(k_d, (DIM, HIDDEN), -127, 128, dtype=jnp.int32)
        return {'x': x, 'w_gate': w_gate, 'w_up': w_up, 'w_down': w_down}
    _L0_ffn_all = _L0_ffn_setup()
    _L0_ffn_in = {k: v for k, v in _L0_ffn_all.items() if k in ('w_gate', 'w_up', 'w_down')}
    del _L0_ffn_all
    return {'x': x, 'ctx_512': ctx_512, 'L0_attn_wq': _L0_attn_in['wq'], 'L0_attn_bq': _L0_attn_in['bq'], 'L0_attn_wk': _L0_attn_in['wk'], 'L0_attn_bk': _L0_attn_in['bk'], 'L0_attn_wv': _L0_attn_in['wv'], 'L0_attn_bv': _L0_attn_in['bv'], 'L0_attn_wo': _L0_attn_in['wo'], 'L0_attn_bo': _L0_attn_in['bo'], 'L0_xattn_Wk': _L0_xattn_in['Wk'], 'L0_xattn_bk': _L0_xattn_in['bk'], 'L0_xattn_Wq': _L0_xattn_in['Wq'], 'L0_xattn_bq': _L0_xattn_in['bq'], 'L0_xattn_Wv': _L0_xattn_in['Wv'], 'L0_xattn_bv': _L0_xattn_in['bv'], 'L0_xattn_Wck': _L0_xattn_in['Wck'], 'L0_xattn_bck': _L0_xattn_in['bck'], 'L0_xattn_Wcq': _L0_xattn_in['Wcq'], 'L0_xattn_bcq': _L0_xattn_in['bcq'], 'L0_xattn_Wcv': _L0_xattn_in['Wcv'], 'L0_xattn_bcv': _L0_xattn_in['bcv'], 'L0_xattn_Wp': _L0_xattn_in['Wp'], 'L0_xattn_bp': _L0_xattn_in['bp'], 'L0_ffn_w_gate': _L0_ffn_in['w_gate'], 'L0_ffn_w_up': _L0_ffn_in['w_up'], 'L0_ffn_w_down': _L0_ffn_in['w_down']}

def reference(x, ctx_512, L0_attn_wq, L0_attn_bq, L0_attn_wk, L0_attn_bk, L0_attn_wv, L0_attn_bv, L0_attn_wo, L0_attn_bo, L0_xattn_Wk, L0_xattn_bk, L0_xattn_Wq, L0_xattn_bq, L0_xattn_Wv, L0_xattn_bv, L0_xattn_Wck, L0_xattn_bck, L0_xattn_Wcq, L0_xattn_bcq, L0_xattn_Wcv, L0_xattn_bcv, L0_xattn_Wp, L0_xattn_bp, L0_ffn_w_gate, L0_ffn_w_up, L0_ffn_w_down):
    import jax
    import jax.numpy as jnp

    def _L0_attn_ref(x, wq, bq, wk, bk, wv, bv, wo, bo):
        import jax, jax.numpy as jnp
        import numpy as np
        E = 128
        H = 16
        D = E // H
        LOCAL_WINDOW = 5
        GATING_THRESHOLD = 0.0
        GAUSS_SIGMA = 2.0
        PERIODIC_STRENGTH = 1.0
        PERIOD = 401.0
        NEG = -1000000000.0
        B, S, _ = x.shape
        q = (x @ wq.T + bq).reshape(B, S, H, D).transpose(0, 2, 1, 3)
        k = (x @ wk.T + bk).reshape(B, S, H, D).transpose(0, 2, 1, 3)
        v = (x @ wv.T + bv).reshape(B, S, H, D).transpose(0, 2, 1, 3)
        scores = jnp.einsum('bhid,bhjd->bhij', q, k) / jnp.sqrt(jnp.float32(D))
        idx = jnp.arange(S)
        dist = idx[:, None] - idx[None, :]
        local_mask = jnp.abs(dist) <= LOCAL_WINDOW // 2
        glob = (idx[:, None] == 0) | (idx[None, :] == 0)
        attn_mask = local_mask | glob
        scores = jnp.where(attn_mask[None, None], scores, NEG)
        diff = dist.astype(jnp.float32)
        pos_bias = jnp.exp(-0.5 * (diff / GAUSS_SIGMA) ** 2) + PERIODIC_STRENGTH * jnp.cos(2.0 * jnp.pi * diff / PERIOD)
        scores = scores + pos_bias[None, None]
        scores = jnp.where(scores < GATING_THRESHOLD, NEG, scores)
        probs = jax.nn.softmax(scores, axis=-1)
        ctx = jnp.einsum('bhij,bhjd->bhid', probs, v)
        ctx = ctx.transpose(0, 2, 1, 3).reshape(B, S, E)
        return ctx @ wo.T + bo

    def _L0_xattn_ref(x, cross_input, Wk, bk, Wq, bq, Wv, bv, Wck, bck, Wcq, bcq, Wcv, bcv, Wp, bp):
        import jax, jax.numpy as jnp
        import numpy as np
        B, T, TC, C, CC, H = (2, 256, 64, 128, 64, 16)
        D = C // H

        def _heads(t):
            b, l, _ = t.shape
            return t.reshape(b, l, H, D).transpose(0, 2, 1, 3)
        scale = np.float32(1.0 / np.sqrt(D))
        q = _heads(x @ Wq + bq)
        k = _heads(x @ Wk + bk)
        v = _heads(x @ Wv + bv)
        att = jnp.einsum('bhqd,bhkd->bhqk', q, k) * scale
        causal = jnp.tril(jnp.ones((T, T), bool))
        att = jnp.where(causal[None, None], att, -jnp.inf)
        y = jnp.einsum('bhqk,bhkd->bhqd', jax.nn.softmax(att, axis=-1), v)
        qc = _heads(x @ Wcq + bcq)
        kc = _heads(cross_input @ Wck + bck)
        vc = _heads(cross_input @ Wcv + bcv)
        attc = jnp.einsum('bhqd,bhkd->bhqk', qc, kc) * scale
        y = y + jnp.einsum('bhqk,bhkd->bhqd', jax.nn.softmax(attc, axis=-1), vc)
        y = y.transpose(0, 2, 1, 3).reshape(x.shape[0], T, C)
        return y @ Wp + bp

    def _L0_ffn_ref(x, w_gate, w_up, w_down):
        import jax, jax.numpy as jnp
        import numpy as np
        DIM = 128
        HIDDEN = 384
        SCALE = 1.0 / 127.0

        def _dequant(w_int, dtype):
            return w_int.astype(dtype) * jnp.asarray(SCALE, dtype)
        wg = _dequant(w_gate, x.dtype)
        wu = _dequant(w_up, x.dtype)
        wd = _dequant(w_down, x.dtype)
        gate = jnp.einsum('bsd,hd->bsh', x, wg)
        up = jnp.einsum('bsd,hd->bsh', x, wu)
        h = jax.nn.silu(gate) * up
        return jnp.einsum('bsh,dh->bsd', h, wd)
    x = _layernorm(x + _L0_attn_ref(x, L0_attn_wq, L0_attn_bq, L0_attn_wk, L0_attn_bk, L0_attn_wv, L0_attn_bv, L0_attn_wo, L0_attn_bo), axis=-1)
    x = _layernorm(x + _L0_xattn_ref(x, ctx_512, L0_xattn_Wk, L0_xattn_bk, L0_xattn_Wq, L0_xattn_bq, L0_xattn_Wv, L0_xattn_bv, L0_xattn_Wck, L0_xattn_bck, L0_xattn_Wcq, L0_xattn_bcq, L0_xattn_Wcv, L0_xattn_bcv, L0_xattn_Wp, L0_xattn_bp), axis=-1)
    x = _layernorm(x + _L0_ffn_ref(x, L0_ffn_w_gate, L0_ffn_w_up, L0_ffn_w_down), axis=-1)
    return x

_drawn_inputs = setup_inputs


def setup_inputs(seed=0):
    import zlib

    import numpy as np

    out = dict(_drawn_inputs(seed))
    spreads = {'L0_attn_bq': (0.0, 0.1),
     'L0_attn_bk': (0.0, 0.719),
     'L0_attn_bv': (0.0, 0.1),
     'L0_attn_bo': (0.0, 0.1),
     'L0_xattn_bk': (0.0, 0.8),
     'L0_xattn_bq': (0.0, 0.296),
     'L0_xattn_bv': (0.0, 0.1),
     'L0_xattn_bck': (0.0, 0.8),
     'L0_xattn_bcq': (0.0, 0.1),
     'L0_xattn_bcv': (0.0, 0.1),
     'L0_xattn_bp': (0.0, 0.1)}
    factors = {}
    for name, (base, spread) in spreads.items():
        noise = np.random.default_rng([zlib.crc32(name.encode()), seed]).standard_normal(out[name].shape)
        drawn = base * np.exp(spread * noise) if base else spread * noise
        out[name] = jnp.asarray(drawn.astype(out[name].dtype))
    for name, factor in factors.items():
        out[name] = (out[name] * factor).astype(out[name].dtype)
    return out
```

```python
import concourse.bass as bass
from concourse import mybir
from contextlib import ExitStack

B, S, E, H, D = 16, 256, 128, 16, 8
SC, CC, HID = 64, 64, 384
P = 128
NT = S // P
PAIRS = H // 2
TERMS = 6
ROWS = 2 * D * TERMS
KROWS = ROWS + 4
WIN = 5
CAND = WIN + 1
SCALE = float(D) ** -0.5
EPS = 1e-5
NEG = -1e9
NBUF = 3

LAG = {"local": 0, "project": 1, "rowmax": 2, "attend": 3, "tail": 4}
SLOTS = [
    ["local.load", "tail.self0", "project.qk", "attend.0", "rowmax.0"],
    ["tail.cross", "project.v", "attend.1", "rowmax.1"],
    ["tail.self1", "project.parts", "attend.2", "rowmax.2", "local.qkv"],
    ["tail.y", "attend.3", "pv.self0", "rowmax.3", "local.products"],
    ["tail.proj", "attend.4", "pv.cross0", "rowmax.4", "local.scores"],
    ["tail.norm2", "attend.5", "pv.self1", "rowmax.5", "local.exp"],
    ["tail.x2t", "attend.6", "rowmax.6", "local.probs", "local.spread0"],
    ["tail.up0", "attend.7", "pv.self2", "rowmax.7", "local.spread1"],
    ["tail.up1", "rowmax.shift", "local.spread2", "local.context"],
    ["tail.up2", "pv.self3", "local.out"],
    ["tail.down", "pv.cross1", "local.norm1"],
    ["tail.norm3", "local.x1t"],
]
STEP_PHASE = {"pv": "attend"}


class Batch:

    def __init__(self, loop, offset):
        self.loop, self.offset, self.buf = loop, offset, offset % NBUF

    def count(self, each, add):
        value = self.offset * each + add
        return value if self.loop is None else self.loop * (NBUF * each) + value

    def reaches(self, each, add):
        return self.loop is not None or self.offset * each + add > 0

    def index(self):
        return self.count(1, 0)


def pipeline(eng, steps):
    def iteration(loop, n):
        for slot in SLOTS:
            for name in slot:
                phase, _, arg = name.partition(".")
                k = n - LAG[STEP_PHASE.get(phase, phase)]
                if loop is None and not 0 <= k < B:
                    continue
                if name in steps:
                    steps[name](Batch(loop, k))
                elif phase in steps:
                    steps[phase](Batch(loop, k), arg)
    first = max(LAG.values()) + 1
    full = (B - first) // NBUF * NBUF
    for n in range(first):
        iteration(None, n)
    with eng.Fori(0, full // NBUF) as i:
        for r in range(NBUF):
            iteration(i, first + r)
    for n in range(first + full, B + first - 1):
        iteration(None, n)


def decoder_layer(nc, x, xt, ctxt, w1, w2, wck, wcv, bias_cols, bias_rows, wgu, wd, k_f32, k_bias, k_spread, k_bf16, k_rows, out):
    k_bf16, k_rows = k_bf16.bitcast(mybir.dt.bfloat16), k_rows.bitcast(mybir.dt.bfloat16)
    f32, bf16, i32 = mybir.dt.float32, mybir.dt.bfloat16, mybir.dt.int32
    ALU, ACT = mybir.AluOpType, mybir.ActivationFunctionType
    X = mybir.AxisListType.X
    QC = 2 * S
    COLS = QC + S + SC

    parts_dram = nc.dram_tensor("parts_dram", [P, TERMS, COLS], bf16).ap()

    stack = ExitStack()
    with stack:
        def sb(name, shape, dt=f32):
            return stack.enter_context(nc.sbuf_tensor(name, shape, dt))

        def ps(name, shape=(P, 512)):
            return stack.enter_context(nc.psum_tensor(name, list(shape), f32))

        def sem(name):
            return stack.enter_context(nc.semaphore(name))

        w1_sb = sb("w1_sb", [P, 4, E])
        w2_sb = sb("w2_sb", [P, 5, E])
        wck_sb = sb("wck_sb", [CC, E])
        wcv_sb = sb("wcv_sb", [CC, E])
        wgu_int = sb("wgu_int", [P, 2 * HID], i32)
        wd_int = sb("wd_int", [P, 3, E], i32)
        wgu_sb = sb("wgu_sb", [P, 2 * HID])
        wd_sb = sb("wd_sb", [P, 3, E])
        cols = sb("cols", [P, 9])
        rows = sb("rows", [P, 2, E])
        consts = sb("consts", [P, 2 * P + H])
        cand_bias = sb("cand_bias", [P, CAND * NT * H])
        row0_bias = sb("row0_bias", [P, S])
        spread = sb("spread", [(CAND + 1) * H, CAND + 1, P])
        const16 = sb("const16", [P, 3 * P], bf16)
        small = sb("small", [P, 4])
        bv_both = sb("bv_both", [P, 1])
        bv_wide = sb("bv_wide", [P, P])
        bp_eff = sb("bp_eff", [P, E])
        ident, same_head, head_of = consts[:, 0:P], consts[:, P:2 * P], consts[:, 2 * P:2 * P + H]
        ident16, causal_q, causal_k = const16[:, 0:P], const16[:, P:2 * P], const16[:, 2 * P:3 * P]

        x_sb = sb("x_sb", [P, NBUF, NT, E])
        xt_sb = sb("xt_sb", [P, NBUF, S])
        ctxt_sb = sb("ctxt_sb", [CC, NBUF, 2 * SC])
        xb = sb("xb", [P, NT, E])
        q1 = sb("q1", [P, S])
        k1 = sb("k1", [P, S + WIN - 1])
        v1 = sb("v1", [P, S + WIN - 1])
        v1_sum = sb("v1_sum", [P, 1])
        prod = sb("prod", [P, WIN, S])
        k0_heads = sb("k0_heads", [P, H])
        q0_heads = sb("q0_heads", [P, P])
        lsc = sb("lsc", [P, CAND, NT * H])
        lmax = sb("lmax", [P, NT * H])
        lneg = sb("lneg", [P, CAND, NT * H])
        lexp = sb("lexp", [P, CAND, NT * H])
        lgated = sb("lgated", [P, CAND, NT * H])
        lsum = sb("lsum", [P, NT * H])
        lnone = sb("lnone", [P, NT * H])
        lden = sb("lden", [P, NT * H])
        lrec = sb("lrec", [P, NT * H])
        probs = sb("probs", [P, NT, CAND + 1, H])
        probs_t = sb("probs_t", [(CAND + 1) * H, S])
        r0s = sb("r0s", [P, S])
        r0g = sb("r0g", [P, S])
        r0v = sb("r0v", [P, S])
        r0max = sb("r0max", [P, 1])
        r0exp = sb("r0exp", [P, S])
        r0sum = sb("r0sum", [P, 1])
        r0pv = sb("r0pv", [P, S])
        r0num = sb("r0num", [P, 1])
        r0rec = sb("r0rec", [P, 1])
        pv01 = sb("pv01", [P, 2, S])
        pv23 = sb("pv23", [P, 2, S])
        pv4 = sb("pv4", [P, S])
        pv5 = sb("pv5", [P, S])
        pv6 = sb("pv6", [P, S])
        pvsum = sb("pvsum", [P, 2, S])
        pvall = sb("pvall", [P, S])
        lctx = sb("lctx", [P, S])
        res1 = sb("res1", [P, NT, E])
        x1 = sb("x1", [P, NBUF, NT, E])
        x1t = sb("x1t", [P, NBUF, S])

        parts = sb("parts", [P, 3, COLS], bf16)
        rest = sb("rest", [P, COLS])
        q_st = sb("q_st", [KROWS, NBUF, PAIRS, QC], bf16)
        k_st = sb("k_st", [KROWS, NBUF, PAIRS, 2, S], bf16)
        kc_st = sb("kc_st", [KROWS, NBUF, PAIRS, 2 * SC], bf16)
        v_sb = sb("v_sb", [P, NBUF, NT, H, 32])
        vc_sb = sb("vc_sb", [P, NBUF, PAIRS, 32])

        rmax = sb("rmax", [P, NT, 2, H])
        rneg = sb("rneg", [P, 2, PAIRS, 2, NT])
        shift = sb("shift", [P, 2, 2, PAIRS, 2, NT], bf16)
        shift_t = sb("shift_t", [P, P], bf16)
        x1res = sb("x1res", [P, NBUF, NT, E])

        RING, CRING = 8, 4
        p_self = sb("p_self", [P, RING, 3 * P])
        p_cross = sb("p_cross", [P, CRING, 2, S])
        y_t = sb("y_t", [P, 6, S])

        rec_s = sb("rec_s", [P, NT, H])
        rec_c = sb("rec_c", [P, NT * PAIRS, 2])
        y_s = sb("y_s", [P, NT, E])
        y_c = sb("y_c", [P, NT * PAIRS, 2 * D])
        y = sb("y", [P, NT, E])
        yt = sb("yt", [P, S])
        res2 = sb("res2", [P, NT, E])
        x2 = sb("x2", [P, NT, E])
        x2t = sb("x2t", [P, S])
        th = sb("th", [P, 3, S])
        ga = sb("ga", [P, 3, S])
        hid = sb("hid", [P, 3, S])
        res3 = sb("res3", [P, NT, E])
        o_sb = sb("o_sb", [P, NT, E])
        stats = [sb(f"stats{i}", [P, NT, 6]) for i in range(3)]
        mv = [sb(f"mv{i}", [P, NT, 2]) for i in range(3)]
        veps = [sb(f"veps{i}", [P, NT]) for i in range(3)]
        rstd = [sb(f"rstd{i}", [P, NT]) for i in range(3)]

        bank_x = [ps("bank_x0"), ps("bank_x1")]
        bank_m = [ps("bank_m0"), ps("bank_m1")]
        bank_s = [ps("bank_s0"), ps("bank_s1")]
        bank_v = ps("bank_v")
        bank_t = ps("bank_t")

        weights_loaded = sem("weights_loaded")
        sp_met, dve_met = sem("sp_met"), sem("dve_met")
        stacks_set = sem("stacks_set")
        pads_set = sem("pads_set")
        weights_ready = sem("weights_ready")
        zeros_set, bv_made = sem("zeros_set"), sem("bv_made")
        bv_ready = sem("bv_ready")
        bp_made = sem("bp_made")
        bp_ready = sem("bp_ready")
        x_loaded = sem("x_loaded")
        xb_ready = sem("xb_ready")
        local_filled = sem("local_filled")
        qk1_ready, v1_ready, prod_ready, heads0_ready = map(sem, ("qk1_ready", "v1_ready", "prod_ready", "heads0_ready"))
        lsc_step = sem("lsc_step")
        lneg_ready, r0max_ready, lexp_ready, r0exp_ready = map(sem, ("lneg_ready", "r0max_ready", "lexp_ready", "r0exp_ready"))
        r0_step = sem("r0_step")
        r0num_ready, r0rec_ready, lden_ready, lrec_ready = map(sem, ("r0num_ready", "r0rec_ready", "lden_ready", "lrec_ready"))
        probs_ready, probs_t_ready = sem("probs_ready"), sem("probs_t_ready")
        pv_ready, pvsum_ready, pvall_ready = sem("pv_ready"), sem("pvsum_ready"), sem("pvall_ready")
        acc_step = sem("acc_step")
        lctx_made, lctx_ready = sem("lctx_made"), sem("lctx_ready")
        res_ready = [sem(f"res_ready{i}") for i in range(3)]
        stats_ready = [sem(f"stats_ready{i}") for i in range(3)]
        mv_ready = [sem(f"mv_ready{i}") for i in range(3)]
        veps_ready = [sem(f"veps_ready{i}") for i in range(3)]
        rstd_ready = [sem(f"rstd_ready{i}") for i in range(3)]
        x1_ready, x1t_ready = sem("x1_ready"), sem("x1t_ready")
        project_filled = sem("project_filled")
        hi_ready, rest_ready, mid_ready, lo_ready = map(sem, ("hi_ready", "rest_ready", "mid_ready", "lo_ready"))
        v_ready = sem("v_ready")
        parts_written, stacks_loaded = sem("parts_written"), sem("stacks_loaded")
        rowmax_filled = sem("rowmax_filled")
        rowmax_read = [sem("rowmax_read0"), sem("rowmax_read1")]
        shift_hi_ready, shift_ready = sem("shift_hi_ready"), sem("shift_ready")
        rneg_ready = sem("rneg_ready")
        shift_t_ready, shift_loaded = sem("shift_t_ready"), sem("shift_loaded")
        x1res_ready = sem("x1res_ready")
        scores_filled = sem("scores_filled")
        exp_done = sem("exp_done")
        pv_filled, pv_emptied = sem("pv_filled"), sem("pv_emptied")
        tail_filled = sem("tail_filled")
        rec_step = sem("rec_step")
        yc_ready = sem("yc_ready")
        ys_ready, y_ready, yt_ready, x2_ready, x2t_ready = map(sem, ("ys_ready", "y_ready", "yt_ready", "x2_ready", "x2t_ready"))
        tanh_ready, gate_ready, hid_ready = sem("tanh_ready"), sem("gate_ready"), sem("hid_ready")
        out_ready, out_stored = sem("out_ready"), sem("out_stored")

        WEIGHTS = 14 * 16
        STACK_INIT = 6 * 16
        UNITS_L, UNITS_P, UNITS_M, UNITS_S, UNITS_T = 10, 4, 17, 20, 10
        block = stack.enter_context(nc.Block())

        @block.sync
        def _(sp):
            for dst, src in (
                (w1_sb[:, :, :], w1), (w2_sb[:, :, :], w2), (wck_sb[:, :], wck), (wcv_sb[:, :], wcv),
                (wgu_int[:, :], wgu), (wd_int[:, :, :], wd), (cols[:, :], bias_cols),
                (rows[:, 0, :], bias_rows[0:1, :].broadcast_to([P, E])),
                (rows[:, 1, :], bias_rows[1:2, :].broadcast_to([P, E])),
                (consts[:, :], k_f32), (cand_bias[:, :], k_bias[:, 0:CAND * NT * H]),
                (row0_bias[:, :], k_bias[:, CAND * NT * H:]), (spread[:, :, :], k_spread),
                (const16[:, :], k_bf16),
            ):
                sp.dma_start(dst, src).then_inc(weights_loaded, 16)
            for b in range(NBUF):
                sp.dma_start(k_st[:, b, :, :, :].rearrange("r p v t -> r p (v t)"),
                             k_rows[:, 0:2 * S].unsqueeze(1).broadcast_to([KROWS, PAIRS, 2 * S])).then_inc(stacks_set, 16)
                sp.dma_start(kc_st[:, b, :, :],
                             k_rows[:, 2 * S:].unsqueeze(1).broadcast_to([KROWS, PAIRS, 2 * SC])).then_inc(stacks_set, 16)

            def load(batch):
                b = batch.buf
                k = batch.index() if batch.loop is None else sp.snap(batch.index(), min_val=0, max_val=B - 1)
                if batch.reaches(64, 0):
                    sp.wait_ge(x_loaded, batch.count(64, 0))
                    sp.sem_inc(sp_met, 1)
                if batch.reaches(UNITS_P, -2 * UNITS_P):
                    sp.wait_ge(project_filled, batch.count(UNITS_P, -2 * UNITS_P))
                    sp.sem_inc(sp_met, 1)
                one = bass.ds(k, 1)
                sp.dma_start(xt_sb[:, b, :], xt[one, :, :].rearrange("a c t -> (a c) t")).then_inc(x_loaded, 16)
                sp.dma_start(x_sb[:, b, :, :], x[one, :, :].rearrange("a (i p) c -> (a p) i c", p=P)).then_inc(x_loaded, 16)
                for half in range(2):
                    sp.dma_start(ctxt_sb[:, b, half * SC:(half + 1) * SC],
                                 ctxt[one, :, :].rearrange("a c t -> (a c) t")).then_inc(x_loaded, 16)

            def parts_out(batch):
                if batch.reaches(96, 0):
                    sp.wait_ge(stacks_loaded, batch.count(96, 0))
                    sp.sem_inc(sp_met, 1)
                sp.wait_ge(hi_ready, batch.count(4, 4))
                sp.sem_inc(sp_met, 1)
                sp.wait_ge(mid_ready, batch.count(1, 1))
                sp.sem_inc(sp_met, 1)
                sp.wait_ge(lo_ready, batch.count(1, 1))
                sp.sem_inc(sp_met, 1)
                one_part = lambda part, n, c0, c1: parts[:, part, c0:c1].unsqueeze(1).broadcast_to([P, n, c1 - c0])
                sp.dma_start(parts_dram[:, 0:3, 0:QC], one_part(0, 3, 0, QC)).then_inc(parts_written, 16)
                sp.dma_start(parts_dram[:, 3:5, 0:QC], one_part(1, 2, 0, QC)).then_inc(parts_written, 16)
                sp.dma_start(parts_dram[:, 5:6, 0:QC], one_part(2, 1, 0, QC)).then_inc(parts_written, 16)
                sp.dma_start(parts_dram[:, 0:3, QC:COLS], parts[:, 0:3, QC:COLS]).then_inc(parts_written, 16)
                sp.dma_start(parts_dram[:, 3:5, QC:COLS], parts[:, 0:2, QC:COLS]).then_inc(parts_written, 16)
                sp.dma_start(parts_dram[:, 5:6, QC:COLS], one_part(0, 1, QC, COLS)).then_inc(parts_written, 16)

            def parts_in(batch):
                sp.wait_ge(parts_written, batch.count(96, 96))
                sp.sem_inc(sp_met, 1)
                if batch.reaches(UNITS_S, -2 * UNITS_S):
                    sp.wait_ge(scores_filled, batch.count(UNITS_S, -2 * UNITS_S))
                    sp.sem_inc(sp_met, 1)
                if batch.loop is None and batch.offset < NBUF:
                    sp.wait_ge(stacks_set, STACK_INIT)
                b = batch.buf
                by_head = parts_dram.rearrange("(p two d) s t -> two (d s) p t", two=2, d=D)
                for par in range(2):
                    r = slice(par * ROWS // 2, (par + 1) * ROWS // 2)
                    sp.dma_start(k_st[r, b, :, par, :], by_head[par][:, :, QC:QC + S]).then_inc(stacks_loaded, 16)
                    sp.dma_start(q_st[r, b, :, :], by_head[par][:, :, 0:QC]).then_inc(stacks_loaded, 16)
                    sp.dma_start(kc_st[r, b, :, par * SC:(par + 1) * SC],
                                 by_head[par][:, :, QC + S:COLS]).then_inc(stacks_loaded, 16)

            def shift_in(batch):
                sp.wait_ge(shift_t_ready, batch.count(1, 1))
                sp.sem_inc(sp_met, 1)
                if batch.reaches(16, 0):
                    sp.wait_ge(shift_loaded, batch.count(16, 0))
                    sp.sem_inc(sp_met, 1)
                if batch.reaches(UNITS_S, -2 * UNITS_S):
                    sp.wait_ge(scores_filled, batch.count(UNITS_S, -2 * UNITS_S))
                    sp.sem_inc(sp_met, 1)
                sp.dma_start(q_st[ROWS:KROWS, batch.buf, :, :].rearrange("r p (x t) -> r (p x) t", t=P),
                             shift_t[:, :]).then_inc(shift_loaded, 16)

            def store(batch):
                k = batch.index() if batch.loop is None else sp.snap(batch.index(), min_val=0, max_val=B - 1)
                sp.wait_ge(out_ready, batch.count(1, 1))
                sp.sem_inc(sp_met, 1)
                if batch.reaches(16, 0):
                    sp.wait_ge(out_stored, batch.count(16, 0))
                    sp.sem_inc(sp_met, 1)
                sp.dma_start(out[bass.ds(k, 1), :, :].rearrange("a (i p) c -> (a p) i c", p=P),
                             o_sb[:, :, :]).then_inc(out_stored, 16)

            pipeline(sp, {
                "local.load": load,
                "project.parts": lambda batch: (parts_out(batch), parts_in(batch)),
                "rowmax.shift": shift_in,
                "tail.norm3": store,
            })
            sp.wait_ge(out_stored, 16 * B)

        @block.tensor
        def _(pe):
            mm = nc.tensor.matmul
            pe.wait_ge(weights_loaded, WEIGHTS)
            pe.wait_ge(bv_ready, 1)
            mm(bank_t[:, 0:E], bv_wide[:, :], w2_sb[:, 4, :], start=True, stop=True).then_inc(bp_made, 1)
            pe.wait_ge(weights_ready, 2)
            pe.wait_ge(bp_ready, 1)

            def local_qkv(batch):
                b = batch.buf
                pe.wait_ge(x_loaded, batch.count(64, 64))
                bank = bank_x[0]
                if batch.reaches(2, -1):
                    pe.wait_ge(v_ready, batch.count(2, -1))
                mm(bank[:, 0:S], w1_sb[:, 0, :], xt_sb[:, b, :], start=True, stop=True)
                mm(bank[:, S:2 * S], w1_sb[:, 1, :], xt_sb[:, b, :], start=True, stop=True).then_inc(local_filled, 1)
                bank = bank_x[1]
                if batch.reaches(2, 0):
                    pe.wait_ge(v_ready, batch.count(2, 0))
                mm(bank[:, 0:S], w1_sb[:, 2, :], xt_sb[:, b, :], start=True, stop=True).then_inc(local_filled, 1)

            def local_scores(batch):
                bank = bank_x[0]
                pe.wait_ge(qk1_ready, batch.count(2, 2))
                pe.wait_ge(prod_ready, batch.count(1, 1))
                pe.wait_ge(heads0_ready, batch.count(2, 1))
                for t in range(NT):
                    for c in range(WIN):
                        mm(bank[:, c * NT * H + t * H:c * NT * H + (t + 1) * H], prod[:, c, t * P:(t + 1) * P], head_of,
                           start=(t == 0 and c == 0), stop=False, skip_group_check=True)
                    mm(bank[:, WIN * NT * H + t * H:WIN * NT * H + (t + 1) * H], q1[:, t * P:(t + 1) * P], k0_heads[:, :],
                       start=False, stop=False, skip_group_check=True)
                pe.wait_ge(heads0_ready, batch.count(2, 2))
                mm(bank[:, S:2 * S], q0_heads[:, :], k1[:, 2:2 + S], start=False, stop=True,
                   skip_group_check=True).then_inc(local_filled, 1)

            def local_spread0(batch):
                bank = bank_x[1]
                pe.wait_ge(v1_ready, batch.count(1, 1))
                pe.wait_ge(probs_ready, batch.count(1, 1))
                nrow = (CAND + 1) * H
                nc.tensor.transpose(bank[0:nrow, 0:P], probs[:, 0, :, :].rearrange("p c h -> p (c h)"), ident)
                nc.tensor.transpose(bank[0:nrow, P:2 * P], probs[:, 1, :, :].rearrange("p c h -> p (c h)"),
                                    ident).then_inc(local_filled, 1)

            def spread_out(bank, cands):
                for j, c in enumerate(cands):
                    last = mm(bank[:, j * S:(j + 1) * S], spread[:, c, :], probs_t[:, :], start=True, stop=True)
                last.then_inc(local_filled, 1)

            def local_spread1(batch):
                pe.wait_ge(r0_step, batch.count(4, 1))
                pe.wait_ge(probs_t_ready, batch.count(1, 1))
                spread_out(bank_x[0], (0, 1))
                spread_out(bank_x[1], (2, 3))

            def local_spread2(batch):
                pe.wait_ge(pv_ready, batch.count(2, 1))
                spread_out(bank_x[0], (4, 5))
                pe.wait_ge(pv_ready, batch.count(2, 2))
                spread_out(bank_x[1], (6,))

            def local_out(batch):
                bank = bank_x[0]
                pe.wait_ge(lctx_ready, batch.count(1, 1))
                mm(bank[:, 0:E], lctx[:, 0:P], w1_sb[:, 3, :], start=True, stop=True)
                mm(bank[:, E:2 * E], lctx[:, P:2 * P], w1_sb[:, 3, :], start=True, stop=True).then_inc(local_filled, 1)

            def local_x1t(batch):
                bank = bank_x[1]
                pe.wait_ge(pvall_ready, batch.count(1, 1))
                pe.wait_ge(x1_ready, batch.count(1, 1))
                nc.tensor.transpose(bank[:, 0:P], x1[:, batch.buf, 0, :], ident)
                nc.tensor.transpose(bank[:, P:2 * P], x1[:, batch.buf, 1, :], ident).then_inc(local_filled, 1)

            def project_qk(batch):
                b = batch.buf
                bank = bank_x[0]
                pe.wait_ge(res_ready[0], batch.count(1, 1))
                pe.wait_ge(x1t_ready, batch.count(1, 1))
                mm(bank[:, 0:S], w2_sb[:, 0, :], x1t[:, b, :], start=True, stop=True)
                mm(bank[:, S:2 * S], w2_sb[:, 3, :], x1t[:, b, :], start=True, stop=True).then_inc(project_filled, 1)
                bank = bank_x[1]
                mm(bank[:, 0:S], w2_sb[:, 1, :], x1t[:, b, :], start=True, stop=True)
                mm(bank[:, S:S + SC], wck_sb[:, :], ctxt_sb[:, b, 0:SC], start=True, stop=True).then_inc(project_filled, 1)

            def project_v(batch):
                b = batch.buf
                bank = bank_x[0]
                pe.wait_ge(rest_ready, batch.count(4, 2))
                mm(bank[:, 0:E], x1t[:, b, 0:P], w2_sb[:, 2, :], start=True, stop=True)
                mm(bank[:, E:2 * E], x1t[:, b, P:2 * P], w2_sb[:, 2, :], start=True, stop=True).then_inc(project_filled, 1)
                bank = bank_x[1]
                pe.wait_ge(rest_ready, batch.count(4, 4))
                mm(bank[:, 0:E], ctxt_sb[:, b, :], wcv_sb[:, :], start=True, stop=True).then_inc(project_filled, 1)

            def rowmax_pair(batch, arg):
                if arg == "shift":
                    pe.wait_ge(shift_ready, batch.count(1, 1))
                    nc.tensor.transpose(bank_m[0][:, 0:P // 2].bitcast(bf16),
                                        shift[:, :, :, :, :, :].rearrange("p a b c d e -> p (a b c d e)"),
                                        ident16).then_inc(rowmax_filled, 1)
                    return
                pair, b = int(arg), batch.buf
                if pair == 0:
                    pe.wait_ge(stacks_loaded, batch.count(96, 96))
                if pair == 0:
                    if batch.reaches(1, 0):
                        pe.wait_ge(shift_t_ready, batch.count(1, 0))
                else:
                    pe.wait_ge(rowmax_read[0], batch.count(8, pair))
                bank = bank_m[0].rearrange("p (v k) -> p v k", v=2)
                mm(bank[:, :, :], q_st[0:ROWS, b, pair, P:2 * P], k_st[0:ROWS, b, pair, :, :], start=True, stop=False)
                mm(bank[:, :, P:2 * P], ident16, causal_q.unsqueeze(1).broadcast_to([P, 2, P]), start=False, stop=True,
                   ).then_inc(rowmax_filled, 1)
                pe.wait_ge(rowmax_read[1], batch.count(8, pair))
                bank = bank_m[1]
                own = bank[:, 0:2 * P].rearrange("p (v k) -> p v k", v=2)
                mm(own, q_st[0:ROWS, b, pair, 0:P], k_st[0:ROWS, b, pair, :, 0:P], start=True, stop=False)
                mm(own, ident16, causal_q.unsqueeze(1).broadcast_to([P, 2, P]), start=False, stop=True)
                for t in range(NT):
                    last = mm(bank[:, 2 * P + t * P:2 * P + (t + 1) * P], q_st[0:ROWS, b, pair, S + t * P:S + (t + 1) * P],
                              kc_st[0:ROWS, b, pair, :], start=True, stop=True)
                last.then_inc(rowmax_filled, 1)

            def attend_pair(batch, arg):
                pair, b = int(arg), batch.buf
                if pair == 0:
                    pe.wait_ge(stacks_loaded, batch.count(96, 96))
                    pe.wait_ge(shift_loaded, batch.count(16, 16))
                units = [pair * 2 + pair // 2, pair * 2 + pair // 2 + 1]
                for v, u in enumerate(units):
                    if batch.reaches(UNITS_S, u - 1):
                        pe.wait_ge(exp_done, batch.count(UNITS_S, u - 1))
                    bank = bank_s[u % 2]
                    mm(bank[:, 0:S], k_st[0:KROWS, b, pair, v, 0:P], q_st[0:KROWS, b, pair, 0:S],
                       start=True, stop=False, skip_group_check=True)
                    mm(bank[:, S:S + P], k_st[0:KROWS, b, pair, v, P:2 * P], q_st[0:KROWS, b, pair, P:2 * P],
                       start=False, stop=False, skip_group_check=True)
                    diag = bank[:, 0:4 * P].rearrange("p (a q) -> p a q", a=2)[:, :, 0:P]
                    mm(diag, ident16, causal_k.unsqueeze(1).broadcast_to([P, 2, P]), start=False, stop=True,
                       skip_group_check=True).then_inc(scores_filled, 1)
                if pair % 2 == 1:
                    u = units[1] + 1
                    if batch.reaches(UNITS_S, u - 1):
                        pe.wait_ge(exp_done, batch.count(UNITS_S, u - 1))
                    for j, pr in enumerate((pair - 1, pair)):
                        last = mm(bank_s[u % 2][:, j * S:(j + 1) * S], kc_st[0:KROWS, b, pr, :], q_st[0:KROWS, b, pr, S:2 * S],
                                  start=True, stop=True)
                    last.then_inc(scores_filled, 1)

            PV_ORDER = ["self0", "cross0", "self1", "self2", "self3", "cross1"]

            def pv(batch, arg):
                u = PV_ORDER.index(arg)
                if batch.reaches(6, u):
                    pe.wait_ge(pv_emptied, batch.count(6, u))
                if u == 0:
                    pe.wait_ge(v_ready, batch.count(2, 2))
                g, b = int(arg[-1]), batch.buf
                if arg.startswith("self"):
                    pe.wait_ge(exp_done, batch.count(UNITS_S, 5 * g + 4))
                    for j in range(4):
                        h = 4 * g + j
                        mm(bank_v[32 * j:32 * j + 32, 0:S], v_sb[:, b, 0, h, :], p_self[:, h % RING, 0:S], start=True,
                           stop=False)
                    for j in range(4):
                        h = 4 * g + j
                        last = mm(bank_v[32 * j:32 * j + 32, P:2 * P], v_sb[:, b, 1, h, :], p_self[:, h % RING, S:S + P],
                                  start=False, stop=True)
                else:
                    pe.wait_ge(exp_done, batch.count(UNITS_S, 10 * g + 10))
                    for j in range(4):
                        pr = 4 * g + j
                        last = mm(bank_v[32 * j:32 * j + 32, 0:S], vc_sb[:, b, pr, :], p_cross[:, (pr // 2) % CRING, pr % 2, :],
                                  start=True, stop=True)
                last.then_inc(pv_filled, 1)

            def tail_self(batch, t):
                for g in range(4):
                    last = nc.tensor.transpose(bank_t[:, g * P:(g + 1) * P], y_t[:, g, t * P:(t + 1) * P], ident)
                last.then_inc(tail_filled, 1)

            def tail_self0(batch):
                if batch.reaches(1, 0):
                    pe.wait_ge(res_ready[2], batch.count(1, 0))
                pe.wait_ge(pv_emptied, batch.count(6, 6))
                tail_self(batch, 0)

            def tail_cross(batch):
                pe.wait_ge(ys_ready, batch.count(2, 1))
                for t in range(NT):
                    for g in range(2):
                        last = nc.tensor.transpose(bank_t[:, (t * 2 + g) * P:(t * 2 + g + 1) * P],
                                                   y_t[:, 4 + g, t * P:(t + 1) * P], ident)
                last.then_inc(tail_filled, 1)

            def tail_self1(batch):
                pe.wait_ge(yc_ready, batch.count(1, 1))
                tail_self(batch, 1)

            def transpose_tail(src):
                for t in range(NT):
                    last = nc.tensor.transpose(bank_t[:, t * P:(t + 1) * P], src[:, t, :], ident)
                last.then_inc(tail_filled, 1)

            def tail_y(batch):
                pe.wait_ge(ys_ready, batch.count(2, 2))
                pe.wait_ge(y_ready, batch.count(1, 1))
                transpose_tail(y)

            def tail_proj(batch):
                pe.wait_ge(yt_ready, batch.count(1, 1))
                for t in range(NT):
                    last = mm(bank_t[:, t * E:(t + 1) * E], yt[:, t * P:(t + 1) * P], w2_sb[:, 4, :], start=True, stop=True)
                last.then_inc(tail_filled, 1)

            def tail_x2t(batch):
                pe.wait_ge(res_ready[1], batch.count(1, 1))
                pe.wait_ge(x2_ready, batch.count(1, 1))
                transpose_tail(x2)

            def gate_up(i):
                mm(bank_t[:, 0:S], wgu_sb[:, i * P:(i + 1) * P], x2t[:, :], start=True, stop=True)
                mm(bank_t[:, S:2 * S], wgu_sb[:, HID + i * P:HID + (i + 1) * P], x2t[:, :], start=True,
                   stop=True).then_inc(tail_filled, 1)

            def tail_up0(batch):
                pe.wait_ge(x2t_ready, batch.count(1, 1))
                gate_up(0)

            def tail_up1(batch):
                pe.wait_ge(hid_ready, batch.count(3, 1))
                gate_up(1)

            def tail_up2(batch):
                pe.wait_ge(hid_ready, batch.count(3, 2))
                gate_up(2)

            def tail_down(batch):
                pe.wait_ge(hid_ready, batch.count(3, 3))
                for t in range(NT):
                    for c in range(3):
                        last = mm(bank_t[:, t * E:(t + 1) * E], hid[:, c, t * P:(t + 1) * P], wd_sb[:, c, :],
                                  start=(c == 0), stop=(c == 2))
                last.then_inc(tail_filled, 1)

            pipeline(pe, {
                "local.qkv": local_qkv,
                "local.scores": local_scores,
                "local.spread0": local_spread0,
                "local.spread1": local_spread1,
                "local.spread2": local_spread2,
                "local.out": local_out,
                "local.x1t": local_x1t,
                "project.qk": project_qk,
                "project.v": project_v,
                "rowmax": rowmax_pair,
                "attend": attend_pair,
                "pv": pv,
                "tail.self0": tail_self0,
                "tail.cross": tail_cross,
                "tail.self1": tail_self1,
                "tail.y": tail_y,
                "tail.proj": tail_proj,
                "tail.x2t": tail_x2t,
                "tail.up0": tail_up0,
                "tail.up1": tail_up1,
                "tail.up2": tail_up2,
                "tail.down": tail_down,
            })

        @block.scalar
        def _(act):
            A = nc.scalar.activation
            act.wait_ge(weights_loaded, WEIGHTS)
            act.wait_ge(pads_set, 7)

            def local_qkv(batch):
                act.wait_ge(local_filled, batch.count(UNITS_L, 1))
                A(q1[:, :], bank_x[0][:, 0:S], ACT.Identity, bias=cols[:, 0:1]).then_inc(qk1_ready, 1)
                A(k1[:, 2:2 + S], bank_x[0][:, S:2 * S], ACT.Identity, bias=cols[:, 1:2]).then_inc(qk1_ready, 1)
                act.wait_ge(local_filled, batch.count(UNITS_L, 2))
                A(v1[:, 2:2 + S], bank_x[1][:, 0:S], ACT.Identity, bias=cols[:, 2:3],
                  accum_out=v1_sum[:, :]).then_inc(v1_ready, 1)

            def local_exp(batch):
                act.wait_ge(lneg_ready, batch.count(1, 1))
                A(lexp[:, :, :], lneg[:, :, :], ACT.Exp, scale=-1.0).then_inc(lexp_ready, 1)
                act.wait_ge(r0max_ready, batch.count(1, 1))
                A(r0exp[:, :], r0v[:, :], ACT.Exp, bias=r0max[:, :], accum_out=r0sum[:, :]).then_inc(r0exp_ready, 1)

            def local_spread0(batch):
                act.wait_ge(local_filled, batch.count(UNITS_L, 4))
                A(probs_t[:, :], bank_x[1][0:(CAND + 1) * H, 0:S], ACT.Identity).then_inc(probs_t_ready, 1)

            def local_x1t(batch):
                act.wait_ge(local_filled, batch.count(UNITS_L, 10))
                A(x1t[:, batch.buf, :], bank_x[1][:, 0:S], ACT.Identity).then_inc(x1t_ready, 1)

            def project_qk(batch):
                if batch.reaches(96, 0):
                    act.wait_ge(parts_written, batch.count(96, 0))
                act.wait_ge(project_filled, batch.count(UNITS_P, 1))
                A(parts[:, 0, 0:S], bank_x[0][:, 0:S], ACT.Identity, bias=cols[:, 3:4]).then_inc(hi_ready, 1)
                A(parts[:, 0, S:QC], bank_x[0][:, S:2 * S], ACT.Identity, bias=cols[:, 5:6]).then_inc(hi_ready, 1)
                act.wait_ge(project_filled, batch.count(UNITS_P, 2))
                A(parts[:, 0, QC:QC + S], bank_x[1][:, 0:S], ACT.Identity, bias=cols[:, 4:5]).then_inc(hi_ready, 1)
                A(parts[:, 0, QC + S:COLS], bank_x[1][:, S:S + SC], ACT.Identity, bias=cols[:, 6:7]).then_inc(hi_ready, 1)

            def project_v(batch):
                b = batch.buf
                if batch.reaches(6, -12):
                    act.wait_ge(pv_filled, batch.count(6, -12))
                act.wait_ge(project_filled, batch.count(UNITS_P, 3))
                A(v_sb[:, b, :, :, 0:D], bank_x[0][:, 0:2 * E].rearrange("p (t h d) -> p t h d", t=NT, d=D),
                  ACT.Identity).then_inc(v_ready, 1)
                act.wait_ge(project_filled, batch.count(UNITS_P, 4))
                heads = bank_x[1][:, 0:E].rearrange("p (q two d) -> p q two d", two=2, d=D)
                A(vc_sb[0:SC, b, :, 0:D], heads[0:SC, :, 0, :], ACT.Identity)
                A(vc_sb[SC:2 * SC, b, :, D + 1:2 * D + 1], heads[SC:2 * SC, :, 1, :], ACT.Identity
                  ).then_inc(v_ready, 1)

            def project_parts(batch):
                act.wait_ge(rest_ready, batch.count(4, 4))
                A(parts[:, 1, :], rest[:, :], ACT.Identity).then_inc(mid_ready, 1)

            def attend_pair(batch, arg):
                pair = int(arg)
                units = [pair * 2 + pair // 2, pair * 2 + pair // 2 + 1]
                for v, u in enumerate(units):
                    h = 2 * pair + v
                    if h % 4 == 0:
                        if batch.reaches(6, [-2, 0 - 1, 1, 3][h // 4]):
                            act.wait_ge(pv_filled, batch.count(6, [-2, 0 - 1, 1, 3][h // 4]))
                    act.wait_ge(scores_filled, batch.count(UNITS_S, u + 1))
                    A(p_self[:, h % RING, :], bank_s[u % 2][:, 0:3 * P], ACT.Exp, scale=SCALE).then_inc(exp_done, 1)
                if pair % 2 == 1:
                    u = units[1] + 1
                    c = pair // 2
                    if c % 2 == 0:
                        if batch.reaches(6, [-4, 0][c // 2]):
                            act.wait_ge(pv_filled, batch.count(6, [-4, 0][c // 2]))
                    act.wait_ge(scores_filled, batch.count(UNITS_S, u + 1))
                    A(p_cross[:, c % CRING, :, :].rearrange("p a q -> p (a q)"), bank_s[u % 2][:, :], ACT.Exp,
                      scale=SCALE).then_inc(exp_done, 1)

            PV_ORDER = ["self0", "cross0", "self1", "self2", "self3", "cross1"]

            def pv(batch, arg):
                u = PV_ORDER.index(arg)
                g = int(arg[-1]) + (4 if arg.startswith("cross") else 0)
                act.wait_ge(pv_filled, batch.count(6, u + 1))
                A(y_t[:, g, :], bank_v[:, 0:S], ACT.Identity).then_inc(pv_emptied, 1)

            def tail_y(batch):
                act.wait_ge(tail_filled, batch.count(UNITS_T, 4))
                A(yt[:, :], bank_t[:, 0:S], ACT.Identity).then_inc(yt_ready, 1)

            def tail_x2t(batch):
                act.wait_ge(tail_filled, batch.count(UNITS_T, 6))
                A(x2t[:, :], bank_t[:, 0:S], ACT.Identity).then_inc(x2t_ready, 1)

            def tail_up(batch, i):
                act.wait_ge(tail_filled, batch.count(UNITS_T, 7 + i))
                A(th[:, i, :], bank_t[:, 0:S], ACT.Tanh, scale=0.5).then_inc(tanh_ready, 1)

            pipeline(act, {
                "local.qkv": local_qkv,
                "local.exp": local_exp,
                "local.spread0": local_spread0,
                "local.x1t": local_x1t,
                "project.qk": project_qk,
                "project.v": project_v,
                "project.parts": project_parts,
                "attend": attend_pair,
                "pv": pv,
                "tail.y": tail_y,
                "tail.x2t": tail_x2t,
                "tail.up0": lambda batch: tail_up(batch, 0),
                "tail.up1": lambda batch: tail_up(batch, 1),
                "tail.up2": lambda batch: tail_up(batch, 2),
            })

        @block.vector
        def _(dve):
            V = nc.vector
            V.memset(k1[:, :], 0.0).then_inc(pads_set, 1)
            V.memset(v1[:, :], 0.0).then_inc(pads_set, 1)
            V.memset(v_sb[:, :, :, :, :], 0.0).then_inc(zeros_set, 1)
            V.memset(vc_sb[:, :, :, :], 0.0).then_inc(zeros_set, 1)
            V.memset(small[:, 0:2], EPS).then_inc(pads_set, 1)
            V.memset(small[:, 2:4], -0.5).then_inc(pads_set, 1)
            dve.wait_ge(zeros_set, 2)
            V.memset(v_sb[:, :, :, :, D:D + 1], 1.0).then_inc(pads_set, 1)
            V.memset(vc_sb[0:SC, :, :, D:D + 1], 1.0).then_inc(pads_set, 1)
            V.memset(vc_sb[SC:2 * SC, :, :, 2 * D + 1:2 * D + 2], 1.0).then_inc(pads_set, 1)
            dve.wait_ge(weights_loaded, WEIGHTS)
            V.tensor_scalar(wgu_sb[:, :], wgu_int[:, :], 1.0 / 127.0, None, ALU.mult).then_inc(weights_ready, 1)
            V.tensor_scalar(wd_sb[:, :, :], wd_int[:, :, :], 1.0 / 127.0, None, ALU.mult).then_inc(weights_ready, 1)
            V.tensor_tensor(bv_both[:, :], cols[:, 7:8], cols[:, 8:9], ALU.add).then_inc(bv_made, 1)
            dve.wait_ge(bv_made, 1)
            V.tensor_copy(bv_wide[:, :], bv_both[:, 0:1].broadcast_to([P, P])).then_inc(bv_ready, 1)
            dve.wait_ge(bp_made, 1)
            V.tensor_tensor(bp_eff[:, :], bank_t[:, 0:E], rows[:, 1, :], ALU.add).then_inc(bp_ready, 1)

            def bn(batch, which, res):
                dve.wait_ge(res_ready[which], batch.count(1, 1))
                for t in range(NT):
                    V.bn_stats(stats[which][:, t, :], res[:, t, :]).then_inc(stats_ready[which], 1)
                dve.wait_ge(stats_ready[which], batch.count(NT, NT))
                dve.sem_inc(dve_met, 1)
                for t in range(NT):
                    V.bn_aggr(mv[which][:, t, :], stats[which][:, t, :]).then_inc(mv_ready[which], 1)

            def normalise(batch, which, res, dst, done):
                dve.wait_ge(rstd_ready[which], batch.count(1, 1))
                for t in range(NT):
                    last = V.tensor_scalar(dst[:, t, :], res[:, t, :], mv[which][:, t, 0:1], rstd[which][:, t:t + 1],
                                           ALU.subtract, ALU.mult)
                last.then_inc(done, 1)

            def local_products(batch):
                dve.wait_ge(qk1_ready, batch.count(2, 2))
                V.tensor_scalar(k0_heads[:, :], head_of, k1[:, 2:3], None, ALU.mult).then_inc(heads0_ready, 1)
                V.tensor_scalar(q0_heads[:, :], same_head, q1[:, 0:1], None, ALU.mult).then_inc(heads0_ready, 1)

            def local_scores(batch):
                dve.wait_ge(local_filled, batch.count(UNITS_L, 3))
                flat = lambda t: t[:, :, :].rearrange("p c x -> p (c x)")
                n = CAND * NT * H
                V.scalar_tensor_tensor(flat(lsc), bank_x[0][:, 0:n], SCALE, cand_bias[:, :], ALU.mult, ALU.add
                                       ).then_inc(lsc_step, 1)
                V.scalar_tensor_tensor(r0s[:, :], bank_x[0][:, S:2 * S], SCALE, row0_bias[:, :], ALU.mult, ALU.add
                                       ).then_inc(r0_step, 1)
                dve.wait_ge(lsc_step, batch.count(6, 1))
                V.tensor_reduce(lmax[:, :], lsc[:, :, :].rearrange("p c x -> p x c"), X, ALU.max).then_inc(lsc_step, 1)
                dve.wait_ge(r0_step, batch.count(4, 1))
                V.tensor_scalar(r0g[:, :], r0s[:, :], 0.0, NEG, ALU.is_lt, ALU.mult).then_inc(r0_step, 1)
                dve.wait_ge(lsc_step, batch.count(6, 2))
                V.tensor_scalar(lmax[:, :], lmax[:, :], 0.0, None, ALU.max).then_inc(lsc_step, 1)
                dve.wait_ge(r0_step, batch.count(4, 2))
                V.scalar_tensor_tensor(r0v[:, :], r0s[:, :], 0.0, r0g[:, :], ALU.max, ALU.add).then_inc(r0_step, 1)
                dve.wait_ge(lsc_step, batch.count(6, 3))
                V.tensor_tensor(lneg[:, :, :], lmax[:, :].unsqueeze(1).broadcast_to([P, CAND, NT * H]), lsc[:, :, :],
                                ALU.subtract).then_inc(lneg_ready, 1)
                dve.wait_ge(r0_step, batch.count(4, 3))
                V.tensor_reduce(r0max[:, :], r0v[:, :], X, ALU.max, negate=True).then_inc(r0max_ready, 1)

            def local_probs(batch):
                dve.wait_ge(lexp_ready, batch.count(1, 1))
                V.scalar_tensor_tensor(lgated[:, :, :], lsc[:, :, :], 0.0, lexp[:, :, :], ALU.is_ge, ALU.mult
                                       ).then_inc(lsc_step, 1)
                dve.wait_ge(r0exp_ready, batch.count(1, 1))
                V.tensor_tensor(r0pv[:, :], r0exp[:, :], v1[:, 2:2 + S], ALU.mult).then_inc(r0_step, 1)
                dve.wait_ge(lsc_step, batch.count(6, 4))
                V.tensor_reduce(lsum[:, :], lgated[:, :, :].rearrange("p c x -> p x c"), X, ALU.add).then_inc(lsc_step, 1)
                dve.wait_ge(r0_step, batch.count(4, 4))
                V.tensor_reduce(r0num[:, :], r0pv[:, :], X, ALU.add).then_inc(r0num_ready, 1)
                dve.wait_ge(lsc_step, batch.count(6, 5))
                V.tensor_scalar(lnone[:, :], lsum[:, :], 0.0, None, ALU.is_equal).then_inc(lsc_step, 1)
                V.reciprocal(r0rec[:, :], r0sum[:, :]).then_inc(r0rec_ready, 1)
                dve.wait_ge(lsc_step, batch.count(6, 6))
                V.scalar_tensor_tensor(lden[:, :], lnone[:, :], float(S), lsum[:, :], ALU.mult, ALU.add).then_inc(lden_ready, 1)
                dve.wait_ge(lden_ready, batch.count(1, 1))
                V.reciprocal(lrec[:, :], lden[:, :]).then_inc(lrec_ready, 1)
                dve.wait_ge(lrec_ready, batch.count(1, 1))
                th_ = lambda a: a.rearrange("p c (t h) -> p c t h", t=NT)
                V.tensor_tensor(probs[:, :, 0:CAND, :].rearrange("p t c h -> p c t h"), th_(lgated[:, :, :]),
                                th_(lrec[:, :].unsqueeze(1).broadcast_to([P, CAND, NT * H])), ALU.mult)
                V.tensor_tensor(probs[:, :, CAND, :], lnone[:, :].rearrange("p (t h) -> p t h", t=NT),
                                lrec[:, :].rearrange("p (t h) -> p t h", t=NT), ALU.mult).then_inc(probs_ready, 1)

            def window(first, n):
                return bass.AP(v1[:, :].tensor, first, [[S + WIN - 1, P], [1, n], [1, S]])

            def local_spread1(batch):
                for u, first, dst in ((5, 0, pv01), (6, 2, pv23)):
                    dve.wait_ge(local_filled, batch.count(UNITS_L, u))
                    V.tensor_tensor(dst[:, :, :], bank_x[(u - 1) % 2][:, :].rearrange("p (a t) -> p a t", a=2),
                                    window(first, 2), ALU.mult).then_inc(pv_ready, 1)

            def local_spread2(batch):
                dve.wait_ge(local_filled, batch.count(UNITS_L, 7))
                V.tensor_tensor(pv4[:, :], bank_x[0][:, 0:S], v1[:, 4:4 + S], ALU.mult).then_inc(acc_step, 1)
                dve.wait_ge(acc_step, batch.count(2, 1))
                V.scalar_tensor_tensor(pv5[:, :], bank_x[0][:, S:2 * S], v1[:, 2:3], pv4[:, :], ALU.mult, ALU.add
                                       ).then_inc(acc_step, 1)
                dve.wait_ge(acc_step, batch.count(2, 2))
                dve.wait_ge(local_filled, batch.count(UNITS_L, 8))
                V.scalar_tensor_tensor(pv6[:, :], bank_x[1][:, 0:S], v1_sum[:, 0:1], pv5[:, :], ALU.mult, ALU.add
                                       ).then_inc(pvall_ready, 1)

            def local_context(batch):
                dve.wait_ge(pvall_ready, batch.count(1, 1))
                dve.wait_ge(pvsum_ready, batch.count(2, 2))
                V.tensor_tensor(lctx[:, :], pvall[:, :], pv6[:, :], ALU.add).then_inc(lctx_made, 1)
                dve.wait_ge(lctx_made, batch.count(1, 1))
                dve.wait_ge(r0rec_ready, batch.count(1, 1))
                dve.wait_ge(r0num_ready, batch.count(1, 1))
                V.tensor_tensor(lctx[:, 0:1], r0num[:, :], r0rec[:, :], ALU.mult).then_inc(lctx_ready, 1)

            def local_out(batch):
                dve.wait_ge(local_filled, batch.count(UNITS_L, 9))
                dve.wait_ge(xb_ready, batch.count(1, 1))
                V.tensor_tensor(res1[:, :, :], bank_x[0][:, 0:2 * E].rearrange("p (t c) -> p t c", t=NT), xb[:, :, :],
                                ALU.add).then_inc(res_ready[0], 1)
                bn(batch, 0, res1)

            def local_norm1(batch):
                if batch.reaches(1, -2):
                    dve.wait_ge(x1res_ready, batch.count(1, -2))
                normalise(batch, 0, res1, x1[:, batch.buf], x1_ready)

            def project_qk(batch):
                if batch.reaches(1, 0):
                    dve.wait_ge(lo_ready, batch.count(1, 0))
                for n, (bank, c0, w, bias, at) in enumerate(((0, 0, S, 3, 0), (0, S, S, 5, S), (1, 0, S, 4, QC),
                                                             (1, S, SC, 6, QC + S))):
                    dve.wait_ge(hi_ready, batch.count(4, [2, 2, 4, 4][n]))
                    V.scalar_tensor_tensor(rest[:, at:at + w], bank_x[bank][:, c0:c0 + w], cols[:, bias:bias + 1],
                                           parts[:, 0, at:at + w], ALU.add, ALU.subtract).then_inc(rest_ready, 1)

            def rowmax_pair(batch, arg):
                if arg == "shift":
                    heads = lambda a: a.rearrange("p t k (q v) -> p t k q v", v=2)
                    dve.wait_ge(rowmax_read[0], batch.count(8, 8))
                    dve.wait_ge(rowmax_read[1], batch.count(8, 8))
                    for v in range(2):
                        m = rmax[:, :, :, :].rearrange("p t k (q v) -> p v q k t", v=2)[:, v]
                        V.tensor_scalar(shift[:, 0, v], m, -1.0, None, ALU.mult).then_inc(shift_hi_ready, 1)
                    dve.wait_ge(shift_hi_ready, batch.count(2, 2))
                    for v in range(2):
                        m = rmax[:, :, :, :].rearrange("p t k (q v) -> p v q k t", v=2)[:, v]
                        V.tensor_tensor(rneg[:, v], m, shift[:, 0, v], ALU.add).then_inc(rneg_ready, 1)
                    dve.wait_ge(rneg_ready, batch.count(2, 2))
                    V.tensor_scalar(shift[:, 1], rneg[:, :], -1.0, None, ALU.mult).then_inc(shift_ready, 1)
                    dve.wait_ge(rowmax_filled, batch.count(UNITS_M, UNITS_M))
                    if batch.reaches(16, 0):
                        dve.wait_ge(shift_loaded, batch.count(16, 0))
                    V.tensor_copy(shift_t[:, :], bank_m[0][:, 0:P // 2].bitcast(bf16)).then_inc(shift_t_ready, 1)
                    return
                pair = int(arg)
                h = slice(2 * pair, 2 * pair + 2)
                dve.wait_ge(rowmax_filled, batch.count(UNITS_M, 2 * pair + 1))
                V.tensor_reduce(rmax[:, 1, 0, h], bank_m[0][:, :].rearrange("p (v k) -> p v k", v=2), X, ALU.max
                                ).then_inc(rowmax_read[0], 1)
                dve.wait_ge(rowmax_filled, batch.count(UNITS_M, 2 * pair + 2))
                V.tensor_reduce(rmax[:, 0, 0, h], bank_m[1][:, 0:2 * P].rearrange("p (v k) -> p v k", v=2), X, ALU.max)
                V.tensor_reduce(rmax[:, :, 1, h], bank_m[1][:, 2 * P:4 * P].rearrange("p (t v k) -> p t v k", t=NT, v=2), X,
                                ALU.max).then_inc(rowmax_read[1], 1)

            def tail_self(batch, t):
                dve.wait_ge(tail_filled, batch.count(UNITS_T, 1 if t == 0 else 3))
                heads = bank_t[:, :].rearrange("p (h c) -> p h c", c=32)
                V.reciprocal(rec_s[:, t, :], heads[:, :, D]).then_inc(rec_step, 1)
                dve.wait_ge(rec_step, batch.count(3, 1 if t == 0 else 3))
                V.tensor_tensor(y_s[:, t, :].rearrange("p (h d) -> p h d", d=D), heads[:, :, 0:D],
                                rec_s[:, t, :].unsqueeze(2).broadcast_to([P, H, D]), ALU.mult).then_inc(ys_ready, 1)

            def tail_cross(batch):
                dve.wait_ge(tail_filled, batch.count(UNITS_T, 2))
                pairs = bank_t[:, :].rearrange("p (q c) -> p q c", c=32)[:, :, 0:2 * (D + 1)].rearrange(
                    "p q (v c) -> p q v c", v=2)
                V.reciprocal(rec_c[:, :, :], pairs[:, :, :, D]).then_inc(rec_step, 1)
                dve.wait_ge(rec_step, batch.count(3, 2))
                V.tensor_tensor(y_c[:, :, :].rearrange("p q (v d) -> p q v d", v=2), pairs[:, :, :, 0:D],
                                rec_c[:, :, :].unsqueeze(3).broadcast_to([P, NT * PAIRS, 2, D]), ALU.mult).then_inc(yc_ready, 1)

            def tail_norm(batch, which, unit, skip, res):
                dve.wait_ge(tail_filled, batch.count(UNITS_T, unit))
                if which == 1:
                    dve.wait_ge(x1res_ready, batch.count(1, 1))
                V.tensor_tensor(res[:, :, :], bank_t[:, 0:2 * E].rearrange("p (t c) -> p t c", t=NT), skip, ALU.add
                                ).then_inc(res_ready[which], 1)
                bn(batch, which, res)

            def tail_up(batch, i):
                dve.wait_ge(tanh_ready, batch.count(3, i + 1))
                V.scalar_tensor_tensor(ga[:, i, :], th[:, i, :], 1.0, bank_t[:, 0:S], ALU.add, ALU.mult).then_inc(gate_ready, 1)
                dve.wait_ge(gate_ready, batch.count(3, i + 1))
                V.scalar_tensor_tensor(hid[:, i, :], ga[:, i, :], 0.5, bank_t[:, S:2 * S], ALU.mult, ALU.mult
                                       ).then_inc(hid_ready, 1)

            def tail_norm3(batch):
                if batch.reaches(16, 0):
                    dve.wait_ge(out_stored, batch.count(16, 0))
                normalise(batch, 2, res3, o_sb, out_ready)

            pipeline(dve, {
                "local.products": local_products,
                "local.scores": local_scores,
                "local.probs": local_probs,
                "local.spread1": local_spread1,
                "local.spread2": local_spread2,
                "local.context": local_context,
                "local.out": local_out,
                "local.norm1": local_norm1,
                "project.qk": project_qk,
                "rowmax": rowmax_pair,
                "tail.self0": lambda batch: tail_self(batch, 0),
                "tail.cross": tail_cross,
                "tail.self1": lambda batch: tail_self(batch, 1),
                "tail.proj": lambda batch: tail_norm(batch, 1, 5, x1res[:, batch.buf], res2),
                "tail.norm2": lambda batch: normalise(batch, 1, res2, x2, x2_ready),
                "tail.up0": lambda batch: tail_up(batch, 0),
                "tail.up1": lambda batch: tail_up(batch, 1),
                "tail.up2": lambda batch: tail_up(batch, 2),
                "tail.down": lambda batch: tail_norm(batch, 2, 10, x2[:, :, :], res3),
                "tail.norm3": tail_norm3,
            })

        @block.gpsimd
        def _(pool):
            TT = nc.gpsimd.tensor_tensor
            pool.wait_ge(weights_loaded, WEIGHTS)
            pool.wait_ge(pads_set, 7)
            pool.wait_ge(bp_ready, 1)

            def rsqrt(batch, which):
                pool.wait_ge(mv_ready[which], batch.count(NT, NT))
                TT(veps[which][:, :], mv[which][:, :, 1], small[:, 0:2], ALU.add).then_inc(veps_ready[which], 1)
                pool.wait_ge(veps_ready[which], batch.count(1, 1))
                TT(rstd[which][:, :], veps[which][:, :], small[:, 2:4], ALU.pow).then_inc(rstd_ready[which], 1)

            def local_qkv(batch):
                pool.wait_ge(x_loaded, batch.count(64, 64))
                TT(xb[:, :, :], x_sb[:, batch.buf, :, :], rows[:, 0, :].unsqueeze(1).broadcast_to([P, NT, E]), ALU.add
                   ).then_inc(xb_ready, 1)

            def local_products(batch):
                pool.wait_ge(qk1_ready, batch.count(2, 2))
                TT(prod[:, :, :], bass.AP(k1[:, :].tensor, 0, [[S + WIN - 1, P], [1, WIN], [1, S]]),
                   q1[:, :].unsqueeze(1).broadcast_to([P, WIN, S]), ALU.mult).then_inc(prod_ready, 1)

            def local_context(batch):
                pool.wait_ge(pv_ready, batch.count(2, 2))
                TT(pvsum[:, :, :], pv01[:, :, :], pv23[:, :, :], ALU.add).then_inc(pvsum_ready, 1)
                pool.wait_ge(pvsum_ready, batch.count(2, 1))
                TT(pvall[:, :], pvsum[:, 0, :], pvsum[:, 1, :], ALU.add).then_inc(pvsum_ready, 1)

            def project_parts(batch):
                pool.wait_ge(mid_ready, batch.count(1, 1))
                pool.wait_ge(rest_ready, batch.count(4, 4))
                TT(parts[:, 2, :], rest[:, :], parts[:, 1, :], ALU.subtract).then_inc(lo_ready, 1)

            def rowmax(batch, arg):
                if arg == "0":
                    pool.wait_ge(x1_ready, batch.count(1, 1))
                    if batch.reaches(1, -2):
                        pool.wait_ge(res_ready[1], batch.count(1, -2))
                    TT(x1res[:, batch.buf, :, :], x1[:, batch.buf, :, :], bp_eff[:, :].unsqueeze(1).broadcast_to([P, NT, E]),
                       ALU.add).then_inc(x1res_ready, 1)

            def tail_y(batch):
                pool.wait_ge(ys_ready, batch.count(2, 2))
                pool.wait_ge(yc_ready, batch.count(1, 1))
                TT(y[:, :, :].rearrange("p t c -> p (t c)"), y_s[:, :, :].rearrange("p t c -> p (t c)"),
                   y_c[:, :, :].rearrange("p q c -> p (q c)"), ALU.add).then_inc(y_ready, 1)

            pipeline(pool, {
                "local.qkv": local_qkv,
                "local.products": local_products,
                "local.context": local_context,
                "local.out": lambda batch: rsqrt(batch, 0),
                "project.parts": project_parts,
                "rowmax": rowmax,
                "tail.y": tail_y,
                "tail.proj": lambda batch: rsqrt(batch, 1),
                "tail.down": lambda batch: rsqrt(batch, 2),
            })


def constants():
    import numpy as np
    head = np.arange(P) // D
    f32c = np.concatenate([np.eye(P), head[:, None] == head[None, :], head[:, None] == np.arange(H)[None, :]],
                          1).astype(np.float32)

    def pos_bias(diff):
        diff = diff.astype(np.float32)
        return (np.exp(np.float32(-0.5) * (diff / np.float32(2.0)) ** 2)
                + np.cos(np.float32(2.0 * np.pi) * diff / np.float32(401.0))).astype(np.float32)

    tok = np.arange(NT)[None, :] * P + np.arange(P)[:, None]
    cand = np.zeros((P, CAND, NT, H), np.float32)
    for c in range(WIN):
        key = tok + c - WIN // 2
        ok = (key >= 1) & (key < S)
        cand[:, c] = np.where(ok, pos_bias(tok - key), np.float32(-1e30))[:, :, None]
    cand[:, WIN] = pos_bias(tok)[:, :, None]
    row0 = np.broadcast_to(pos_bias(-np.arange(S))[None, :], (P, S))
    bias = np.ascontiguousarray(np.concatenate([cand.reshape(P, -1), row0], 1))
    spread = np.zeros((CAND + 1, H, CAND + 1, P), np.float32)
    for c in range(CAND + 1):
        spread[c, :, c, :] = head[None, :] == np.arange(H)[:, None]
    spread = spread.reshape((CAND + 1) * H, CAND + 1, P)
    i, j = np.arange(P)[:, None], np.arange(P)[None, :]
    b16 = np.concatenate([np.eye(P), np.where(j <= i, 0.0, -3e38), np.where(i <= j, 0.0, -3e38)], 1)
    rows = np.zeros((KROWS, 2 * S + 2 * SC), np.float32)
    for part in range(2):
        for par in range(2):
            r = ROWS + 2 * part + par
            rows[r, par * S:(par + 1) * S] = 1.0
            rows[r, 2 * S + par * SC:2 * S + (par + 1) * SC] = 1.0
    bits = lambda v: (np.ascontiguousarray(v, np.float32).view(np.uint32) >> 16).astype(np.uint16)
    return f32c, bias, spread, bits(b16), bits(rows)


def kernel(**inputs):
    import numpy as np
    import concourse.bacc as bacc
    from concourse.bass_utils import run_bass_kernel_spmd

    a = {k: np.asarray(v) for k, v in inputs.items()}
    local = lambda n: a["L0_attn_" + n]
    cross = lambda n: a["L0_xattn_" + n]
    k_f32, k_bias, k_spread, k_bf16, k_rows = constants()
    arrays = {
        "x": a["x"],
        "xt": a["x"].transpose(0, 2, 1),
        "ctxt": a["ctx_512"].transpose(0, 2, 1),
        "w1": np.stack([local(n).T for n in ("wq", "wk", "wv", "wo")], 1),
        "w2": np.stack([cross(n) for n in ("Wq", "Wk", "Wv", "Wcq", "Wp")], 1),
        "wck": cross("Wck"),
        "wcv": cross("Wcv"),
        "bias_cols": np.stack([local("bq"), local("bk"), local("bv"), cross("bq"), cross("bk"), cross("bcq"),
                               cross("bck"), cross("bv"), cross("bcv")], 1),
        "bias_rows": np.stack([local("bo"), cross("bp")], 0),
        "wgu": np.concatenate([a["L0_ffn_w_gate"].T, a["L0_ffn_w_up"].T], 1),
        "wd": a["L0_ffn_w_down"].T.reshape(3, P, E).transpose(1, 0, 2),
        "k_f32": k_f32, "k_bias": k_bias, "k_spread": k_spread, "k_bf16": k_bf16, "k_rows": k_rows,
    }
    arrays = {k: np.ascontiguousarray(v) for k, v in arrays.items()}
    nc = bacc.Bacc("TRN2", target_bir_lowering=False, num_devices=1)
    args = {k: nc.dram_tensor(k, list(v.shape), mybir.dt.from_np(v.dtype), kind="ExternalInput").ap()
            for k, v in arrays.items()}
    out = nc.dram_tensor("out", [B, S, E], mybir.dt.float32, kind="ExternalOutput").ap()
    decoder_layer(nc, out=out, **args)
    r = run_bass_kernel_spmd(nc, [arrays], core_ids=[0])
    return r.results[0]["out"]
```

```python
import concourse.bass as bass
from concourse import mybir
from contextlib import ExitStack

B, S, E, H, D = 16, 256, 128, 16, 8
SC, CC, HID = 64, 64, 384
P = 128
NT = S // P
PAIRS = H // 2
TERMS = 6
ROWS = 2 * D * TERMS
PROB_ROWS = 2 * 3 * H
KROWS = ROWS + 4
WIN = 5
CAND = WIN + 1
SCALE = float(D) ** -0.5
EPS = 1e-5
NEG = -1e9
NBUF = 3

SP_ORDER = [
    "0:local.load 5:tail.store 1:project.out 1:project.in 2:rowmax.in",
]
PE_ORDER = [
    "1:project.q 1:project.k 2:late.2 3:attend.5 4:tail.cross 1:project.v 3:attend.6 1:project.vc 2:early.2",
    "4:tail.self1 0:local.qkv 3:attend.7 2:late.3 3:pv.self0 2:early.3 4:tail.y 3:attend.8 2:late.4",
    "3:attend.9 4:tail.proj 2:early.4 2:late.5 0:local.scores 3:attend.10 3:pv.cross0 3:attend.11 3:attend.12",
    "2:early.5 3:attend.13 4:tail.x2t 2:late.6 3:attend.14 4:tail.up0 3:attend.15 2:early.6 3:pv.self1",
    "2:late.7 2:early.7 0:local.probs_t 3:attend.16 4:tail.up1 3:attend.17 0:local.spread0 0:local.spread2",
    "3:attend.18 0:local.spread4 2:rowmax.shift_t 3:pv.self2 3:attend.19 0:local.spread6 4:tail.up2 1:late.0",
    "1:early.0 3:pv.self3 1:late.1 0:local.out 2:attend.0 4:tail.down 2:attend.1 2:attend.2 3:pv.cross1",
    "1:early.1 2:attend.3 0:local.x1t 3:tail.self0 2:attend.4",
]
ACT_ORDER = [
    "3:attend.0 4:pv.self3 3:attend.1 4:pv.cross1 3:attend.2 1:local.x1t 3:attend.3 3:attend.4 1:project.q",
    "1:project.k 1:project.hi 1:project.v 3:attend.5 3:attend.6 1:project.vc 0:local.qk 1:project.mid",
    "3:attend.7 4:tail.y 3:pv.self0 0:local.v 3:attend.8 3:attend.9 3:attend.10 0:local.exp 3:attend.11",
    "0:local.exp_row0 3:attend.12 4:tail.x2t 3:pv.cross0 3:attend.13 0:local.prob_hi 4:up.0 0:local.prob_mid",
    "3:attend.14 3:attend.15 0:local.row0_num 3:pv.self1 0:local.probs_t 3:attend.16 4:up.1 3:attend.17",
    "3:attend.18 3:pv.self2 3:attend.19 4:up.2",
]
DVE_ORDER = [
    "4:tail.self1 2:early.2 2:late.3 2:early.3 2:late.4 0:local.products 4:tail.res2 4:tail.stats2 2:early.4",
    "2:late.5 0:local.scores 0:local.max 4:tail.norm2 0:local.gate 0:local.sum 0:local.probs 2:early.5",
    "2:late.6 2:early.6 4:up.0 2:late.7 2:early.7 2:rowmax.shift 0:spread.0 0:spread.2 4:up.1",
    "2:rowmax.shift_t 0:local.spread4 0:local.spread6 1:late.0 0:local.context 4:up.2 0:local.res",
    "0:local.stats 1:early.0 4:tail.res3 0:local.norm 4:tail.stats3 1:late.1 4:tail.norm3 3:tail.self0",
    "1:early.1 3:tail.cross 1:late.2",
]
POOL_ORDER = [
    "4:mask.2 4:mask.3 2:project.rest 5:tail.y 1:local.products 2:project.lo 5:tail.rstd2 4:mask.4 4:mask.5",
    "3:rowmax.x1res 4:mask.6 4:mask.7 1:local.row0_products 1:local.prob_rest 4:mask.8 1:local.prob_lo",
    "4:mask.9 4:mask.10 4:mask.11 4:mask.12 4:mask.13 4:mask.14 4:mask.15 1:local.context 3:mask.0",
    "1:local.rstd 3:mask.1 0:local.xb 5:tail.rstd3",
]
BUFFER_REUSE = ("local.load", "project.in", "rowmax.in", "project.v", "rowmax.x1res", "local.norm")


class Batch:

    def __init__(self, loop, offset):
        self.loop, self.offset, self.buf = loop, offset, offset % NBUF

    def count(self, each, add):
        value = self.offset * each + add
        return value if self.loop is None else self.loop * (NBUF * each) + value

    def reaches(self, each, add):
        return self.loop is not None or self.offset * each + add > 0

    def index(self):
        return self.count(1, 0)


def pipeline(eng, order, steps):
    def iteration(loop, n):
        for line in order:
            for entry in line.split():
                lag, name = entry.split(":")
                k = n - int(lag)
                if loop is None and not 0 <= k < B:
                    continue
                if name in steps:
                    steps[name](Batch(loop, k))
                else:
                    phase, arg = name.split(".")
                    steps[phase](Batch(loop, k), arg)
    entries = [entry.split(":") for line in order for entry in line.split()]
    first = max(int(lag) + (NBUF if name in BUFFER_REUSE else 1) for lag, name in entries)
    last = B + max(int(lag) for lag, _ in entries)
    full = (B - first) // NBUF * NBUF
    for n in range(first):
        iteration(None, n)
    with eng.Fori(0, full // NBUF) as i:
        for r in range(NBUF):
            iteration(i, first + r)
    for n in range(first + full, last):
        iteration(None, n)


def decoder_layer(nc, x, xt, ctxt, w1, w2, wck, wcv, bias_cols, bias_rows, wgu, wd, k_f32, k_bias, k_spread, k_bf16, k_rows, out):
    k_spread, k_bf16, k_rows = (a.bitcast(mybir.dt.bfloat16) for a in (k_spread, k_bf16, k_rows))
    f32, bf16, i32 = mybir.dt.float32, mybir.dt.bfloat16, mybir.dt.int32
    ALU, ACT = mybir.AluOpType, mybir.ActivationFunctionType
    X = mybir.AxisListType.X
    QC = 2 * S
    COLS = QC + S + SC

    parts_dram = nc.dram_tensor("parts_dram", [P, TERMS, COLS], bf16).ap()

    stack = ExitStack()
    with stack:
        def sb(name, shape, dt=f32):
            return stack.enter_context(nc.sbuf_tensor(name, shape, dt))

        def ps(name, shape=(P, 512)):
            return stack.enter_context(nc.psum_tensor(name, list(shape), f32))

        def sem(name):
            return stack.enter_context(nc.semaphore(name))

        w1_sb = sb("w1_sb", [P, 4, E])
        w2_sb = sb("w2_sb", [P, 5, E])
        wck_sb = sb("wck_sb", [CC, E])
        wcv_sb = sb("wcv_sb", [CC, E])
        wgu_int = sb("wgu_int", [P, 2 * HID], i32)
        wd_int = sb("wd_int", [P, 3, E], i32)
        wgu_sb = sb("wgu_sb", [P, 2 * HID])
        wd_sb = sb("wd_sb", [P, 3, E])
        cols = sb("cols", [P, 9])
        rows = sb("rows", [P, 2, E])
        consts = sb("consts", [P, 2 * P + H])
        cand_bias = sb("cand_bias", [P, CAND * NT * H])
        row0_bias = sb("row0_bias", [P, S])
        spread = sb("spread", [PROB_ROWS, 2, P], bf16)
        const16 = sb("const16", [P, 2 * P], bf16)
        small = sb("small", [P, 4])
        bv_both = sb("bv_both", [P, 1])
        bv_wide = sb("bv_wide", [P, P])
        bp_eff = sb("bp_eff", [P, E])
        ident, same_head, head_of = consts[:, 0:P], consts[:, P:2 * P], consts[:, 2 * P:2 * P + H]
        ident16, causal_q = const16[:, 0:P], const16[:, P:2 * P]

        x_sb = sb("x_sb", [P, NBUF, NT, E])
        xt_sb = sb("xt_sb", [P, NBUF, S])
        ctxt_sb = sb("ctxt_sb", [CC, NBUF, 2 * SC])
        xb = sb("xb", [P, NT, E])
        q1 = sb("q1", [P, S])
        k1 = sb("k1", [P, S + WIN - 1])
        v1 = sb("v1", [P, S + WIN - 1])
        v1_sum = sb("v1_sum", [P, 1])
        prod = sb("prod", [P, WIN, S])
        k0_heads = sb("k0_heads", [P, H])
        q0_heads = sb("q0_heads", [P, P])
        lsc = sb("lsc", [P, CAND, NT * H])
        lmax = sb("lmax", [P, NT * H])
        lneg = sb("lneg", [P, CAND, NT * H])
        lexp = sb("lexp", [P, CAND, NT * H])
        lgated = sb("lgated", [P, CAND, NT * H])
        lsum = sb("lsum", [P, NT * H])
        lnone = sb("lnone", [P, NT * H])
        lden = sb("lden", [P, NT * H])
        lrec = sb("lrec", [P, NT * H])
        probs = sb("probs", [P, NT, CAND + 1, H])
        prob_rest = sb("prob_rest", [P, NT, CAND + 1, H])
        prob_parts = sb("prob_parts", [P, NT, CAND + 2, 3, H], bf16)
        probs_t = sb("probs_t", [PROB_ROWS, 4, S], bf16)
        r0s = sb("r0s", [P, S])
        r0g = sb("r0g", [P, S])
        r0v = sb("r0v", [P, S])
        r0max = sb("r0max", [P, 1])
        r0exp = sb("r0exp", [P, S])
        r0sum = sb("r0sum", [P, 1])
        r0pv = sb("r0pv", [P, S])
        r0num = sb("r0num", [P, 1])
        r0all = sb("r0all", [P, S])
        r0rec = sb("r0rec", [P, 1])
        pv01 = sb("pv01", [P, 2, S])
        pv23 = sb("pv23", [P, 2, S])
        pv4 = sb("pv4", [P, S])
        pv5 = sb("pv5", [P, S])
        pv6 = sb("pv6", [P, S])
        pvsum = sb("pvsum", [P, 2, S])
        pvall = sb("pvall", [P, S])
        lctx = sb("lctx", [P, S])
        res1 = sb("res1", [P, NT, E])
        x1 = sb("x1", [P, NBUF, NT, E])
        x1t = sb("x1t", [P, NBUF, S])

        parts = sb("parts", [P, 3, COLS], bf16)
        full = sb("full", [P, COLS])
        rest = sb("rest", [P, COLS])
        q_st = sb("q_st", [KROWS, NBUF, PAIRS, QC], bf16)
        k_st = sb("k_st", [KROWS, NBUF, PAIRS, 2, S], bf16)
        kc_st = sb("kc_st", [KROWS, NBUF, PAIRS, 2 * SC], bf16)
        v_sb = sb("v_sb", [P, NBUF, NT, H, 32])
        vc_sb = sb("vc_sb", [P, NBUF, PAIRS, 32])

        rmax = sb("rmax", [P, NT, 2, H])
        rneg = sb("rneg", [P, 2, PAIRS, 2, NT])
        shift = sb("shift", [P, 2, 2, PAIRS, 2, NT], bf16)
        shift_t = sb("shift_t", [P, P], bf16)
        x1res = sb("x1res", [P, NBUF, NT, E])

        RING, CRING = 8, 4
        p_self = sb("p_self", [P, RING, 3 * P])
        p_cross = sb("p_cross", [P, CRING, 2, S])
        y_t = sb("y_t", [P, 6, S])

        rec_s = sb("rec_s", [P, NT, H])
        rec_c = sb("rec_c", [P, NT * PAIRS, 2])
        y_s = sb("y_s", [P, NT, E])
        y_c = sb("y_c", [P, NT * PAIRS, 2 * D])
        y = sb("y", [P, NT, E])
        yt = sb("yt", [P, S])
        res2 = sb("res2", [P, NT, E])
        x2 = sb("x2", [P, NT, E])
        x2t = sb("x2t", [P, S])
        th = sb("th", [P, 3, S])
        ga = sb("ga", [P, 3, S])
        hid = sb("hid", [P, 3, S])
        res3 = sb("res3", [P, NT, E])
        o_sb = sb("o_sb", [P, NT, E])
        stats = [sb(f"stats{i}", [P, NT, 6]) for i in range(3)]
        mv = [sb(f"mv{i}", [P, NT, 2]) for i in range(3)]
        veps = [sb(f"veps{i}", [P, NT]) for i in range(3)]
        rstd = [sb(f"rstd{i}", [P, NT]) for i in range(3)]

        bank_x = [ps("bank_x0"), ps("bank_x1")]
        bank_m = [ps("bank_m0"), ps("bank_m1")]
        bank_s = [ps("bank_s0"), ps("bank_s1")]
        bank_v = ps("bank_v")
        bank_t = ps("bank_t")

        weights_loaded = sem("weights_loaded")
        sp_met, dve_met, pool_met = sem("sp_met"), sem("dve_met"), sem("pool_met")
        stacks_set = sem("stacks_set")
        pads_set = sem("pads_set")
        weights_ready = sem("weights_ready")
        zeros_set, bv_made = sem("zeros_set"), sem("bv_made")
        bv_ready = sem("bv_ready")
        bp_made = sem("bp_made")
        bp_ready = sem("bp_ready")
        x_loaded = sem("x_loaded")
        xb_ready = sem("xb_ready")
        local_filled = sem("local_filled")
        qk1_ready, v1_ready, prod_ready, heads0_ready = map(sem, ("qk1_ready", "v1_ready", "prod_ready", "heads0_ready"))
        lsc_step = sem("lsc_step")
        lneg_ready, r0max_ready, lexp_ready, r0exp_ready = map(sem, ("lneg_ready", "r0max_ready", "lexp_ready", "r0exp_ready"))
        r0_step, r0pv_ready = sem("r0_step"), sem("r0pv_ready")
        r0num_ready, r0rec_ready, lden_ready, lrec_ready = map(sem, ("r0num_ready", "r0rec_ready", "lden_ready", "lrec_ready"))
        probs_ready, probs_t_ready = sem("probs_ready"), sem("probs_t_ready")
        prob_hi_ready, prob_rest_ready, prob_mid_ready, prob_lo_ready = map(
            sem, ("prob_hi_ready", "prob_rest_ready", "prob_mid_ready", "prob_lo_ready"))
        pv_ready, pvsum_ready, pvall_ready = sem("pv_ready"), sem("pvsum_ready"), sem("pvall_ready")
        acc_step = sem("acc_step")
        lctx_made, lctx_ready = sem("lctx_made"), sem("lctx_ready")
        res_ready = [sem(f"res_ready{i}") for i in range(3)]
        stats_ready = [sem(f"stats_ready{i}") for i in range(3)]
        mv_ready = [sem(f"mv_ready{i}") for i in range(3)]
        veps_ready = [sem(f"veps_ready{i}") for i in range(3)]
        rstd_ready = [sem(f"rstd_ready{i}") for i in range(3)]
        x1_ready, x1t_ready = sem("x1_ready"), sem("x1t_ready")
        project_filled = sem("project_filled")
        full_ready, hi_ready, rest_ready, mid_ready, lo_ready = map(sem, ("full_ready", "hi_ready", "rest_ready", "mid_ready", "lo_ready"))
        v_ready = sem("v_ready")
        parts_written, stacks_loaded = sem("parts_written"), sem("stacks_loaded")
        rowmax_filled = sem("rowmax_filled")
        rowmax_read = [sem("rowmax_read0"), sem("rowmax_read1")]
        shift_hi_ready, shift_ready = sem("shift_hi_ready"), sem("shift_ready")
        rneg_ready = sem("rneg_ready")
        shift_t_ready, shift_loaded = sem("shift_t_ready"), sem("shift_loaded")
        x1res_ready = sem("x1res_ready")
        scores_filled = sem("scores_filled")
        exp_done = sem("exp_done")
        masked = sem("masked")
        pv_filled, pv_emptied = sem("pv_filled"), sem("pv_emptied")
        tail_filled = sem("tail_filled")
        rec_step = sem("rec_step")
        yc_ready = sem("yc_ready")
        ys_ready, y_ready, yt_ready, x2_ready, x2t_ready = map(sem, ("ys_ready", "y_ready", "yt_ready", "x2_ready", "x2t_ready"))
        tanh_ready, gate_ready, hid_ready = sem("tanh_ready"), sem("gate_ready"), sem("hid_ready")
        out_ready, out_stored = sem("out_ready"), sem("out_stored")

        WEIGHTS = 14 * 16
        STACK_INIT = 6 * 16
        UNITS_L, UNITS_P, UNITS_M, UNITS_S, UNITS_T = 10, 4, 17, 20, 10
        block = stack.enter_context(nc.Block())

        @block.sync
        def _(sp):
            for dst, src in (
                (w1_sb[:, :, :], w1), (w2_sb[:, :, :], w2), (wck_sb[:, :], wck), (wcv_sb[:, :], wcv),
                (wgu_int[:, :], wgu), (wd_int[:, :, :], wd), (cols[:, :], bias_cols),
                (rows[:, 0, :], bias_rows[0:1, :].broadcast_to([P, E])),
                (rows[:, 1, :], bias_rows[1:2, :].broadcast_to([P, E])),
                (consts[:, :], k_f32), (cand_bias[:, :], k_bias[:, 0:CAND * NT * H]),
                (row0_bias[:, :], k_bias[:, CAND * NT * H:]), (spread[:, :, :], k_spread),
                (const16[:, :], k_bf16),
            ):
                sp.dma_start(dst, src).then_inc(weights_loaded, 16)
            for b in range(NBUF):
                sp.dma_start(k_st[:, b, :, :, :].rearrange("r p v t -> r p (v t)"),
                             k_rows[:, 0:2 * S].unsqueeze(1).broadcast_to([KROWS, PAIRS, 2 * S])).then_inc(stacks_set, 16)
                sp.dma_start(kc_st[:, b, :, :],
                             k_rows[:, 2 * S:].unsqueeze(1).broadcast_to([KROWS, PAIRS, 2 * SC])).then_inc(stacks_set, 16)

            def load(batch):
                b = batch.buf
                k = batch.index() if batch.loop is None else sp.snap(batch.index(), min_val=0, max_val=B - 1)
                if batch.reaches(64, 0):
                    sp.wait_ge(x_loaded, batch.count(64, 0))
                    sp.sem_inc(sp_met, 1)
                if batch.reaches(UNITS_P, -2 * UNITS_P):
                    sp.wait_ge(project_filled, batch.count(UNITS_P, -2 * UNITS_P))
                    sp.sem_inc(sp_met, 1)
                one = bass.ds(k, 1)
                sp.dma_start(xt_sb[:, b, :], xt[one, :, :].rearrange("a c t -> (a c) t")).then_inc(x_loaded, 16)
                sp.dma_start(x_sb[:, b, :, :], x[one, :, :].rearrange("a (i p) c -> (a p) i c", p=P)).then_inc(x_loaded, 16)
                for half in range(2):
                    sp.dma_start(ctxt_sb[:, b, half * SC:(half + 1) * SC],
                                 ctxt[one, :, :].rearrange("a c t -> (a c) t")).then_inc(x_loaded, 16)

            def parts_out(batch):
                if batch.reaches(96, 0):
                    sp.wait_ge(stacks_loaded, batch.count(96, 0))
                    sp.sem_inc(sp_met, 1)
                sp.wait_ge(hi_ready, batch.count(1, 1))
                sp.sem_inc(sp_met, 1)
                sp.wait_ge(mid_ready, batch.count(1, 1))
                sp.sem_inc(sp_met, 1)
                sp.wait_ge(lo_ready, batch.count(1, 1))
                sp.sem_inc(sp_met, 1)
                one_part = lambda part, n, c0, c1: parts[:, part, c0:c1].unsqueeze(1).broadcast_to([P, n, c1 - c0])
                sp.dma_start(parts_dram[:, 0:3, 0:QC], one_part(0, 3, 0, QC)).then_inc(parts_written, 16)
                sp.dma_start(parts_dram[:, 3:5, 0:QC], one_part(1, 2, 0, QC)).then_inc(parts_written, 16)
                sp.dma_start(parts_dram[:, 5:6, 0:QC], one_part(2, 1, 0, QC)).then_inc(parts_written, 16)
                sp.dma_start(parts_dram[:, 0:3, QC:COLS], parts[:, 0:3, QC:COLS]).then_inc(parts_written, 16)
                sp.dma_start(parts_dram[:, 3:5, QC:COLS], parts[:, 0:2, QC:COLS]).then_inc(parts_written, 16)
                sp.dma_start(parts_dram[:, 5:6, QC:COLS], one_part(0, 1, QC, COLS)).then_inc(parts_written, 16)

            def parts_in(batch):
                sp.wait_ge(parts_written, batch.count(96, 96))
                sp.sem_inc(sp_met, 1)
                if batch.reaches(UNITS_S, -2 * UNITS_S):
                    sp.wait_ge(scores_filled, batch.count(UNITS_S, -2 * UNITS_S))
                    sp.sem_inc(sp_met, 1)
                if batch.loop is None and batch.offset < NBUF:
                    sp.wait_ge(stacks_set, STACK_INIT)
                b = batch.buf
                by_head = parts_dram.rearrange("(p two d) s t -> two (d s) p t", two=2, d=D)
                for par in range(2):
                    r = slice(par * ROWS // 2, (par + 1) * ROWS // 2)
                    sp.dma_start(k_st[r, b, :, par, :], by_head[par][:, :, QC:QC + S]).then_inc(stacks_loaded, 16)
                    sp.dma_start(q_st[r, b, :, :], by_head[par][:, :, 0:QC]).then_inc(stacks_loaded, 16)
                    sp.dma_start(kc_st[r, b, :, par * SC:(par + 1) * SC],
                                 by_head[par][:, :, QC + S:COLS]).then_inc(stacks_loaded, 16)

            def shift_in(batch):
                sp.wait_ge(shift_t_ready, batch.count(1, 1))
                sp.sem_inc(sp_met, 1)
                if batch.reaches(16, 0):
                    sp.wait_ge(shift_loaded, batch.count(16, 0))
                    sp.sem_inc(sp_met, 1)
                if batch.reaches(UNITS_S, -2 * UNITS_S):
                    sp.wait_ge(scores_filled, batch.count(UNITS_S, -2 * UNITS_S))
                    sp.sem_inc(sp_met, 1)
                sp.dma_start(q_st[ROWS:KROWS, batch.buf, :, :].rearrange("r p (x t) -> r (p x) t", t=P),
                             shift_t[:, :]).then_inc(shift_loaded, 16)

            def store(batch):
                k = batch.index() if batch.loop is None else sp.snap(batch.index(), min_val=0, max_val=B - 1)
                sp.wait_ge(out_ready, batch.count(1, 1))
                sp.sem_inc(sp_met, 1)
                if batch.reaches(16, 0):
                    sp.wait_ge(out_stored, batch.count(16, 0))
                    sp.sem_inc(sp_met, 1)
                sp.dma_start(out[bass.ds(k, 1), :, :].rearrange("a (i p) c -> (a p) i c", p=P),
                             o_sb[:, :, :]).then_inc(out_stored, 16)

            pipeline(sp, SP_ORDER, {
                "local.load": load,
                "project.out": parts_out,
                "project.in": parts_in,
                "rowmax.in": shift_in,
                "tail.store": store,
            })
            sp.wait_ge(out_stored, 16 * B)

        @block.tensor
        def _(pe):
            mm = nc.tensor.matmul
            pe.wait_ge(weights_loaded, WEIGHTS)
            pe.wait_ge(bv_ready, 1)
            mm(bank_t[:, 0:E], bv_wide[:, :], w2_sb[:, 4, :], start=True, stop=True).then_inc(bp_made, 1)
            pe.wait_ge(weights_ready, 2)
            pe.wait_ge(bp_ready, 1)

            def local_qkv(batch):
                b = batch.buf
                pe.wait_ge(x_loaded, batch.count(64, 64))
                bank = bank_x[0]
                if batch.reaches(2, -1):
                    pe.wait_ge(v_ready, batch.count(2, -1))
                mm(bank[:, 0:S], w1_sb[:, 0, :], xt_sb[:, b, :], start=True, stop=True)
                mm(bank[:, S:2 * S], w1_sb[:, 1, :], xt_sb[:, b, :], start=True, stop=True).then_inc(local_filled, 1)
                bank = bank_x[1]
                if batch.reaches(2, 0):
                    pe.wait_ge(v_ready, batch.count(2, 0))
                mm(bank[:, 0:S], w1_sb[:, 2, :], xt_sb[:, b, :], start=True, stop=True).then_inc(local_filled, 1)

            def local_scores(batch):
                bank = bank_x[0]
                pe.wait_ge(qk1_ready, batch.count(2, 2))
                pe.wait_ge(prod_ready, batch.count(1, 1))
                pe.wait_ge(heads0_ready, batch.count(2, 1))
                for t in range(NT):
                    for c in range(WIN):
                        mm(bank[:, c * NT * H + t * H:c * NT * H + (t + 1) * H], prod[:, c, t * P:(t + 1) * P], head_of,
                           start=(t == 0 and c == 0), stop=False, skip_group_check=True)
                    mm(bank[:, WIN * NT * H + t * H:WIN * NT * H + (t + 1) * H], q1[:, t * P:(t + 1) * P], k0_heads[:, :],
                       start=False, stop=False, skip_group_check=True)
                pe.wait_ge(heads0_ready, batch.count(2, 2))
                mm(bank[:, S:2 * S], q0_heads[:, :], k1[:, 2:2 + S], start=False, stop=True,
                   skip_group_check=True).then_inc(local_filled, 1)

            def local_probs_t(batch):
                bank = bank_x[1]
                pe.wait_ge(v1_ready, batch.count(1, 1))
                pe.wait_ge(prob_mid_ready, batch.count(1, 1))
                pe.wait_ge(prob_lo_ready, batch.count(1, 1))
                out16 = bank[0:PROB_ROWS, :].bitcast(bf16)
                for j in range(4):
                    for t in range(NT):
                        last = nc.tensor.transpose(out16[:, j * S + t * P:j * S + (t + 1) * P],
                                                   prob_parts[:, t, 2 * j:2 * j + 2].rearrange("p c a h -> p (c a h)"), ident16)
                last.then_inc(local_filled, 1)

            def spread_out(bank, cands):
                for j, c in enumerate(cands):
                    last = mm(bank[:, j * S:(j + 1) * S], spread[:, c % 2, :], probs_t[:, c // 2, :], start=True, stop=True)
                last.then_inc(local_filled, 1)

            def local_spread0(batch):
                pe.wait_ge(r0_step, batch.count(3, 1))
                pe.wait_ge(probs_t_ready, batch.count(1, 1))
                spread_out(bank_x[0], (0, 1))

            def local_spread2(batch):
                spread_out(bank_x[1], (2, 3))

            def local_spread4(batch):
                pe.wait_ge(pv_ready, batch.count(2, 1))
                spread_out(bank_x[0], (4, 5))

            def local_spread6(batch):
                pe.wait_ge(pv_ready, batch.count(2, 2))
                spread_out(bank_x[1], (6,))

            def local_out(batch):
                bank = bank_x[0]
                pe.wait_ge(lctx_ready, batch.count(1, 1))
                mm(bank[:, 0:E], lctx[:, 0:P], w1_sb[:, 3, :], start=True, stop=True)
                mm(bank[:, E:2 * E], lctx[:, P:2 * P], w1_sb[:, 3, :], start=True, stop=True).then_inc(local_filled, 1)

            def local_x1t(batch):
                bank = bank_x[1]
                pe.wait_ge(pvall_ready, batch.count(1, 1))
                pe.wait_ge(x1_ready, batch.count(1, 1))
                nc.tensor.transpose(bank[:, 0:P], x1[:, batch.buf, 0, :], ident)
                nc.tensor.transpose(bank[:, P:2 * P], x1[:, batch.buf, 1, :], ident).then_inc(local_filled, 1)

            def project_q(batch):
                b = batch.buf
                bank = bank_x[0]
                pe.wait_ge(res_ready[0], batch.count(1, 1))
                pe.wait_ge(x1t_ready, batch.count(1, 1))
                mm(bank[:, 0:S], w2_sb[:, 0, :], x1t[:, b, :], start=True, stop=True)
                mm(bank[:, S:2 * S], w2_sb[:, 3, :], x1t[:, b, :], start=True, stop=True).then_inc(project_filled, 1)

            def project_k(batch):
                b = batch.buf
                bank = bank_x[1]
                mm(bank[:, 0:S], w2_sb[:, 1, :], x1t[:, b, :], start=True, stop=True)
                mm(bank[:, S:S + SC], wck_sb[:, :], ctxt_sb[:, b, 0:SC], start=True, stop=True).then_inc(project_filled, 1)

            def project_v(batch):
                b = batch.buf
                bank = bank_x[0]
                pe.wait_ge(full_ready, batch.count(4, 2))
                mm(bank[:, 0:E], x1t[:, b, 0:P], w2_sb[:, 2, :], start=True, stop=True)
                mm(bank[:, E:2 * E], x1t[:, b, P:2 * P], w2_sb[:, 2, :], start=True, stop=True).then_inc(project_filled, 1)

            def project_vc(batch):
                b = batch.buf
                bank = bank_x[1]
                pe.wait_ge(full_ready, batch.count(4, 4))
                mm(bank[:, 0:E], ctxt_sb[:, b, :], wcv_sb[:, :], start=True, stop=True).then_inc(project_filled, 1)

            def rowmax_shift_t(batch):
                pe.wait_ge(shift_ready, batch.count(1, 1))
                nc.tensor.transpose(bank_m[0][:, 0:P // 2].bitcast(bf16),
                                    shift[:, :, :, :, :, :].rearrange("p a b c d e -> p (a b c d e)"),
                                    ident16).then_inc(rowmax_filled, 1)

            def rowmax_late(batch, arg):
                pair, b = int(arg), batch.buf
                if pair == 0:
                    pe.wait_ge(stacks_loaded, batch.count(96, 96))
                    if batch.reaches(1, 0):
                        pe.wait_ge(shift_t_ready, batch.count(1, 0))
                else:
                    pe.wait_ge(rowmax_read[0], batch.count(8, pair))
                bank = bank_m[0].rearrange("p (v k) -> p v k", v=2)
                mm(bank[:, :, :], q_st[0:ROWS, b, pair, P:2 * P], k_st[0:ROWS, b, pair, :, :], start=True, stop=False)
                mm(bank[:, :, P:2 * P], ident16, causal_q.unsqueeze(1).broadcast_to([P, 2, P]), start=False, stop=True,
                   ).then_inc(rowmax_filled, 1)

            def rowmax_early(batch, arg):
                pair, b = int(arg), batch.buf
                pe.wait_ge(rowmax_read[1], batch.count(8, pair))
                bank = bank_m[1]
                own = bank[:, 0:2 * P].rearrange("p (v k) -> p v k", v=2)
                mm(own, q_st[0:ROWS, b, pair, 0:P], k_st[0:ROWS, b, pair, :, 0:P], start=True, stop=False)
                mm(own, ident16, causal_q.unsqueeze(1).broadcast_to([P, 2, P]), start=False, stop=True)
                for t in range(NT):
                    last = mm(bank[:, 2 * P + t * P:2 * P + (t + 1) * P], q_st[0:ROWS, b, pair, S + t * P:S + (t + 1) * P],
                              kc_st[0:ROWS, b, pair, :], start=True, stop=True)
                last.then_inc(rowmax_filled, 1)

            def attend(batch, arg):
                u, b = int(arg), batch.buf
                if u == 0:
                    pe.wait_ge(stacks_loaded, batch.count(96, 96))
                    pe.wait_ge(shift_loaded, batch.count(16, 16))
                if batch.reaches(UNITS_S, u - 1):
                    pe.wait_ge(exp_done, batch.count(UNITS_S, u - 1))
                bank = bank_s[u % 2]
                if u % 5 < 4:
                    pair, v = divmod(u // 5 * 4 + u % 5, 2)
                    mm(bank[:, 0:S], k_st[0:KROWS, b, pair, v, 0:P], q_st[0:KROWS, b, pair, 0:S], start=True, stop=True)
                    mm(bank[:, S:S + P], k_st[0:KROWS, b, pair, v, P:2 * P], q_st[0:KROWS, b, pair, P:2 * P],
                       start=True, stop=True).then_inc(scores_filled, 1)
                else:
                    for j in range(2):
                        pair = u // 5 * 2 + j
                        last = mm(bank[:, j * S:(j + 1) * S], kc_st[0:KROWS, b, pair, :], q_st[0:KROWS, b, pair, S:2 * S],
                                  start=True, stop=True)
                    last.then_inc(scores_filled, 1)

            PV_ORDER = ["self0", "cross0", "self1", "self2", "self3", "cross1"]

            def pv(batch, arg):
                u = PV_ORDER.index(arg)
                if batch.reaches(6, u):
                    pe.wait_ge(pv_emptied, batch.count(6, u))
                if u == 0:
                    pe.wait_ge(v_ready, batch.count(2, 2))
                g, b = int(arg[-1]), batch.buf
                if arg.startswith("self"):
                    pe.wait_ge(masked, batch.count(H, 4 * g + 4))
                    for j in range(4):
                        h = 4 * g + j
                        mm(bank_v[32 * j:32 * j + 32, 0:S], v_sb[:, b, 0, h, :], p_self[:, h % RING, 0:S], start=True,
                           stop=False)
                    for j in range(4):
                        h = 4 * g + j
                        last = mm(bank_v[32 * j:32 * j + 32, P:2 * P], v_sb[:, b, 1, h, :], p_self[:, h % RING, S:S + P],
                                  start=False, stop=True)
                else:
                    pe.wait_ge(exp_done, batch.count(UNITS_S, 10 * g + 10))
                    for j in range(4):
                        pr = 4 * g + j
                        last = mm(bank_v[32 * j:32 * j + 32, 0:S], vc_sb[:, b, pr, :], p_cross[:, (pr // 2) % CRING, pr % 2, :],
                                  start=True, stop=True)
                last.then_inc(pv_filled, 1)

            def tail_self(batch, t):
                for g in range(4):
                    last = nc.tensor.transpose(bank_t[:, g * P:(g + 1) * P], y_t[:, g, t * P:(t + 1) * P], ident)
                last.then_inc(tail_filled, 1)

            def tail_self0(batch):
                if batch.reaches(1, 0):
                    pe.wait_ge(res_ready[2], batch.count(1, 0))
                pe.wait_ge(pv_emptied, batch.count(6, 6))
                tail_self(batch, 0)

            def tail_cross(batch):
                pe.wait_ge(ys_ready, batch.count(2, 1))
                for t in range(NT):
                    for g in range(2):
                        last = nc.tensor.transpose(bank_t[:, (t * 2 + g) * P:(t * 2 + g + 1) * P],
                                                   y_t[:, 4 + g, t * P:(t + 1) * P], ident)
                last.then_inc(tail_filled, 1)

            def tail_self1(batch):
                pe.wait_ge(yc_ready, batch.count(1, 1))
                tail_self(batch, 1)

            def transpose_tail(src):
                for t in range(NT):
                    last = nc.tensor.transpose(bank_t[:, t * P:(t + 1) * P], src[:, t, :], ident)
                last.then_inc(tail_filled, 1)

            def tail_y(batch):
                pe.wait_ge(ys_ready, batch.count(2, 2))
                pe.wait_ge(y_ready, batch.count(1, 1))
                transpose_tail(y)

            def tail_proj(batch):
                pe.wait_ge(yt_ready, batch.count(1, 1))
                for t in range(NT):
                    last = mm(bank_t[:, t * E:(t + 1) * E], yt[:, t * P:(t + 1) * P], w2_sb[:, 4, :], start=True, stop=True)
                last.then_inc(tail_filled, 1)

            def tail_x2t(batch):
                pe.wait_ge(res_ready[1], batch.count(1, 1))
                pe.wait_ge(x2_ready, batch.count(1, 1))
                transpose_tail(x2)

            def gate_up(i):
                mm(bank_t[:, 0:S], wgu_sb[:, i * P:(i + 1) * P], x2t[:, :], start=True, stop=True)
                mm(bank_t[:, S:2 * S], wgu_sb[:, HID + i * P:HID + (i + 1) * P], x2t[:, :], start=True,
                   stop=True).then_inc(tail_filled, 1)

            def tail_up0(batch):
                pe.wait_ge(x2t_ready, batch.count(1, 1))
                gate_up(0)

            def tail_up1(batch):
                pe.wait_ge(hid_ready, batch.count(3, 1))
                gate_up(1)

            def tail_up2(batch):
                pe.wait_ge(hid_ready, batch.count(3, 2))
                gate_up(2)

            def tail_down(batch):
                pe.wait_ge(hid_ready, batch.count(3, 3))
                for t in range(NT):
                    for c in range(3):
                        last = mm(bank_t[:, t * E:(t + 1) * E], hid[:, c, t * P:(t + 1) * P], wd_sb[:, c, :],
                                  start=(c == 0), stop=(c == 2))
                last.then_inc(tail_filled, 1)

            pipeline(pe, PE_ORDER, {
                "local.qkv": local_qkv,
                "local.scores": local_scores,
                "local.probs_t": local_probs_t,
                "local.spread0": local_spread0,
                "local.spread2": local_spread2,
                "local.spread4": local_spread4,
                "local.spread6": local_spread6,
                "local.out": local_out,
                "local.x1t": local_x1t,
                "project.q": project_q,
                "project.k": project_k,
                "project.v": project_v,
                "project.vc": project_vc,
                "late": rowmax_late,
                "early": rowmax_early,
                "rowmax.shift_t": rowmax_shift_t,
                "attend": attend,
                "pv": pv,
                "tail.self0": tail_self0,
                "tail.cross": tail_cross,
                "tail.self1": tail_self1,
                "tail.y": tail_y,
                "tail.proj": tail_proj,
                "tail.x2t": tail_x2t,
                "tail.up0": tail_up0,
                "tail.up1": tail_up1,
                "tail.up2": tail_up2,
                "tail.down": tail_down,
            })

        @block.scalar
        def _(act):
            A = nc.scalar.activation
            act.wait_ge(weights_loaded, WEIGHTS)
            act.wait_ge(pads_set, 8)

            def local_qk(batch):
                act.wait_ge(local_filled, batch.count(UNITS_L, 1))
                A(q1[:, :], bank_x[0][:, 0:S], ACT.Identity, bias=cols[:, 0:1]).then_inc(qk1_ready, 1)
                A(k1[:, 2:2 + S], bank_x[0][:, S:2 * S], ACT.Identity, bias=cols[:, 1:2]).then_inc(qk1_ready, 1)

            def local_v(batch):
                act.wait_ge(local_filled, batch.count(UNITS_L, 2))
                A(v1[:, 2:2 + S], bank_x[1][:, 0:S], ACT.Identity, bias=cols[:, 2:3],
                  accum_out=v1_sum[:, :]).then_inc(v1_ready, 1)

            def local_exp(batch):
                act.wait_ge(lneg_ready, batch.count(1, 1))
                A(lexp[:, :, :], lneg[:, :, :], ACT.Exp, scale=-1.0).then_inc(lexp_ready, 1)

            def local_exp_row0(batch):
                act.wait_ge(r0max_ready, batch.count(1, 1))
                A(r0exp[:, :], r0v[:, :], ACT.Exp, bias=r0max[:, :], accum_out=r0sum[:, :]).then_inc(r0exp_ready, 1)

            def local_probs_t(batch):
                act.wait_ge(local_filled, batch.count(UNITS_L, 4))
                A(probs_t[:, :, :].rearrange("r j t -> r (j t)"), bank_x[1][0:PROB_ROWS, :].bitcast(bf16), ACT.Identity
                  ).then_inc(probs_t_ready, 1)

            def local_row0_num(batch):
                act.wait_ge(r0pv_ready, batch.count(1, 1))
                A(r0all[:, :], r0pv[:, :], ACT.Identity, accum_out=r0num[:, :]).then_inc(r0num_ready, 1)

            def local_prob_hi(batch):
                act.wait_ge(probs_ready, batch.count(1, 1))
                A(prob_parts[:, :, 0:CAND + 1, 0, :], probs[:, :, :, :], ACT.Identity).then_inc(prob_hi_ready, 1)

            def local_prob_mid(batch):
                act.wait_ge(prob_rest_ready, batch.count(1, 1))
                A(prob_parts[:, :, 0:CAND + 1, 1, :], prob_rest[:, :, :, :], ACT.Identity).then_inc(prob_mid_ready, 1)

            def local_x1t(batch):
                act.wait_ge(local_filled, batch.count(UNITS_L, 10))
                A(x1t[:, batch.buf, :], bank_x[1][:, 0:S], ACT.Identity).then_inc(x1t_ready, 1)

            def project_q(batch):
                if batch.reaches(1, 0):
                    act.wait_ge(rest_ready, batch.count(1, 0))
                act.wait_ge(project_filled, batch.count(UNITS_P, 1))
                A(full[:, 0:S], bank_x[0][:, 0:S], ACT.Identity, bias=cols[:, 3:4]).then_inc(full_ready, 1)
                A(full[:, S:QC], bank_x[0][:, S:2 * S], ACT.Identity, bias=cols[:, 5:6]).then_inc(full_ready, 1)

            def project_k(batch):
                act.wait_ge(project_filled, batch.count(UNITS_P, 2))
                A(full[:, QC:QC + S], bank_x[1][:, 0:S], ACT.Identity, bias=cols[:, 4:5]).then_inc(full_ready, 1)
                A(full[:, QC + S:COLS], bank_x[1][:, S:S + SC], ACT.Identity, bias=cols[:, 6:7]).then_inc(full_ready, 1)

            def project_hi(batch):
                if batch.reaches(96, 0):
                    act.wait_ge(parts_written, batch.count(96, 0))
                act.wait_ge(full_ready, batch.count(4, 4))
                A(parts[:, 0, :], full[:, :], ACT.Identity).then_inc(hi_ready, 1)

            def project_v(batch):
                b = batch.buf
                if batch.reaches(6, -12):
                    act.wait_ge(pv_filled, batch.count(6, -12))
                act.wait_ge(project_filled, batch.count(UNITS_P, 3))
                A(v_sb[:, b, :, :, 0:D], bank_x[0][:, 0:2 * E].rearrange("p (t h d) -> p t h d", t=NT, d=D),
                  ACT.Identity).then_inc(v_ready, 1)

            def project_vc(batch):
                b = batch.buf
                act.wait_ge(project_filled, batch.count(UNITS_P, 4))
                heads = bank_x[1][:, 0:E].rearrange("p (q two d) -> p q two d", two=2, d=D)
                A(vc_sb[0:SC, b, :, 0:D], heads[0:SC, :, 0, :], ACT.Identity)
                A(vc_sb[SC:2 * SC, b, :, D + 1:2 * D + 1], heads[SC:2 * SC, :, 1, :], ACT.Identity
                  ).then_inc(v_ready, 1)

            def project_mid(batch):
                act.wait_ge(rest_ready, batch.count(1, 1))
                A(parts[:, 1, :], rest[:, :], ACT.Identity).then_inc(mid_ready, 1)

            def attend(batch, arg):
                u = int(arg)
                g, r = divmod(u, 5)
                if r == 0:
                    before = [-2, -1, 1, 3][g]
                    if batch.reaches(6, before):
                        act.wait_ge(pv_filled, batch.count(6, before))
                if r == 4 and g % 2 == 0:
                    before = [-4, 0][g // 2]
                    if batch.reaches(6, before):
                        act.wait_ge(pv_filled, batch.count(6, before))
                act.wait_ge(scores_filled, batch.count(UNITS_S, u + 1))
                if r < 4:
                    A(p_self[:, (4 * g + r) % RING, :], bank_s[u % 2][:, 0:3 * P], ACT.Exp, scale=SCALE).then_inc(exp_done, 1)
                else:
                    A(p_cross[:, g % CRING, :, :].rearrange("p a q -> p (a q)"), bank_s[u % 2][:, :], ACT.Exp,
                      scale=SCALE).then_inc(exp_done, 1)

            PV_ORDER = ["self0", "cross0", "self1", "self2", "self3", "cross1"]

            def pv(batch, arg):
                u = PV_ORDER.index(arg)
                g = int(arg[-1]) + (4 if arg.startswith("cross") else 0)
                act.wait_ge(pv_filled, batch.count(6, u + 1))
                A(y_t[:, g, :], bank_v[:, 0:S], ACT.Identity).then_inc(pv_emptied, 1)

            def tail_y(batch):
                act.wait_ge(tail_filled, batch.count(UNITS_T, 4))
                A(yt[:, :], bank_t[:, 0:S], ACT.Identity).then_inc(yt_ready, 1)

            def tail_x2t(batch):
                act.wait_ge(tail_filled, batch.count(UNITS_T, 6))
                A(x2t[:, :], bank_t[:, 0:S], ACT.Identity).then_inc(x2t_ready, 1)

            def tail_up(batch, arg):
                i = int(arg)
                act.wait_ge(tail_filled, batch.count(UNITS_T, 7 + i))
                A(th[:, i, :], bank_t[:, 0:S], ACT.Tanh, scale=0.5).then_inc(tanh_ready, 1)

            pipeline(act, ACT_ORDER, {
                "local.qk": local_qk,
                "local.v": local_v,
                "local.exp": local_exp,
                "local.exp_row0": local_exp_row0,
                "local.prob_hi": local_prob_hi,
                "local.prob_mid": local_prob_mid,
                "local.probs_t": local_probs_t,
                "local.row0_num": local_row0_num,
                "local.x1t": local_x1t,
                "project.q": project_q,
                "project.k": project_k,
                "project.v": project_v,
                "project.vc": project_vc,
                "project.hi": project_hi,
                "project.mid": project_mid,
                "attend": attend,
                "pv": pv,
                "tail.y": tail_y,
                "tail.x2t": tail_x2t,
                "up": tail_up,
            })

        @block.vector
        def _(dve):
            V = nc.vector
            V.memset(k1[:, :], 0.0).then_inc(pads_set, 1)
            V.memset(v1[:, :], 0.0).then_inc(pads_set, 1)
            V.memset(prob_parts[:, :, :, :, :], 0.0).then_inc(pads_set, 1)
            V.memset(v_sb[:, :, :, :, :], 0.0).then_inc(zeros_set, 1)
            V.memset(vc_sb[:, :, :, :], 0.0).then_inc(zeros_set, 1)
            V.memset(small[:, 0:2], EPS).then_inc(pads_set, 1)
            V.memset(small[:, 2:4], -0.5).then_inc(pads_set, 1)
            dve.wait_ge(zeros_set, 2)
            V.memset(v_sb[:, :, :, :, D:D + 1], 1.0).then_inc(pads_set, 1)
            V.memset(vc_sb[0:SC, :, :, D:D + 1], 1.0).then_inc(pads_set, 1)
            V.memset(vc_sb[SC:2 * SC, :, :, 2 * D + 1:2 * D + 2], 1.0).then_inc(pads_set, 1)
            dve.wait_ge(weights_loaded, WEIGHTS)
            V.tensor_scalar(wgu_sb[:, :], wgu_int[:, :], 1.0 / 127.0, None, ALU.mult).then_inc(weights_ready, 1)
            V.tensor_scalar(wd_sb[:, :, :], wd_int[:, :, :], 1.0 / 127.0, None, ALU.mult).then_inc(weights_ready, 1)
            V.tensor_tensor(bv_both[:, :], cols[:, 7:8], cols[:, 8:9], ALU.add).then_inc(bv_made, 1)
            dve.wait_ge(bv_made, 1)
            V.tensor_copy(bv_wide[:, :], bv_both[:, 0:1].broadcast_to([P, P])).then_inc(bv_ready, 1)
            dve.wait_ge(bp_made, 1)
            V.tensor_tensor(bp_eff[:, :], bank_t[:, 0:E], rows[:, 1, :], ALU.add).then_inc(bp_ready, 1)

            def bn(batch, which, res):
                dve.wait_ge(res_ready[which], batch.count(1, 1))
                for t in range(NT):
                    V.bn_stats(stats[which][:, t, :], res[:, t, :]).then_inc(stats_ready[which], 1)
                dve.wait_ge(stats_ready[which], batch.count(NT, NT))
                dve.sem_inc(dve_met, 1)
                for t in range(NT):
                    V.bn_aggr(mv[which][:, t, :], stats[which][:, t, :]).then_inc(mv_ready[which], 1)

            def normalise(batch, which, res, dst, done):
                dve.wait_ge(rstd_ready[which], batch.count(1, 1))
                for t in range(NT):
                    last = V.tensor_scalar(dst[:, t, :], res[:, t, :], mv[which][:, t, 0:1], rstd[which][:, t:t + 1],
                                           ALU.subtract, ALU.mult)
                last.then_inc(done, 1)

            def local_products(batch):
                dve.wait_ge(qk1_ready, batch.count(2, 2))
                V.tensor_scalar(k0_heads[:, :], head_of, k1[:, 2:3], None, ALU.mult).then_inc(heads0_ready, 1)
                V.tensor_scalar(q0_heads[:, :], same_head, q1[:, 0:1], None, ALU.mult).then_inc(heads0_ready, 1)

            def local_scores(batch):
                dve.wait_ge(local_filled, batch.count(UNITS_L, 3))
                flat = lambda t: t[:, :, :].rearrange("p c x -> p (c x)")
                n = CAND * NT * H
                V.scalar_tensor_tensor(flat(lsc), bank_x[0][:, 0:n], SCALE, cand_bias[:, :], ALU.mult, ALU.add
                                       ).then_inc(lsc_step, 1)
                V.scalar_tensor_tensor(r0s[:, :], bank_x[0][:, S:2 * S], SCALE, row0_bias[:, :], ALU.mult, ALU.add
                                       ).then_inc(r0_step, 1)

            def local_max(batch):
                dve.wait_ge(lsc_step, batch.count(6, 1))
                V.tensor_reduce(lmax[:, :], lsc[:, :, :].rearrange("p c x -> p x c"), X, ALU.max).then_inc(lsc_step, 1)
                dve.wait_ge(r0_step, batch.count(3, 1))
                V.tensor_scalar(r0g[:, :], r0s[:, :], 0.0, NEG, ALU.is_lt, ALU.mult).then_inc(r0_step, 1)
                dve.wait_ge(lsc_step, batch.count(6, 2))
                V.tensor_scalar(lmax[:, :], lmax[:, :], 0.0, None, ALU.max).then_inc(lsc_step, 1)
                dve.wait_ge(r0_step, batch.count(3, 2))
                V.scalar_tensor_tensor(r0v[:, :], r0s[:, :], 0.0, r0g[:, :], ALU.max, ALU.add).then_inc(r0_step, 1)
                dve.wait_ge(lsc_step, batch.count(6, 3))
                V.tensor_tensor(lneg[:, :, :], lmax[:, :].unsqueeze(1).broadcast_to([P, CAND, NT * H]), lsc[:, :, :],
                                ALU.subtract).then_inc(lneg_ready, 1)
                dve.wait_ge(r0_step, batch.count(3, 3))
                V.tensor_reduce(r0max[:, :], r0v[:, :], X, ALU.max, negate=True).then_inc(r0max_ready, 1)

            def local_gate(batch):
                dve.wait_ge(lexp_ready, batch.count(1, 1))
                V.scalar_tensor_tensor(lgated[:, :, :], lsc[:, :, :], 0.0, lexp[:, :, :], ALU.is_ge, ALU.mult
                                       ).then_inc(lsc_step, 1)

            def local_sum(batch):
                dve.wait_ge(lsc_step, batch.count(6, 4))
                V.tensor_reduce(lsum[:, :], lgated[:, :, :].rearrange("p c x -> p x c"), X, ALU.add).then_inc(lsc_step, 1)
                dve.wait_ge(r0exp_ready, batch.count(1, 1))
                dve.wait_ge(lsc_step, batch.count(6, 5))
                V.tensor_scalar(lnone[:, :], lsum[:, :], 0.0, None, ALU.is_equal).then_inc(lsc_step, 1)
                V.reciprocal(r0rec[:, :], r0sum[:, :]).then_inc(r0rec_ready, 1)
                dve.wait_ge(lsc_step, batch.count(6, 6))
                V.scalar_tensor_tensor(lden[:, :], lnone[:, :], float(S), lsum[:, :], ALU.mult, ALU.add).then_inc(lden_ready, 1)

            def local_probs(batch):
                dve.wait_ge(lden_ready, batch.count(1, 1))
                V.reciprocal(lrec[:, :], lden[:, :]).then_inc(lrec_ready, 1)
                dve.wait_ge(lrec_ready, batch.count(1, 1))
                th_ = lambda a: a.rearrange("p c (t h) -> p c t h", t=NT)
                V.tensor_tensor(probs[:, :, 0:CAND, :].rearrange("p t c h -> p c t h"), th_(lgated[:, :, :]),
                                th_(lrec[:, :].unsqueeze(1).broadcast_to([P, CAND, NT * H])), ALU.mult)
                V.tensor_tensor(probs[:, :, CAND, :], lnone[:, :].rearrange("p (t h) -> p t h", t=NT),
                                lrec[:, :].rearrange("p (t h) -> p t h", t=NT), ALU.mult).then_inc(probs_ready, 1)

            def window(first, n):
                return bass.AP(v1[:, :].tensor, first, [[S + WIN - 1, P], [1, n], [1, S]])

            def spread_products(batch, arg):
                u, dst = (5, pv01) if arg == "0" else (6, pv23)
                dve.wait_ge(local_filled, batch.count(UNITS_L, u))
                V.tensor_tensor(dst[:, :, :], bank_x[(u - 1) % 2][:, :].rearrange("p (a t) -> p a t", a=2),
                                window(int(arg), 2), ALU.mult).then_inc(pv_ready, 1)

            def local_spread4(batch):
                dve.wait_ge(local_filled, batch.count(UNITS_L, 7))
                V.tensor_tensor(pv4[:, :], bank_x[0][:, 0:S], v1[:, 4:4 + S], ALU.mult).then_inc(acc_step, 1)
                dve.wait_ge(acc_step, batch.count(2, 1))
                V.scalar_tensor_tensor(pv5[:, :], bank_x[0][:, S:2 * S], v1[:, 2:3], pv4[:, :], ALU.mult, ALU.add
                                       ).then_inc(acc_step, 1)

            def local_spread6(batch):
                dve.wait_ge(acc_step, batch.count(2, 2))
                dve.wait_ge(local_filled, batch.count(UNITS_L, 8))
                V.scalar_tensor_tensor(pv6[:, :], bank_x[1][:, 0:S], v1_sum[:, 0:1], pv5[:, :], ALU.mult, ALU.add
                                       ).then_inc(pvall_ready, 1)

            def local_context(batch):
                dve.wait_ge(pvall_ready, batch.count(1, 1))
                dve.wait_ge(pvsum_ready, batch.count(2, 2))
                V.tensor_tensor(lctx[:, :], pvall[:, :], pv6[:, :], ALU.add).then_inc(lctx_made, 1)
                dve.wait_ge(lctx_made, batch.count(1, 1))
                dve.wait_ge(r0rec_ready, batch.count(1, 1))
                dve.wait_ge(r0num_ready, batch.count(1, 1))
                V.tensor_tensor(lctx[:, 0:1], r0num[:, :], r0rec[:, :], ALU.mult).then_inc(lctx_ready, 1)

            def local_out(batch):
                dve.wait_ge(local_filled, batch.count(UNITS_L, 9))
                dve.wait_ge(xb_ready, batch.count(1, 1))
                V.tensor_tensor(res1[:, :, :], bank_x[0][:, 0:2 * E].rearrange("p (t c) -> p t c", t=NT), xb[:, :, :],
                                ALU.add).then_inc(res_ready[0], 1)

            def local_norm1(batch):
                if batch.reaches(1, -2):
                    dve.wait_ge(x1res_ready, batch.count(1, -2))
                normalise(batch, 0, res1, x1[:, batch.buf], x1_ready)

            def rowmax_late(batch, arg):
                pair = int(arg)
                h = slice(2 * pair, 2 * pair + 2)
                dve.wait_ge(rowmax_filled, batch.count(UNITS_M, 2 * pair + 1))
                V.tensor_reduce(rmax[:, 1, 0, h], bank_m[0][:, :].rearrange("p (v k) -> p v k", v=2), X, ALU.max
                                ).then_inc(rowmax_read[0], 1)

            def rowmax_early(batch, arg):
                pair = int(arg)
                h = slice(2 * pair, 2 * pair + 2)
                dve.wait_ge(rowmax_filled, batch.count(UNITS_M, 2 * pair + 2))
                V.tensor_reduce(rmax[:, 0, 0, h], bank_m[1][:, 0:2 * P].rearrange("p (v k) -> p v k", v=2), X, ALU.max)
                V.tensor_reduce(rmax[:, :, 1, h], bank_m[1][:, 2 * P:4 * P].rearrange("p (t v k) -> p t v k", t=NT, v=2), X,
                                ALU.max).then_inc(rowmax_read[1], 1)

            def rowmax_shift(batch):
                dve.wait_ge(rowmax_read[0], batch.count(8, 8))
                dve.wait_ge(rowmax_read[1], batch.count(8, 8))
                for v in range(2):
                    m = rmax[:, :, :, :].rearrange("p t k (q v) -> p v q k t", v=2)[:, v]
                    V.tensor_scalar(shift[:, 0, v], m, -1.0, None, ALU.mult).then_inc(shift_hi_ready, 1)
                dve.wait_ge(shift_hi_ready, batch.count(2, 2))
                for v in range(2):
                    m = rmax[:, :, :, :].rearrange("p t k (q v) -> p v q k t", v=2)[:, v]
                    V.tensor_tensor(rneg[:, v], m, shift[:, 0, v], ALU.add).then_inc(rneg_ready, 1)
                dve.wait_ge(rneg_ready, batch.count(2, 2))
                V.tensor_scalar(shift[:, 1], rneg[:, :], -1.0, None, ALU.mult).then_inc(shift_ready, 1)

            def rowmax_shift_t(batch):
                dve.wait_ge(rowmax_filled, batch.count(UNITS_M, UNITS_M))
                if batch.reaches(16, 0):
                    dve.wait_ge(shift_loaded, batch.count(16, 0))
                V.tensor_copy(shift_t[:, :], bank_m[0][:, 0:P // 2].bitcast(bf16)).then_inc(shift_t_ready, 1)

            def tail_self(batch, t):
                dve.wait_ge(tail_filled, batch.count(UNITS_T, 1 if t == 0 else 3))
                heads = bank_t[:, :].rearrange("p (h c) -> p h c", c=32)
                V.reciprocal(rec_s[:, t, :], heads[:, :, D]).then_inc(rec_step, 1)
                dve.wait_ge(rec_step, batch.count(3, 1 if t == 0 else 3))
                V.tensor_tensor(y_s[:, t, :].rearrange("p (h d) -> p h d", d=D), heads[:, :, 0:D],
                                rec_s[:, t, :].unsqueeze(2).broadcast_to([P, H, D]), ALU.mult).then_inc(ys_ready, 1)

            def tail_cross(batch):
                dve.wait_ge(tail_filled, batch.count(UNITS_T, 2))
                pairs = bank_t[:, :].rearrange("p (q c) -> p q c", c=32)[:, :, 0:2 * (D + 1)].rearrange(
                    "p q (v c) -> p q v c", v=2)
                V.reciprocal(rec_c[:, :, :], pairs[:, :, :, D]).then_inc(rec_step, 1)
                dve.wait_ge(rec_step, batch.count(3, 2))
                V.tensor_tensor(y_c[:, :, :].rearrange("p q (v d) -> p q v d", v=2), pairs[:, :, :, 0:D],
                                rec_c[:, :, :].unsqueeze(3).broadcast_to([P, NT * PAIRS, 2, D]), ALU.mult).then_inc(yc_ready, 1)

            def tail_res(batch, which, unit, skip, res):
                dve.wait_ge(tail_filled, batch.count(UNITS_T, unit))
                if which == 1:
                    dve.wait_ge(x1res_ready, batch.count(1, 1))
                V.tensor_tensor(res[:, :, :], bank_t[:, 0:2 * E].rearrange("p (t c) -> p t c", t=NT), skip, ALU.add
                                ).then_inc(res_ready[which], 1)

            def tail_up(batch, arg):
                i = int(arg)
                dve.wait_ge(tanh_ready, batch.count(3, i + 1))
                V.scalar_tensor_tensor(ga[:, i, :], th[:, i, :], 1.0, bank_t[:, 0:S], ALU.add, ALU.mult).then_inc(gate_ready, 1)
                dve.wait_ge(gate_ready, batch.count(3, i + 1))
                V.scalar_tensor_tensor(hid[:, i, :], ga[:, i, :], 0.5, bank_t[:, S:2 * S], ALU.mult, ALU.mult
                                       ).then_inc(hid_ready, 1)

            def tail_norm3(batch):
                if batch.reaches(16, 0):
                    dve.wait_ge(out_stored, batch.count(16, 0))
                normalise(batch, 2, res3, o_sb, out_ready)

            pipeline(dve, DVE_ORDER, {
                "local.products": local_products,
                "local.scores": local_scores,
                "local.max": local_max,
                "local.gate": local_gate,
                "local.sum": local_sum,
                "local.probs": local_probs,
                "spread": spread_products,
                "local.spread4": local_spread4,
                "local.spread6": local_spread6,
                "local.context": local_context,
                "local.res": local_out,
                "local.stats": lambda batch: bn(batch, 0, res1),
                "local.norm": local_norm1,
                "late": rowmax_late,
                "early": rowmax_early,
                "rowmax.shift": rowmax_shift,
                "rowmax.shift_t": rowmax_shift_t,
                "tail.self0": lambda batch: tail_self(batch, 0),
                "tail.cross": tail_cross,
                "tail.self1": lambda batch: tail_self(batch, 1),
                "tail.res2": lambda batch: tail_res(batch, 1, 5, x1res[:, batch.buf], res2),
                "tail.stats2": lambda batch: bn(batch, 1, res2),
                "tail.norm2": lambda batch: normalise(batch, 1, res2, x2, x2_ready),
                "up": tail_up,
                "tail.res3": lambda batch: tail_res(batch, 2, 10, x2[:, :, :], res3),
                "tail.stats3": lambda batch: bn(batch, 2, res3),
                "tail.norm3": tail_norm3,
            })

        @block.gpsimd
        def _(pool):
            TT = nc.gpsimd.tensor_tensor
            pool.wait_ge(weights_loaded, WEIGHTS)
            pool.wait_ge(pads_set, 8)
            pool.wait_ge(bp_ready, 1)

            def rsqrt(batch, which):
                pool.wait_ge(mv_ready[which], batch.count(NT, NT))
                TT(veps[which][:, :], mv[which][:, :, 1], small[:, 0:2], ALU.add).then_inc(veps_ready[which], 1)
                pool.wait_ge(veps_ready[which], batch.count(1, 1))
                TT(rstd[which][:, :], veps[which][:, :], small[:, 2:4], ALU.pow).then_inc(rstd_ready[which], 1)

            def local_xb(batch):
                pool.wait_ge(x_loaded, batch.count(64, 64))
                TT(xb[:, :, :], x_sb[:, batch.buf, :, :], rows[:, 0, :].unsqueeze(1).broadcast_to([P, NT, E]), ALU.add
                   ).then_inc(xb_ready, 1)

            def local_products(batch):
                pool.wait_ge(qk1_ready, batch.count(2, 2))
                TT(prod[:, :, :], bass.AP(k1[:, :].tensor, 0, [[S + WIN - 1, P], [1, WIN], [1, S]]),
                   q1[:, :].unsqueeze(1).broadcast_to([P, WIN, S]), ALU.mult).then_inc(prod_ready, 1)

            def local_prob_rest(batch):
                pool.wait_ge(prob_hi_ready, batch.count(1, 1))
                TT(prob_rest[:, :, :, :], probs[:, :, :, :], prob_parts[:, :, 0:CAND + 1, 0, :], ALU.subtract
                   ).then_inc(prob_rest_ready, 1)

            def local_prob_lo(batch):
                pool.wait_ge(prob_mid_ready, batch.count(1, 1))
                TT(prob_parts[:, :, 0:CAND + 1, 2, :], prob_rest[:, :, :, :], prob_parts[:, :, 0:CAND + 1, 1, :], ALU.subtract
                   ).then_inc(prob_lo_ready, 1)

            def local_row0_products(batch):
                pool.wait_ge(v1_ready, batch.count(1, 1))
                pool.wait_ge(r0exp_ready, batch.count(1, 1))
                TT(r0pv[:, :], r0exp[:, :], v1[:, 2:2 + S], ALU.mult).then_inc(r0pv_ready, 1)

            def local_context(batch):
                pool.wait_ge(pv_ready, batch.count(2, 2))
                TT(pvsum[:, :, :], pv01[:, :, :], pv23[:, :, :], ALU.add).then_inc(pvsum_ready, 1)
                pool.wait_ge(pvsum_ready, batch.count(2, 1))
                TT(pvall[:, :], pvsum[:, 0, :], pvsum[:, 1, :], ALU.add).then_inc(pvsum_ready, 1)

            def project_rest(batch):
                pool.wait_ge(hi_ready, batch.count(1, 1))
                TT(rest[:, :], full[:, :], parts[:, 0, :], ALU.subtract).then_inc(rest_ready, 1)

            def project_lo(batch):
                pool.wait_ge(mid_ready, batch.count(1, 1))
                TT(parts[:, 2, :], rest[:, :], parts[:, 1, :], ALU.subtract).then_inc(lo_ready, 1)

            def rowmax_x1res(batch):
                pool.wait_ge(x1_ready, batch.count(1, 1))
                if batch.reaches(1, -2):
                    pool.wait_ge(res_ready[1], batch.count(1, -2))
                TT(x1res[:, batch.buf, :, :], x1[:, batch.buf, :, :], bp_eff[:, :].unsqueeze(1).broadcast_to([P, NT, E]),
                   ALU.add).then_inc(x1res_ready, 1)

            def mask(batch, arg):
                h = int(arg)
                pool.wait_ge(exp_done, batch.count(UNITS_S, h // 4 * 5 + h % 4 + 1))
                pool.sem_inc(pool_met, 1)
                diag = p_self[:, h % RING, :].rearrange("p (a q) -> p a q", q=P)[:, 0:3:2, :]
                nc.gpsimd.affine_select(out=diag, in_=diag, compare_op=ALU.is_ge, fill=0.0, base=0,
                                        pattern=[[0, 2], [1, P]], channel_multiplier=-1).then_inc(masked, 1)

            def tail_y(batch):
                pool.wait_ge(ys_ready, batch.count(2, 2))
                pool.wait_ge(yc_ready, batch.count(1, 1))
                TT(y[:, :, :].rearrange("p t c -> p (t c)"), y_s[:, :, :].rearrange("p t c -> p (t c)"),
                   y_c[:, :, :].rearrange("p q c -> p (q c)"), ALU.add).then_inc(y_ready, 1)

            pipeline(pool, POOL_ORDER, {
                "local.xb": local_xb,
                "local.products": local_products,
                "local.prob_rest": local_prob_rest,
                "local.prob_lo": local_prob_lo,
                "local.row0_products": local_row0_products,
                "local.context": local_context,
                "local.rstd": lambda batch: rsqrt(batch, 0),
                "project.rest": project_rest,
                "project.lo": project_lo,
                "rowmax.x1res": rowmax_x1res,
                "mask": mask,
                "tail.y": tail_y,
                "tail.rstd2": lambda batch: rsqrt(batch, 1),
                "tail.rstd3": lambda batch: rsqrt(batch, 2),
            })


def constants():
    import numpy as np
    head = np.arange(P) // D
    f32c = np.concatenate([np.eye(P), head[:, None] == head[None, :], head[:, None] == np.arange(H)[None, :]],
                          1).astype(np.float32)

    def pos_bias(diff):
        diff = diff.astype(np.float32)
        return (np.exp(np.float32(-0.5) * (diff / np.float32(2.0)) ** 2)
                + np.cos(np.float32(2.0 * np.pi) * diff / np.float32(401.0))).astype(np.float32)

    tok = np.arange(NT)[None, :] * P + np.arange(P)[:, None]
    cand = np.zeros((P, CAND, NT, H), np.float32)
    for c in range(WIN):
        key = tok + c - WIN // 2
        ok = (key >= 1) & (key < S)
        cand[:, c] = np.where(ok, pos_bias(tok - key), np.float32(-1e30))[:, :, None]
    cand[:, WIN] = pos_bias(tok)[:, :, None]
    row0 = np.broadcast_to(pos_bias(-np.arange(S))[None, :], (P, S))
    bias = np.ascontiguousarray(np.concatenate([cand.reshape(P, -1), row0], 1))
    spread = np.zeros((2, 3, H, 2, P), np.float32)
    for c in range(2):
        spread[c, :, :, c, :] = head[None, :] == np.arange(H)[:, None]
    spread = spread.reshape(PROB_ROWS, 2, P)
    i, j = np.arange(P)[:, None], np.arange(P)[None, :]
    b16 = np.concatenate([np.eye(P), np.where(j <= i, 0.0, -3e38)], 1)
    rows = np.zeros((KROWS, 2 * S + 2 * SC), np.float32)
    for part in range(2):
        for par in range(2):
            r = ROWS + 2 * part + par
            rows[r, par * S:(par + 1) * S] = 1.0
            rows[r, 2 * S + par * SC:2 * S + (par + 1) * SC] = 1.0
    bits = lambda v: (np.ascontiguousarray(v, np.float32).view(np.uint32) >> 16).astype(np.uint16)
    return f32c, bias, bits(spread), bits(b16), bits(rows)


def kernel(**inputs):
    import numpy as np
    import concourse.bacc as bacc
    from concourse.bass_utils import run_bass_kernel_spmd

    a = {k: np.asarray(v) for k, v in inputs.items()}
    local = lambda n: a["L0_attn_" + n]
    cross = lambda n: a["L0_xattn_" + n]
    k_f32, k_bias, k_spread, k_bf16, k_rows = constants()
    arrays = {
        "x": a["x"],
        "xt": a["x"].transpose(0, 2, 1),
        "ctxt": a["ctx_512"].transpose(0, 2, 1),
        "w1": np.stack([local(n).T for n in ("wq", "wk", "wv", "wo")], 1),
        "w2": np.stack([cross(n) for n in ("Wq", "Wk", "Wv", "Wcq", "Wp")], 1),
        "wck": cross("Wck"),
        "wcv": cross("Wcv"),
        "bias_cols": np.stack([local("bq"), local("bk"), local("bv"), cross("bq"), cross("bk"), cross("bcq"),
                               cross("bck"), cross("bv"), cross("bcv")], 1),
        "bias_rows": np.stack([local("bo"), cross("bp")], 0),
        "wgu": np.concatenate([a["L0_ffn_w_gate"].T, a["L0_ffn_w_up"].T], 1),
        "wd": a["L0_ffn_w_down"].T.reshape(3, P, E).transpose(1, 0, 2),
        "k_f32": k_f32, "k_bias": k_bias, "k_spread": k_spread, "k_bf16": k_bf16, "k_rows": k_rows,
    }
    arrays = {k: np.ascontiguousarray(v) for k, v in arrays.items()}
    nc = bacc.Bacc("TRN2", target_bir_lowering=False, num_devices=1)
    args = {k: nc.dram_tensor(k, list(v.shape), mybir.dt.from_np(v.dtype), kind="ExternalInput").ap()
            for k, v in arrays.items()}
    out = nc.dram_tensor("out", [B, S, E], mybir.dt.float32, kind="ExternalOutput").ap()
    decoder_layer(nc, out=out, **args)
    r = run_bass_kernel_spmd(nc, [arrays], core_ids=[0])
    return r.results[0]["out"]
```

```python
import concourse.bass as bass
from concourse import mybir
from contextlib import ExitStack

B, S, E, H, D = 16, 256, 128, 16, 8
SC, CC, HID = 64, 64, 384
P = 128
NT = S // P
PAIRS = H // 2
TERMS = 6
ROWS = 2 * D * TERMS
PROB_ROWS = 2 * 3 * H
KROWS = ROWS + 4
WIN = 5
CAND = WIN + 1
SCALE = float(D) ** -0.5
EPS = 1e-5
NEG = -1e9
NBUF = 3

SP_ORDER = [
    "3:project.out 0:local.load 3:project.in 4:rowmax.in 7:tail.store",
]
PE_ORDER = [
    "3:late.2 4:attend.6 5:tail.y 2:project.k 4:attend.7 3:early.2 4:attend.8 5:tail.proj 2:project.v",
    "3:late.3 4:attend.9 3:early.3 4:pv.self0 4:attend.10 4:attend.11 3:late.4 4:pv.cross0 4:attend.12",
    "3:early.4 5:tail.x2t 4:attend.13 3:late.5 4:attend.14 5:tail.up0 3:early.5 4:attend.15 3:late.6",
    "4:pv.self1 1:local.probs_t 3:early.6 4:attend.16 4:attend.17 3:late.7 1:local.spread0 3:early.7",
    "5:tail.up1 1:local.spread2 4:attend.18 4:pv.self2 0:local.qk 1:local.spread4 3:rowmax.shift_t",
    "4:attend.19 4:pv.self3 5:tail.up2 1:local.spread6 4:pv.cross1 0:local.v 4:tail.self0 1:local.out",
    "3:attend.0 3:attend.1 2:late.0 2:early.0 0:local.scores 4:tail.cross 3:attend.2 2:late.1 5:tail.down",
    "1:local.x1t 4:tail.self1 3:attend.3 3:attend.4 1:project.q 2:early.1 3:attend.5",
]
ACT_ORDER = [
    "5:tail.x2t 1:local.prob_hi 4:attend.13 1:local.prob_mid 4:attend.14 5:up.0 1:local.row0_num 4:attend.15",
    "1:local.probs_t 4:attend.16 4:pv.self1 4:attend.17 5:up.1 4:attend.18 4:pv.self2 0:local.qk 4:attend.19",
    "4:pv.self3 5:up.2 4:pv.cross1 0:local.v 3:attend.0 3:attend.1 3:attend.2 1:local.x1t 3:attend.3",
    "3:attend.4 1:project.q 3:attend.5 3:attend.6 0:local.exp 4:tail.y 1:project.k 3:attend.7 1:project.hi",
    "0:local.exp_row0 3:attend.8 3:attend.9 1:project.v 3:pv.self0 1:project.mid 3:attend.10 3:attend.11",
    "3:pv.cross0 3:attend.12",
]
DVE_ORDER = [
    "3:late.7 1:spread.0 3:early.7 1:spread.2 3:rowmax.shift 5:up.1 3:rowmax.shift_t 1:local.spread4",
    "0:local.products 1:local.spread6 1:local.context 5:up.2 1:local.res 4:tail.self0 1:local.stats 2:late.0",
    "2:early.0 1:local.norm 4:tail.cross 2:late.1 0:local.scores 5:tail.res3 4:tail.self1 0:local.max",
    "2:early.1 5:tail.stats3 0:local.gate 2:late.2 2:early.2 4:tail.res2 0:local.sum 4:tail.stats2 2:late.3",
    "2:early.3 4:tail.norm2 2:late.4 0:local.probs 2:early.4 2:late.5 5:tail.norm3 2:early.5 2:late.6 4:up.0",
    "2:early.6",
]
POOL_ORDER = [
    "4:mask.6 2:project.rest 5:tail.rstd2 1:local.row0_products 2:project.lo 1:local.prob_rest 4:mask.7",
    "1:local.prob_lo 4:mask.8 4:mask.9 4:mask.10 4:mask.11 2:rowmax.x1res 4:mask.12 4:mask.13 1:local.xb",
    "4:mask.14 4:mask.15 1:local.context 0:local.products 1:local.rstd 3:mask.0 3:mask.1 3:mask.2 4:tail.y",
    "3:mask.3 3:mask.4 3:mask.5 5:tail.rstd3",
]
BUFFER_REUSE = ("local.load", "project.in", "rowmax.in", "project.v", "rowmax.x1res", "local.norm")


class Batch:

    def __init__(self, loop, offset):
        self.loop, self.offset, self.buf = loop, offset, offset % NBUF

    def count(self, each, add):
        value = self.offset * each + add
        return value if self.loop is None else self.loop * (NBUF * each) + value

    def reaches(self, each, add):
        return self.loop is not None or self.offset * each + add > 0

    def index(self):
        return self.count(1, 0)


def pipeline(eng, order, steps):
    def iteration(loop, n):
        for line in order:
            for entry in line.split():
                lag, name = entry.split(":")
                k = n - int(lag)
                if loop is None and not 0 <= k < B:
                    continue
                if name in steps:
                    steps[name](Batch(loop, k))
                else:
                    phase, arg = name.split(".")
                    steps[phase](Batch(loop, k), arg)
    entries = [entry.split(":") for line in order for entry in line.split()]
    first = max(int(lag) + (NBUF if name in BUFFER_REUSE else 1) for lag, name in entries)
    last = B + max(int(lag) for lag, _ in entries)
    full = (B - first) // NBUF * NBUF
    for n in range(first):
        iteration(None, n)
    with eng.Fori(0, full // NBUF) as i:
        for r in range(NBUF):
            iteration(i, first + r)
    for n in range(first + full, last):
        iteration(None, n)


def decoder_layer(nc, x, xt, ctxt, w1, w2, wck, wcv, bias_cols, bias_rows, wgu, wd, k_f32, k_bias, k_spread, k_bf16, k_rows, out):
    k_spread, k_bf16, k_rows = (a.bitcast(mybir.dt.bfloat16) for a in (k_spread, k_bf16, k_rows))
    f32, bf16, i32 = mybir.dt.float32, mybir.dt.bfloat16, mybir.dt.int32
    ALU, ACT = mybir.AluOpType, mybir.ActivationFunctionType
    X = mybir.AxisListType.X
    QC = 2 * S
    COLS = QC + S + SC

    parts_dram = nc.dram_tensor("parts_dram", [P, TERMS, COLS], bf16).ap()

    stack = ExitStack()
    with stack:
        def sb(name, shape, dt=f32):
            return stack.enter_context(nc.sbuf_tensor(name, shape, dt))

        def ps(name, shape=(P, 512)):
            return stack.enter_context(nc.psum_tensor(name, list(shape), f32))

        def sem(name):
            return stack.enter_context(nc.semaphore(name))

        w1_sb = sb("w1_sb", [P, 4, E])
        w2_sb = sb("w2_sb", [P, 5, E])
        wck_sb = sb("wck_sb", [CC, E])
        wcv_sb = sb("wcv_sb", [CC, E])
        wgu_int = sb("wgu_int", [P, 2 * HID], i32)
        wd_int = sb("wd_int", [P, 3, E], i32)
        wgu_sb = sb("wgu_sb", [P, 2 * HID])
        wd_sb = sb("wd_sb", [P, 3, E])
        cols = sb("cols", [P, 9])
        rows = sb("rows", [P, 2, E])
        consts = sb("consts", [P, 2 * P + H])
        cand_bias = sb("cand_bias", [P, CAND * NT * H])
        row0_bias = sb("row0_bias", [P, S])
        spread = sb("spread", [PROB_ROWS, 2, P], bf16)
        const16 = sb("const16", [P, 2 * P], bf16)
        small = sb("small", [P, 4])
        bv_both = sb("bv_both", [P, 1])
        bv_wide = sb("bv_wide", [P, P])
        bp_eff = sb("bp_eff", [P, E])
        ident, same_head, head_of = consts[:, 0:P], consts[:, P:2 * P], consts[:, 2 * P:2 * P + H]
        ident16, causal_q = const16[:, 0:P], const16[:, P:2 * P]

        x_sb = sb("x_sb", [P, NBUF, NT, E])
        xt_sb = sb("xt_sb", [P, NBUF, S])
        ctxt_sb = sb("ctxt_sb", [CC, NBUF, 2 * SC])
        xb = sb("xb", [P, NT, E])
        q1 = sb("q1", [P, S])
        k1 = sb("k1", [P, S + WIN - 1])
        v1 = sb("v1", [P, NBUF, S + WIN - 1])
        v1_sum = sb("v1_sum", [P, NBUF])
        prod = sb("prod", [P, WIN, S])
        k0_heads = sb("k0_heads", [P, H])
        q0_heads = sb("q0_heads", [P, P])
        lsc = sb("lsc", [P, CAND, NT * H])
        lmax = sb("lmax", [P, NT * H])
        lneg = sb("lneg", [P, CAND, NT * H])
        lexp = sb("lexp", [P, CAND, NT * H])
        lgated = sb("lgated", [P, CAND, NT * H])
        lsum = sb("lsum", [P, NT * H])
        lnone = sb("lnone", [P, NT * H])
        lden = sb("lden", [P, NT * H])
        lrec = sb("lrec", [P, NT * H])
        probs = sb("probs", [P, NT, CAND + 1, H])
        prob_rest = sb("prob_rest", [P, NT, CAND + 1, H])
        prob_parts = sb("prob_parts", [P, NT, CAND + 2, 3, H], bf16)
        probs_t = sb("probs_t", [PROB_ROWS, NBUF, 4, S], bf16)
        r0s = sb("r0s", [P, S])
        r0g = sb("r0g", [P, S])
        r0v = sb("r0v", [P, S])
        r0max = sb("r0max", [P, 1])
        r0exp = sb("r0exp", [P, S])
        r0sum = sb("r0sum", [P, 1])
        r0pv = sb("r0pv", [P, S])
        r0num = sb("r0num", [P, NBUF])
        r0all = sb("r0all", [P, S])
        r0rec = sb("r0rec", [P, NBUF])
        pv01 = sb("pv01", [P, 2, S])
        pv23 = sb("pv23", [P, 2, S])
        pv4 = sb("pv4", [P, S])
        pv5 = sb("pv5", [P, S])
        pv6 = sb("pv6", [P, S])
        pvsum = sb("pvsum", [P, 2, S])
        pvall = sb("pvall", [P, S])
        lctx = sb("lctx", [P, S])
        res1 = sb("res1", [P, NT, E])
        x1 = sb("x1", [P, NBUF, NT, E])
        x1t = sb("x1t", [P, NBUF, S])

        parts = sb("parts", [P, 3, COLS], bf16)
        full = sb("full", [P, COLS])
        rest = sb("rest", [P, COLS])
        q_st = sb("q_st", [KROWS, NBUF, PAIRS, QC], bf16)
        k_st = sb("k_st", [KROWS, NBUF, PAIRS, 2, S], bf16)
        kc_st = sb("kc_st", [KROWS, NBUF, PAIRS, 2 * SC], bf16)
        v_sb = sb("v_sb", [P, NBUF, NT, H, 32])
        vc_sb = sb("vc_sb", [P, NBUF, PAIRS, 32])

        rmax = sb("rmax", [P, NT, 2, H])
        rneg = sb("rneg", [P, 2, PAIRS, 2, NT])
        shift = sb("shift", [P, 2, 2, PAIRS, 2, NT], bf16)
        shift_t = sb("shift_t", [P, P], bf16)
        x1res = sb("x1res", [P, NBUF, NT, E])

        RING, CRING = 8, 4
        p_self = sb("p_self", [P, RING, 3 * P])
        p_cross = sb("p_cross", [P, CRING, 2, S])
        y_t = sb("y_t", [P, 6, S])

        rec_s = sb("rec_s", [P, NT, H])
        rec_c = sb("rec_c", [P, NT * PAIRS, 2])
        y_s = sb("y_s", [P, NT, E])
        y_c = sb("y_c", [P, NT * PAIRS, 2 * D])
        y = sb("y", [P, NT, E])
        yt = sb("yt", [P, S])
        res2 = sb("res2", [P, NT, E])
        x2 = sb("x2", [P, NBUF, NT, E])
        x2t = sb("x2t", [P, S])
        th = sb("th", [P, 3, S])
        ga = sb("ga", [P, 3, S])
        hid = sb("hid", [P, 3, S])
        res3 = sb("res3", [P, NT, E])
        o_sb = sb("o_sb", [P, NT, E])
        stats = [sb(f"stats{i}", [P, NT, 6]) for i in range(3)]
        mv = [sb(f"mv{i}", [P, NT, 2]) for i in range(3)]
        veps = [sb(f"veps{i}", [P, NT]) for i in range(3)]
        rstd = [sb(f"rstd{i}", [P, NT]) for i in range(3)]

        bank_l = ps("bank_l")
        bank_p = ps("bank_p")
        bank_m = [ps("bank_m0"), ps("bank_m1")]
        bank_s = [ps("bank_s0"), ps("bank_s1")]
        bank_v = ps("bank_v")
        bank_t = ps("bank_t")

        local_weights_loaded, weights_loaded = sem("local_weights_loaded"), sem("weights_loaded")
        sp_met, dve_met, pool_met = sem("sp_met"), sem("dve_met"), sem("pool_met")
        stacks_set = sem("stacks_set")
        pads_set = sem("pads_set")
        weights_ready = sem("weights_ready")
        zeros_set, bv_made = sem("zeros_set"), sem("bv_made")
        bv_ready = sem("bv_ready")
        bp_made = sem("bp_made")
        bp_ready = sem("bp_ready")
        x_loaded = sem("x_loaded")
        xb_ready = sem("xb_ready")
        local_filled = sem("local_filled")
        context_filled = sem("context_filled")
        qk1_ready, v1_ready, prod_ready, heads0_ready = map(sem, ("qk1_ready", "v1_ready", "prod_ready", "heads0_ready"))
        lsc_step = sem("lsc_step")
        lneg_ready, r0max_ready, lexp_ready, r0exp_ready = map(sem, ("lneg_ready", "r0max_ready", "lexp_ready", "r0exp_ready"))
        r0_step, r0pv_ready = sem("r0_step"), sem("r0pv_ready")
        r0num_ready, r0rec_ready, lden_ready, lrec_ready = map(sem, ("r0num_ready", "r0rec_ready", "lden_ready", "lrec_ready"))
        probs_ready, probs_t_ready = sem("probs_ready"), sem("probs_t_ready")
        prob_hi_ready, prob_rest_ready, prob_mid_ready, prob_lo_ready = map(
            sem, ("prob_hi_ready", "prob_rest_ready", "prob_mid_ready", "prob_lo_ready"))
        pv_ready, pvsum_ready, pvall_ready = sem("pv_ready"), sem("pvsum_ready"), sem("pvall_ready")
        acc_step = sem("acc_step")
        lctx_made, lctx_ready = sem("lctx_made"), sem("lctx_ready")
        res_ready = [sem(f"res_ready{i}") for i in range(3)]
        stats_ready = [sem(f"stats_ready{i}") for i in range(3)]
        mv_ready = [sem(f"mv_ready{i}") for i in range(3)]
        veps_ready = [sem(f"veps_ready{i}") for i in range(3)]
        rstd_ready = [sem(f"rstd_ready{i}") for i in range(3)]
        x1_ready, x1t_ready = sem("x1_ready"), sem("x1t_ready")
        project_filled = sem("project_filled")
        full_ready, hi_ready, rest_ready, mid_ready, lo_ready = map(sem, ("full_ready", "hi_ready", "rest_ready", "mid_ready", "lo_ready"))
        v_ready = sem("v_ready")
        parts_written, stacks_loaded = sem("parts_written"), sem("stacks_loaded")
        rowmax_filled = sem("rowmax_filled")
        rowmax_read = [sem("rowmax_read0"), sem("rowmax_read1")]
        shift_hi_ready, shift_ready = sem("shift_hi_ready"), sem("shift_ready")
        rneg_ready = sem("rneg_ready")
        shift_t_ready, shift_loaded = sem("shift_t_ready"), sem("shift_loaded")
        x1res_ready = sem("x1res_ready")
        scores_filled = sem("scores_filled")
        exp_done = sem("exp_done")
        masked = sem("masked")
        pv_filled, pv_emptied = sem("pv_filled"), sem("pv_emptied")
        mixed_filled = sem("mixed_filled")
        tail_filled = sem("tail_filled")
        rec_step = sem("rec_step")
        yc_ready = sem("yc_ready")
        ys_ready, y_ready, yt_ready, x2_ready, x2t_ready = map(sem, ("ys_ready", "y_ready", "yt_ready", "x2_ready", "x2t_ready"))
        tanh_ready, gate_ready, hid_ready = sem("tanh_ready"), sem("gate_ready"), sem("hid_ready")
        out_ready, out_stored = sem("out_ready"), sem("out_stored")

        LOCAL_WEIGHTS, WEIGHTS = 9 * 16, 5 * 16
        STACK_INIT = 6 * 16
        UNITS_L, UNITS_C, UNITS_P, UNITS_M, UNITS_S, UNITS_T = 4, 6, 3, 17, 20, 5
        block = stack.enter_context(nc.Block())

        @block.sync
        def _(sp):
            for dst, src in (
                (w1_sb[:, :, :], w1), (cols[:, :], bias_cols),
                (rows[:, 0, :], bias_rows[0:1, :].broadcast_to([P, E])),
                (rows[:, 1, :], bias_rows[1:2, :].broadcast_to([P, E])),
                (consts[:, :], k_f32), (cand_bias[:, :], k_bias[:, 0:CAND * NT * H]),
                (row0_bias[:, :], k_bias[:, CAND * NT * H:]), (spread[:, :, :], k_spread),
                (const16[:, :], k_bf16),
            ):
                sp.dma_start(dst, src).then_inc(local_weights_loaded, 16)

            def load_later_weights():
                for dst, src in (
                    (w2_sb[:, :, :], w2), (wck_sb[:, :], wck), (wcv_sb[:, :], wcv), (wgu_int[:, :], wgu), (wd_int[:, :, :], wd),
                ):
                    sp.dma_start(dst, src).then_inc(weights_loaded, 16)

            def set_stacks(b):
                sp.dma_start(k_st[:, b, :, :, :].rearrange("r p v t -> r p (v t)"),
                             k_rows[:, 0:2 * S].unsqueeze(1).broadcast_to([KROWS, PAIRS, 2 * S])).then_inc(stacks_set, 16)
                sp.dma_start(kc_st[:, b, :, :],
                             k_rows[:, 2 * S:].unsqueeze(1).broadcast_to([KROWS, PAIRS, 2 * SC])).then_inc(stacks_set, 16)

            def load(batch):
                b = batch.buf
                k = batch.index() if batch.loop is None else sp.snap(batch.index(), min_val=0, max_val=B - 1)
                if batch.reaches(64, 0):
                    sp.wait_ge(x_loaded, batch.count(64, 0))
                    sp.sem_inc(sp_met, 1)
                if batch.reaches(UNITS_P, -2 * UNITS_P):
                    sp.wait_ge(project_filled, batch.count(UNITS_P, -2 * UNITS_P))
                    sp.sem_inc(sp_met, 1)
                one = bass.ds(k, 1)
                sp.dma_start(xt_sb[:, b, :], xt[one, :, :].rearrange("a c t -> (a c) t")).then_inc(x_loaded, 16)
                sp.dma_start(x_sb[:, b, :, :], x[one, :, :].rearrange("a (i p) c -> (a p) i c", p=P)).then_inc(x_loaded, 16)
                for half in range(2):
                    sp.dma_start(ctxt_sb[:, b, half * SC:(half + 1) * SC],
                                 ctxt[one, :, :].rearrange("a c t -> (a c) t")).then_inc(x_loaded, 16)
                if batch.loop is None and batch.offset == 0:
                    load_later_weights()
                    for buf in range(NBUF):
                        set_stacks(buf)

            def parts_out(batch):
                if batch.reaches(96, 0):
                    sp.wait_ge(stacks_loaded, batch.count(96, 0))
                    sp.sem_inc(sp_met, 1)
                sp.wait_ge(hi_ready, batch.count(1, 1))
                sp.sem_inc(sp_met, 1)
                sp.wait_ge(mid_ready, batch.count(1, 1))
                sp.sem_inc(sp_met, 1)
                sp.wait_ge(lo_ready, batch.count(1, 1))
                sp.sem_inc(sp_met, 1)
                one_part = lambda part, n, c0, c1: parts[:, part, c0:c1].unsqueeze(1).broadcast_to([P, n, c1 - c0])
                sp.dma_start(parts_dram[:, 0:3, 0:QC], one_part(0, 3, 0, QC)).then_inc(parts_written, 16)
                sp.dma_start(parts_dram[:, 3:5, 0:QC], one_part(1, 2, 0, QC)).then_inc(parts_written, 16)
                sp.dma_start(parts_dram[:, 5:6, 0:QC], one_part(2, 1, 0, QC)).then_inc(parts_written, 16)
                sp.dma_start(parts_dram[:, 0:3, QC:COLS], parts[:, 0:3, QC:COLS]).then_inc(parts_written, 16)
                sp.dma_start(parts_dram[:, 3:5, QC:COLS], parts[:, 0:2, QC:COLS]).then_inc(parts_written, 16)
                sp.dma_start(parts_dram[:, 5:6, QC:COLS], one_part(0, 1, QC, COLS)).then_inc(parts_written, 16)

            def parts_in(batch):
                sp.wait_ge(parts_written, batch.count(96, 96))
                sp.sem_inc(sp_met, 1)
                if batch.reaches(UNITS_S, -2 * UNITS_S):
                    sp.wait_ge(scores_filled, batch.count(UNITS_S, -2 * UNITS_S))
                    sp.sem_inc(sp_met, 1)
                if batch.loop is None and batch.offset < NBUF:
                    sp.wait_ge(stacks_set, STACK_INIT)
                b = batch.buf
                by_head = parts_dram.rearrange("(p two d) s t -> two (d s) p t", two=2, d=D)
                for par in range(2):
                    r = slice(par * ROWS // 2, (par + 1) * ROWS // 2)
                    sp.dma_start(k_st[r, b, :, par, :], by_head[par][:, :, QC:QC + S]).then_inc(stacks_loaded, 16)
                    sp.dma_start(q_st[r, b, :, :], by_head[par][:, :, 0:QC]).then_inc(stacks_loaded, 16)
                    sp.dma_start(kc_st[r, b, :, par * SC:(par + 1) * SC],
                                 by_head[par][:, :, QC + S:COLS]).then_inc(stacks_loaded, 16)

            def shift_in(batch):
                sp.wait_ge(shift_t_ready, batch.count(1, 1))
                sp.sem_inc(sp_met, 1)
                if batch.reaches(16, 0):
                    sp.wait_ge(shift_loaded, batch.count(16, 0))
                    sp.sem_inc(sp_met, 1)
                if batch.reaches(UNITS_S, -2 * UNITS_S):
                    sp.wait_ge(scores_filled, batch.count(UNITS_S, -2 * UNITS_S))
                    sp.sem_inc(sp_met, 1)
                sp.dma_start(q_st[ROWS:KROWS, batch.buf, :, :].rearrange("r p (x t) -> r (p x) t", t=P),
                             shift_t[:, :]).then_inc(shift_loaded, 16)

            def store(batch):
                k = batch.index() if batch.loop is None else sp.snap(batch.index(), min_val=0, max_val=B - 1)
                sp.wait_ge(out_ready, batch.count(1, 1))
                sp.sem_inc(sp_met, 1)
                if batch.reaches(16, 0):
                    sp.wait_ge(out_stored, batch.count(16, 0))
                    sp.sem_inc(sp_met, 1)
                sp.dma_start(out[bass.ds(k, 1), :, :].rearrange("a (i p) c -> (a p) i c", p=P),
                             o_sb[:, :, :]).then_inc(out_stored, 16)

            pipeline(sp, SP_ORDER, {
                "local.load": load,
                "project.out": parts_out,
                "project.in": parts_in,
                "rowmax.in": shift_in,
                "tail.store": store,
            })
            sp.wait_ge(out_stored, 16 * B)

        @block.tensor
        def _(pe):
            mm = nc.tensor.matmul
            pe.wait_ge(local_weights_loaded, LOCAL_WEIGHTS)

            def bias_of_projection():
                pe.wait_ge(weights_loaded, WEIGHTS)
                pe.wait_ge(bv_ready, 1)
                mm(bank_t[:, 0:E], bv_wide[:, :], w2_sb[:, 4, :], start=True, stop=True).then_inc(bp_made, 1)
                pe.wait_ge(weights_ready, 2)

            def local_qk(batch):
                b = batch.buf
                pe.wait_ge(x_loaded, batch.count(64, 64))
                if batch.reaches(1, 0):
                    pe.wait_ge(probs_t_ready, batch.count(1, 0))
                mm(bank_l[:, 0:S], w1_sb[:, 0, :], xt_sb[:, b, :], start=True, stop=True)
                mm(bank_l[:, S:2 * S], w1_sb[:, 1, :], xt_sb[:, b, :], start=True, stop=True).then_inc(local_filled, 1)

            def local_v(batch):
                pe.wait_ge(qk1_ready, batch.count(2, 2))
                mm(bank_l[:, 0:S], w1_sb[:, 2, :], xt_sb[:, batch.buf, :], start=True, stop=True).then_inc(local_filled, 1)

            def local_scores(batch):
                bank = bank_l
                pe.wait_ge(v1_ready, batch.count(1, 1))
                pe.wait_ge(prod_ready, batch.count(1, 1))
                pe.wait_ge(heads0_ready, batch.count(2, 1))
                for t in range(NT):
                    for c in range(WIN):
                        mm(bank[:, c * NT * H + t * H:c * NT * H + (t + 1) * H], prod[:, c, t * P:(t + 1) * P], head_of,
                           start=(t == 0 and c == 0), stop=False, skip_group_check=True)
                    mm(bank[:, WIN * NT * H + t * H:WIN * NT * H + (t + 1) * H], q1[:, t * P:(t + 1) * P], k0_heads[:, :],
                       start=False, stop=False, skip_group_check=True)
                pe.wait_ge(heads0_ready, batch.count(2, 2))
                mm(bank[:, S:2 * S], q0_heads[:, :], k1[:, 2:2 + S], start=False, stop=True,
                   skip_group_check=True).then_inc(local_filled, 1)
                if batch.loop is None and batch.offset == 0:
                    bias_of_projection()

            def local_probs_t(batch):
                bank = bank_l
                pe.wait_ge(r0_step, batch.count(3, 1))
                pe.wait_ge(prob_mid_ready, batch.count(1, 1))
                pe.wait_ge(prob_lo_ready, batch.count(1, 1))
                out16 = bank[0:PROB_ROWS, :].bitcast(bf16)
                for j in range(4):
                    for t in range(NT):
                        last = nc.tensor.transpose(out16[:, j * S + t * P:j * S + (t + 1) * P],
                                                   prob_parts[:, t, 2 * j:2 * j + 2].rearrange("p c a h -> p (c a h)"), ident16)
                last.then_inc(local_filled, 1)

            def spread_out(batch, cands):
                for j, c in enumerate(cands):
                    last = mm(bank_p[:, j * S:(j + 1) * S], spread[:, c % 2, :], probs_t[:, batch.buf, c // 2, :],
                              start=True, stop=True)
                last.then_inc(context_filled, 1)

            def local_spread0(batch):
                if batch.reaches(2, 0):
                    pe.wait_ge(v_ready, batch.count(2, 0))
                pe.wait_ge(probs_t_ready, batch.count(1, 1))
                spread_out(batch, (0, 1))

            def local_spread2(batch):
                pe.wait_ge(pv_ready, batch.count(2, 1))
                spread_out(batch, (2, 3))

            def local_spread4(batch):
                pe.wait_ge(pv_ready, batch.count(2, 2))
                spread_out(batch, (4, 5))

            def local_spread6(batch):
                pe.wait_ge(acc_step, batch.count(2, 2))
                spread_out(batch, (6,))

            def local_out(batch):
                pe.wait_ge(lctx_ready, batch.count(1, 1))
                mm(bank_p[:, 0:E], lctx[:, 0:P], w1_sb[:, 3, :], start=True, stop=True)
                mm(bank_p[:, E:2 * E], lctx[:, P:2 * P], w1_sb[:, 3, :], start=True, stop=True).then_inc(context_filled, 1)

            def local_x1t(batch):
                pe.wait_ge(x1_ready, batch.count(1, 1))
                nc.tensor.transpose(bank_p[:, 0:P], x1[:, batch.buf, 0, :], ident)
                nc.tensor.transpose(bank_p[:, P:2 * P], x1[:, batch.buf, 1, :], ident).then_inc(context_filled, 1)

            def project_q(batch):
                b = batch.buf
                pe.wait_ge(x1t_ready, batch.count(1, 1))
                mm(bank_p[:, 0:S], w2_sb[:, 0, :], x1t[:, b, :], start=True, stop=True)
                mm(bank_p[:, S:2 * S], w2_sb[:, 3, :], x1t[:, b, :], start=True, stop=True).then_inc(project_filled, 1)

            def project_k(batch):
                b = batch.buf
                pe.wait_ge(full_ready, batch.count(4, 2))
                mm(bank_p[:, 0:S], w2_sb[:, 1, :], x1t[:, b, :], start=True, stop=True)
                mm(bank_p[:, S:S + SC], wck_sb[:, :], ctxt_sb[:, b, 0:SC], start=True, stop=True).then_inc(project_filled, 1)

            def project_v(batch):
                b = batch.buf
                pe.wait_ge(full_ready, batch.count(4, 4))
                mm(bank_p[:, 0:E], x1t[:, b, 0:P], w2_sb[:, 2, :], start=True, stop=True)
                mm(bank_p[:, E:2 * E], x1t[:, b, P:2 * P], w2_sb[:, 2, :], start=True, stop=True)
                mm(bank_p[:, 2 * E:3 * E], ctxt_sb[:, b, :], wcv_sb[:, :], start=True, stop=True).then_inc(project_filled, 1)

            def rowmax_shift_t(batch):
                pe.wait_ge(shift_ready, batch.count(1, 1))
                nc.tensor.transpose(bank_m[0][:, 0:P // 2].bitcast(bf16),
                                    shift[:, :, :, :, :, :].rearrange("p a b c d e -> p (a b c d e)"),
                                    ident16).then_inc(rowmax_filled, 1)

            def rowmax_late(batch, arg):
                pair, b = int(arg), batch.buf
                if pair == 0:
                    pe.wait_ge(stacks_loaded, batch.count(96, 96))
                    if batch.reaches(1, 0):
                        pe.wait_ge(shift_t_ready, batch.count(1, 0))
                else:
                    pe.wait_ge(rowmax_read[0], batch.count(8, pair))
                bank = bank_m[0].rearrange("p (v k) -> p v k", v=2)
                mm(bank[:, :, :], q_st[0:ROWS, b, pair, P:2 * P], k_st[0:ROWS, b, pair, :, :], start=True, stop=False)
                mm(bank[:, :, P:2 * P], ident16, causal_q.unsqueeze(1).broadcast_to([P, 2, P]), start=False, stop=True,
                   ).then_inc(rowmax_filled, 1)

            def rowmax_early(batch, arg):
                pair, b = int(arg), batch.buf
                pe.wait_ge(rowmax_read[1], batch.count(8, pair))
                bank = bank_m[1]
                own = bank[:, 0:2 * P].rearrange("p (v k) -> p v k", v=2)
                mm(own, q_st[0:ROWS, b, pair, 0:P], k_st[0:ROWS, b, pair, :, 0:P], start=True, stop=False)
                mm(own, ident16, causal_q.unsqueeze(1).broadcast_to([P, 2, P]), start=False, stop=True)
                for t in range(NT):
                    last = mm(bank[:, 2 * P + t * P:2 * P + (t + 1) * P], q_st[0:ROWS, b, pair, S + t * P:S + (t + 1) * P],
                              kc_st[0:ROWS, b, pair, :], start=True, stop=True)
                last.then_inc(rowmax_filled, 1)

            def attend(batch, arg):
                u, b = int(arg), batch.buf
                if u == 0:
                    pe.wait_ge(stacks_loaded, batch.count(96, 96))
                    pe.wait_ge(shift_loaded, batch.count(16, 16))
                if batch.reaches(UNITS_S, u - 1):
                    pe.wait_ge(exp_done, batch.count(UNITS_S, u - 1))
                bank = bank_s[u % 2]
                if u % 5 < 4:
                    pair, v = divmod(u // 5 * 4 + u % 5, 2)
                    mm(bank[:, 0:S], k_st[0:KROWS, b, pair, v, 0:P], q_st[0:KROWS, b, pair, 0:S], start=True, stop=True)
                    mm(bank[:, S:S + P], k_st[0:KROWS, b, pair, v, P:2 * P], q_st[0:KROWS, b, pair, P:2 * P],
                       start=True, stop=True).then_inc(scores_filled, 1)
                else:
                    for j in range(2):
                        pair = u // 5 * 2 + j
                        last = mm(bank[:, j * S:(j + 1) * S], kc_st[0:KROWS, b, pair, :], q_st[0:KROWS, b, pair, S:2 * S],
                                  start=True, stop=True)
                    last.then_inc(scores_filled, 1)

            PV_ORDER = ["self0", "cross0", "self1", "self2", "self3", "cross1"]

            def pv(batch, arg):
                u = PV_ORDER.index(arg)
                if batch.reaches(6, u):
                    pe.wait_ge(pv_emptied, batch.count(6, u))
                if u == 0:
                    pe.wait_ge(v_ready, batch.count(2, 2))
                    if batch.reaches(1, 0):
                        pe.wait_ge(res_ready[1], batch.count(1, 0))
                g, b = int(arg[-1]), batch.buf
                if arg.startswith("self"):
                    pe.wait_ge(masked, batch.count(H, 4 * g + 4))
                    for j in range(4):
                        h = 4 * g + j
                        mm(bank_v[32 * j:32 * j + 32, 0:S], v_sb[:, b, 0, h, :], p_self[:, h % RING, 0:S], start=True,
                           stop=False)
                    for j in range(4):
                        h = 4 * g + j
                        last = mm(bank_v[32 * j:32 * j + 32, P:2 * P], v_sb[:, b, 1, h, :], p_self[:, h % RING, S:S + P],
                                  start=False, stop=True)
                else:
                    pe.wait_ge(exp_done, batch.count(UNITS_S, 10 * g + 10))
                    for j in range(4):
                        pr = 4 * g + j
                        last = mm(bank_v[32 * j:32 * j + 32, 0:S], vc_sb[:, b, pr, :], p_cross[:, (pr // 2) % CRING, pr % 2, :],
                                  start=True, stop=True)
                last.then_inc(pv_filled, 1)

            def tail_self(batch, t):
                for g in range(4):
                    last = nc.tensor.transpose(bank_v[:, g * P:(g + 1) * P], y_t[:, g, t * P:(t + 1) * P], ident)
                last.then_inc(mixed_filled, 1)

            def tail_self0(batch):
                pe.wait_ge(pv_emptied, batch.count(6, 6))
                tail_self(batch, 0)

            def tail_cross(batch):
                pe.wait_ge(ys_ready, batch.count(2, 1))
                for t in range(NT):
                    for g in range(2):
                        last = nc.tensor.transpose(bank_v[:, (t * 2 + g) * P:(t * 2 + g + 1) * P],
                                                   y_t[:, 4 + g, t * P:(t + 1) * P], ident)
                last.then_inc(mixed_filled, 1)

            def tail_self1(batch):
                pe.wait_ge(yc_ready, batch.count(1, 1))
                tail_self(batch, 1)

            def tail_y(batch):
                pe.wait_ge(ys_ready, batch.count(2, 2))
                pe.wait_ge(y_ready, batch.count(1, 1))
                for t in range(NT):
                    last = nc.tensor.transpose(bank_v[:, t * P:(t + 1) * P], y[:, t, :], ident)
                last.then_inc(mixed_filled, 1)

            def tail_proj(batch):
                pe.wait_ge(yt_ready, batch.count(1, 1))
                for t in range(NT):
                    last = mm(bank_v[:, t * E:(t + 1) * E], yt[:, t * P:(t + 1) * P], w2_sb[:, 4, :], start=True, stop=True)
                last.then_inc(mixed_filled, 1)

            def tail_x2t(batch):
                if batch.loop is None and batch.offset == 0:
                    pe.wait_ge(bp_ready, 1)
                if batch.reaches(1, 0):
                    pe.wait_ge(res_ready[2], batch.count(1, 0))
                pe.wait_ge(x2_ready, batch.count(1, 1))
                for t in range(NT):
                    last = nc.tensor.transpose(bank_t[:, t * P:(t + 1) * P], x2[:, batch.buf, t, :], ident)
                last.then_inc(tail_filled, 1)

            def gate_up(i):
                mm(bank_t[:, 0:S], wgu_sb[:, i * P:(i + 1) * P], x2t[:, :], start=True, stop=True)
                mm(bank_t[:, S:2 * S], wgu_sb[:, HID + i * P:HID + (i + 1) * P], x2t[:, :], start=True,
                   stop=True).then_inc(tail_filled, 1)

            def tail_up0(batch):
                pe.wait_ge(x2t_ready, batch.count(1, 1))
                gate_up(0)

            def tail_up1(batch):
                pe.wait_ge(hid_ready, batch.count(3, 1))
                gate_up(1)

            def tail_up2(batch):
                pe.wait_ge(hid_ready, batch.count(3, 2))
                gate_up(2)

            def tail_down(batch):
                pe.wait_ge(hid_ready, batch.count(3, 3))
                for t in range(NT):
                    for c in range(3):
                        last = mm(bank_t[:, t * E:(t + 1) * E], hid[:, c, t * P:(t + 1) * P], wd_sb[:, c, :],
                                  start=(c == 0), stop=(c == 2))
                last.then_inc(tail_filled, 1)

            pipeline(pe, PE_ORDER, {
                "local.qk": local_qk,
                "local.v": local_v,
                "local.scores": local_scores,
                "local.probs_t": local_probs_t,
                "local.spread0": local_spread0,
                "local.spread2": local_spread2,
                "local.spread4": local_spread4,
                "local.spread6": local_spread6,
                "local.out": local_out,
                "local.x1t": local_x1t,
                "project.q": project_q,
                "project.k": project_k,
                "project.v": project_v,
                "late": rowmax_late,
                "early": rowmax_early,
                "rowmax.shift_t": rowmax_shift_t,
                "attend": attend,
                "pv": pv,
                "tail.self0": tail_self0,
                "tail.cross": tail_cross,
                "tail.self1": tail_self1,
                "tail.y": tail_y,
                "tail.proj": tail_proj,
                "tail.x2t": tail_x2t,
                "tail.up0": tail_up0,
                "tail.up1": tail_up1,
                "tail.up2": tail_up2,
                "tail.down": tail_down,
            })

        @block.scalar
        def _(act):
            A = nc.scalar.activation
            act.wait_ge(local_weights_loaded, LOCAL_WEIGHTS)
            act.wait_ge(pads_set, 8)

            def local_qk(batch):
                act.wait_ge(local_filled, batch.count(UNITS_L, 1))
                A(q1[:, :], bank_l[:, 0:S], ACT.Identity, bias=cols[:, 0:1]).then_inc(qk1_ready, 1)
                A(k1[:, 2:2 + S], bank_l[:, S:2 * S], ACT.Identity, bias=cols[:, 1:2]).then_inc(qk1_ready, 1)

            def local_v(batch):
                act.wait_ge(local_filled, batch.count(UNITS_L, 2))
                A(v1[:, batch.buf, 2:2 + S], bank_l[:, 0:S], ACT.Identity, bias=cols[:, 2:3],
                  accum_out=v1_sum[:, batch.buf:batch.buf + 1]).then_inc(v1_ready, 1)

            def local_exp(batch):
                act.wait_ge(lneg_ready, batch.count(1, 1))
                A(lexp[:, :, :], lneg[:, :, :], ACT.Exp, scale=-1.0).then_inc(lexp_ready, 1)

            def local_exp_row0(batch):
                act.wait_ge(r0max_ready, batch.count(1, 1))
                A(r0exp[:, :], r0v[:, :], ACT.Exp, bias=r0max[:, :], accum_out=r0sum[:, :]).then_inc(r0exp_ready, 1)

            def local_probs_t(batch):
                act.wait_ge(local_filled, batch.count(UNITS_L, 4))
                A(probs_t[:, batch.buf, :, :].rearrange("r j t -> r (j t)"), bank_l[0:PROB_ROWS, :].bitcast(bf16), ACT.Identity
                  ).then_inc(probs_t_ready, 1)

            def local_row0_num(batch):
                act.wait_ge(r0pv_ready, batch.count(1, 1))
                A(r0all[:, :], r0pv[:, :], ACT.Identity, accum_out=r0num[:, batch.buf:batch.buf + 1]).then_inc(r0num_ready, 1)

            def local_prob_hi(batch):
                act.wait_ge(probs_ready, batch.count(1, 1))
                A(prob_parts[:, :, 0:CAND + 1, 0, :], probs[:, :, :, :], ACT.Identity).then_inc(prob_hi_ready, 1)

            def local_prob_mid(batch):
                act.wait_ge(prob_rest_ready, batch.count(1, 1))
                A(prob_parts[:, :, 0:CAND + 1, 1, :], prob_rest[:, :, :, :], ACT.Identity).then_inc(prob_mid_ready, 1)

            def local_x1t(batch):
                act.wait_ge(context_filled, batch.count(UNITS_C, 6))
                A(x1t[:, batch.buf, :], bank_p[:, 0:S], ACT.Identity).then_inc(x1t_ready, 1)

            def project_q(batch):
                if batch.reaches(1, 0):
                    act.wait_ge(rest_ready, batch.count(1, 0))
                act.wait_ge(project_filled, batch.count(UNITS_P, 1))
                A(full[:, 0:S], bank_p[:, 0:S], ACT.Identity, bias=cols[:, 3:4]).then_inc(full_ready, 1)
                A(full[:, S:QC], bank_p[:, S:2 * S], ACT.Identity, bias=cols[:, 5:6]).then_inc(full_ready, 1)

            def project_k(batch):
                act.wait_ge(project_filled, batch.count(UNITS_P, 2))
                A(full[:, QC:QC + S], bank_p[:, 0:S], ACT.Identity, bias=cols[:, 4:5]).then_inc(full_ready, 1)
                A(full[:, QC + S:COLS], bank_p[:, S:S + SC], ACT.Identity, bias=cols[:, 6:7]).then_inc(full_ready, 1)

            def project_hi(batch):
                if batch.reaches(96, 0):
                    act.wait_ge(parts_written, batch.count(96, 0))
                act.wait_ge(full_ready, batch.count(4, 4))
                A(parts[:, 0, :], full[:, :], ACT.Identity).then_inc(hi_ready, 1)

            def project_v(batch):
                b = batch.buf
                if batch.reaches(6, -12):
                    act.wait_ge(pv_filled, batch.count(6, -12))
                act.wait_ge(project_filled, batch.count(UNITS_P, 3))
                A(v_sb[:, b, :, :, 0:D], bank_p[:, 0:2 * E].rearrange("p (t h d) -> p t h d", t=NT, d=D),
                  ACT.Identity).then_inc(v_ready, 1)
                heads = bank_p[:, 2 * E:3 * E].rearrange("p (q two d) -> p q two d", two=2, d=D)
                A(vc_sb[0:SC, b, :, 0:D], heads[0:SC, :, 0, :], ACT.Identity)
                A(vc_sb[SC:2 * SC, b, :, D + 1:2 * D + 1], heads[SC:2 * SC, :, 1, :], ACT.Identity
                  ).then_inc(v_ready, 1)

            def project_mid(batch):
                act.wait_ge(rest_ready, batch.count(1, 1))
                A(parts[:, 1, :], rest[:, :], ACT.Identity).then_inc(mid_ready, 1)

            def attend(batch, arg):
                u = int(arg)
                g, r = divmod(u, 5)
                if r == 0:
                    before = [-2, -1, 1, 3][g]
                    if batch.reaches(6, before):
                        act.wait_ge(pv_filled, batch.count(6, before))
                if r == 4 and g % 2 == 0:
                    before = [-4, 0][g // 2]
                    if batch.reaches(6, before):
                        act.wait_ge(pv_filled, batch.count(6, before))
                act.wait_ge(scores_filled, batch.count(UNITS_S, u + 1))
                if r < 4:
                    A(p_self[:, (4 * g + r) % RING, :], bank_s[u % 2][:, 0:3 * P], ACT.Exp, scale=SCALE).then_inc(exp_done, 1)
                else:
                    A(p_cross[:, g % CRING, :, :].rearrange("p a q -> p (a q)"), bank_s[u % 2][:, :], ACT.Exp,
                      scale=SCALE).then_inc(exp_done, 1)

            PV_ORDER = ["self0", "cross0", "self1", "self2", "self3", "cross1"]

            def pv(batch, arg):
                u = PV_ORDER.index(arg)
                g = int(arg[-1]) + (4 if arg.startswith("cross") else 0)
                act.wait_ge(pv_filled, batch.count(6, u + 1))
                A(y_t[:, g, :], bank_v[:, 0:S], ACT.Identity).then_inc(pv_emptied, 1)

            def tail_y(batch):
                act.wait_ge(mixed_filled, batch.count(5, 4))
                A(yt[:, :], bank_v[:, 0:S], ACT.Identity).then_inc(yt_ready, 1)

            def tail_x2t(batch):
                act.wait_ge(tail_filled, batch.count(UNITS_T, 1))
                A(x2t[:, :], bank_t[:, 0:S], ACT.Identity).then_inc(x2t_ready, 1)

            def tail_up(batch, arg):
                i = int(arg)
                act.wait_ge(tail_filled, batch.count(UNITS_T, 2 + i))
                A(th[:, i, :], bank_t[:, 0:S], ACT.Tanh, scale=0.5).then_inc(tanh_ready, 1)

            pipeline(act, ACT_ORDER, {
                "local.qk": local_qk,
                "local.v": local_v,
                "local.exp": local_exp,
                "local.exp_row0": local_exp_row0,
                "local.prob_hi": local_prob_hi,
                "local.prob_mid": local_prob_mid,
                "local.probs_t": local_probs_t,
                "local.row0_num": local_row0_num,
                "local.x1t": local_x1t,
                "project.q": project_q,
                "project.k": project_k,
                "project.v": project_v,
                "project.hi": project_hi,
                "project.mid": project_mid,
                "attend": attend,
                "pv": pv,
                "tail.y": tail_y,
                "tail.x2t": tail_x2t,
                "up": tail_up,
            })

        @block.vector
        def _(dve):
            V = nc.vector
            V.memset(k1[:, :], 0.0).then_inc(pads_set, 1)
            V.memset(v1[:, :, :], 0.0).then_inc(pads_set, 1)
            V.memset(prob_parts[:, :, :, :, :], 0.0).then_inc(pads_set, 1)
            V.memset(v_sb[:, :, :, :, :], 0.0).then_inc(zeros_set, 1)
            V.memset(vc_sb[:, :, :, :], 0.0).then_inc(zeros_set, 1)
            V.memset(small[:, 0:2], EPS).then_inc(pads_set, 1)
            V.memset(small[:, 2:4], -0.5).then_inc(pads_set, 1)
            dve.wait_ge(zeros_set, 2)
            V.memset(v_sb[:, :, :, :, D:D + 1], 1.0).then_inc(pads_set, 1)
            V.memset(vc_sb[0:SC, :, :, D:D + 1], 1.0).then_inc(pads_set, 1)
            V.memset(vc_sb[SC:2 * SC, :, :, 2 * D + 1:2 * D + 2], 1.0).then_inc(pads_set, 1)
            dve.wait_ge(local_weights_loaded, LOCAL_WEIGHTS)
            V.tensor_tensor(bv_both[:, :], cols[:, 7:8], cols[:, 8:9], ALU.add).then_inc(bv_made, 1)
            dve.wait_ge(bv_made, 1)
            V.tensor_copy(bv_wide[:, :], bv_both[:, 0:1].broadcast_to([P, P])).then_inc(bv_ready, 1)

            def dequantise():
                dve.wait_ge(weights_loaded, WEIGHTS)
                V.tensor_scalar(wgu_sb[:, :], wgu_int[:, :], 1.0 / 127.0, None, ALU.mult).then_inc(weights_ready, 1)
                V.tensor_scalar(wd_sb[:, :, :], wd_int[:, :, :], 1.0 / 127.0, None, ALU.mult).then_inc(weights_ready, 1)

            def bn(batch, which, res):
                dve.wait_ge(res_ready[which], batch.count(1, 1))
                for t in range(NT):
                    V.bn_stats(stats[which][:, t, :], res[:, t, :]).then_inc(stats_ready[which], 1)
                dve.wait_ge(stats_ready[which], batch.count(NT, NT))
                dve.sem_inc(dve_met, 1)
                for t in range(NT):
                    V.bn_aggr(mv[which][:, t, :], stats[which][:, t, :]).then_inc(mv_ready[which], 1)

            def normalise(batch, which, res, dst, done):
                dve.wait_ge(rstd_ready[which], batch.count(1, 1))
                for t in range(NT):
                    last = V.tensor_scalar(dst[:, t, :], res[:, t, :], mv[which][:, t, 0:1], rstd[which][:, t:t + 1],
                                           ALU.subtract, ALU.mult)
                last.then_inc(done, 1)

            def local_products(batch):
                dve.wait_ge(qk1_ready, batch.count(2, 2))
                V.tensor_scalar(k0_heads[:, :], head_of, k1[:, 2:3], None, ALU.mult).then_inc(heads0_ready, 1)
                V.tensor_scalar(q0_heads[:, :], same_head, q1[:, 0:1], None, ALU.mult).then_inc(heads0_ready, 1)
                if batch.loop is None and batch.offset == 0:
                    dequantise()

            def local_scores(batch):
                dve.wait_ge(local_filled, batch.count(UNITS_L, 3))
                flat = lambda t: t[:, :, :].rearrange("p c x -> p (c x)")
                n = CAND * NT * H
                V.scalar_tensor_tensor(flat(lsc), bank_l[:, 0:n], SCALE, cand_bias[:, :], ALU.mult, ALU.add
                                       ).then_inc(lsc_step, 1)
                V.scalar_tensor_tensor(r0s[:, :], bank_l[:, S:2 * S], SCALE, row0_bias[:, :], ALU.mult, ALU.add
                                       ).then_inc(r0_step, 1)

            def local_max(batch):
                dve.wait_ge(lsc_step, batch.count(6, 1))
                V.tensor_reduce(lmax[:, :], lsc[:, :, :].rearrange("p c x -> p x c"), X, ALU.max).then_inc(lsc_step, 1)
                dve.wait_ge(r0_step, batch.count(3, 1))
                V.tensor_scalar(r0g[:, :], r0s[:, :], 0.0, NEG, ALU.is_lt, ALU.mult).then_inc(r0_step, 1)
                dve.wait_ge(lsc_step, batch.count(6, 2))
                V.tensor_scalar(lmax[:, :], lmax[:, :], 0.0, None, ALU.max).then_inc(lsc_step, 1)
                dve.wait_ge(r0_step, batch.count(3, 2))
                V.scalar_tensor_tensor(r0v[:, :], r0s[:, :], 0.0, r0g[:, :], ALU.max, ALU.add).then_inc(r0_step, 1)
                dve.wait_ge(lsc_step, batch.count(6, 3))
                V.tensor_tensor(lneg[:, :, :], lmax[:, :].unsqueeze(1).broadcast_to([P, CAND, NT * H]), lsc[:, :, :],
                                ALU.subtract).then_inc(lneg_ready, 1)
                dve.wait_ge(r0_step, batch.count(3, 3))
                V.tensor_reduce(r0max[:, :], r0v[:, :], X, ALU.max, negate=True).then_inc(r0max_ready, 1)

            def local_gate(batch):
                dve.wait_ge(lexp_ready, batch.count(1, 1))
                V.scalar_tensor_tensor(lgated[:, :, :], lsc[:, :, :], 0.0, lexp[:, :, :], ALU.is_ge, ALU.mult
                                       ).then_inc(lsc_step, 1)

            def local_sum(batch):
                dve.wait_ge(lsc_step, batch.count(6, 4))
                V.tensor_reduce(lsum[:, :], lgated[:, :, :].rearrange("p c x -> p x c"), X, ALU.add).then_inc(lsc_step, 1)
                dve.wait_ge(r0exp_ready, batch.count(1, 1))
                dve.wait_ge(lsc_step, batch.count(6, 5))
                V.tensor_scalar(lnone[:, :], lsum[:, :], 0.0, None, ALU.is_equal).then_inc(lsc_step, 1)
                V.reciprocal(r0rec[:, batch.buf:batch.buf + 1], r0sum[:, :]).then_inc(r0rec_ready, 1)
                dve.wait_ge(lsc_step, batch.count(6, 6))
                V.scalar_tensor_tensor(lden[:, :], lnone[:, :], float(S), lsum[:, :], ALU.mult, ALU.add).then_inc(lden_ready, 1)

            def local_probs(batch):
                dve.wait_ge(lden_ready, batch.count(1, 1))
                V.reciprocal(lrec[:, :], lden[:, :]).then_inc(lrec_ready, 1)
                dve.wait_ge(lrec_ready, batch.count(1, 1))
                th_ = lambda a: a.rearrange("p c (t h) -> p c t h", t=NT)
                V.tensor_tensor(probs[:, :, 0:CAND, :].rearrange("p t c h -> p c t h"), th_(lgated[:, :, :]),
                                th_(lrec[:, :].unsqueeze(1).broadcast_to([P, CAND, NT * H])), ALU.mult)
                V.tensor_tensor(probs[:, :, CAND, :], lnone[:, :].rearrange("p (t h) -> p t h", t=NT),
                                lrec[:, :].rearrange("p (t h) -> p t h", t=NT), ALU.mult).then_inc(probs_ready, 1)
                if batch.loop is None and batch.offset == 0:
                    dve.wait_ge(bp_made, 1)
                    V.tensor_tensor(bp_eff[:, :], bank_t[:, 0:E], rows[:, 1, :], ALU.add).then_inc(bp_ready, 1)

            def window(b, first, n):
                return bass.AP(v1[:, :, :].tensor, b * (S + WIN - 1) + first, [[NBUF * (S + WIN - 1), P], [1, n], [1, S]])

            def spread_products(batch, arg):
                u, dst = (1, pv01) if arg == "0" else (2, pv23)
                dve.wait_ge(context_filled, batch.count(UNITS_C, u))
                V.tensor_tensor(dst[:, :, :], bank_p[:, :].rearrange("p (a t) -> p a t", a=2),
                                window(batch.buf, int(arg), 2), ALU.mult).then_inc(pv_ready, 1)

            def local_spread4(batch):
                dve.wait_ge(context_filled, batch.count(UNITS_C, 3))
                V.tensor_tensor(pv4[:, :], bank_p[:, 0:S], v1[:, batch.buf, 4:4 + S], ALU.mult).then_inc(acc_step, 1)
                dve.wait_ge(acc_step, batch.count(2, 1))
                V.scalar_tensor_tensor(pv5[:, :], bank_p[:, S:2 * S], v1[:, batch.buf, 2:3], pv4[:, :], ALU.mult, ALU.add
                                       ).then_inc(acc_step, 1)

            def local_spread6(batch):
                dve.wait_ge(acc_step, batch.count(2, 2))
                dve.wait_ge(context_filled, batch.count(UNITS_C, 4))
                V.scalar_tensor_tensor(pv6[:, :], bank_p[:, 0:S], v1_sum[:, batch.buf:batch.buf + 1], pv5[:, :], ALU.mult, ALU.add
                                       ).then_inc(pvall_ready, 1)

            def local_context(batch):
                dve.wait_ge(pvall_ready, batch.count(1, 1))
                dve.wait_ge(pvsum_ready, batch.count(2, 2))
                V.tensor_tensor(lctx[:, :], pvall[:, :], pv6[:, :], ALU.add).then_inc(lctx_made, 1)
                dve.wait_ge(lctx_made, batch.count(1, 1))
                dve.wait_ge(r0rec_ready, batch.count(1, 1))
                dve.wait_ge(r0num_ready, batch.count(1, 1))
                V.tensor_tensor(lctx[:, 0:1], r0num[:, batch.buf:batch.buf + 1], r0rec[:, batch.buf:batch.buf + 1], ALU.mult).then_inc(lctx_ready, 1)

            def local_out(batch):
                dve.wait_ge(context_filled, batch.count(UNITS_C, 5))
                dve.wait_ge(xb_ready, batch.count(1, 1))
                V.tensor_tensor(res1[:, :, :], bank_p[:, 0:2 * E].rearrange("p (t c) -> p t c", t=NT), xb[:, :, :],
                                ALU.add).then_inc(res_ready[0], 1)

            def local_norm1(batch):
                if batch.reaches(1, -2):
                    dve.wait_ge(x1res_ready, batch.count(1, -2))
                normalise(batch, 0, res1, x1[:, batch.buf], x1_ready)

            def rowmax_late(batch, arg):
                pair = int(arg)
                h = slice(2 * pair, 2 * pair + 2)
                dve.wait_ge(rowmax_filled, batch.count(UNITS_M, 2 * pair + 1))
                V.tensor_reduce(rmax[:, 1, 0, h], bank_m[0][:, :].rearrange("p (v k) -> p v k", v=2), X, ALU.max
                                ).then_inc(rowmax_read[0], 1)

            def rowmax_early(batch, arg):
                pair = int(arg)
                h = slice(2 * pair, 2 * pair + 2)
                dve.wait_ge(rowmax_filled, batch.count(UNITS_M, 2 * pair + 2))
                V.tensor_reduce(rmax[:, 0, 0, h], bank_m[1][:, 0:2 * P].rearrange("p (v k) -> p v k", v=2), X, ALU.max)
                V.tensor_reduce(rmax[:, :, 1, h], bank_m[1][:, 2 * P:4 * P].rearrange("p (t v k) -> p t v k", t=NT, v=2), X,
                                ALU.max).then_inc(rowmax_read[1], 1)

            def rowmax_shift(batch):
                dve.wait_ge(rowmax_read[0], batch.count(8, 8))
                dve.wait_ge(rowmax_read[1], batch.count(8, 8))
                for v in range(2):
                    m = rmax[:, :, :, :].rearrange("p t k (q v) -> p v q k t", v=2)[:, v]
                    V.tensor_scalar(shift[:, 0, v], m, -1.0, None, ALU.mult).then_inc(shift_hi_ready, 1)
                dve.wait_ge(shift_hi_ready, batch.count(2, 2))
                for v in range(2):
                    m = rmax[:, :, :, :].rearrange("p t k (q v) -> p v q k t", v=2)[:, v]
                    V.tensor_tensor(rneg[:, v], m, shift[:, 0, v], ALU.add).then_inc(rneg_ready, 1)
                dve.wait_ge(rneg_ready, batch.count(2, 2))
                V.tensor_scalar(shift[:, 1], rneg[:, :], -1.0, None, ALU.mult).then_inc(shift_ready, 1)

            def rowmax_shift_t(batch):
                dve.wait_ge(rowmax_filled, batch.count(UNITS_M, UNITS_M))
                if batch.reaches(16, 0):
                    dve.wait_ge(shift_loaded, batch.count(16, 0))
                V.tensor_copy(shift_t[:, :], bank_m[0][:, 0:P // 2].bitcast(bf16)).then_inc(shift_t_ready, 1)

            def tail_self(batch, t):
                dve.wait_ge(mixed_filled, batch.count(5, 1 if t == 0 else 3))
                heads = bank_v[:, :].rearrange("p (h c) -> p h c", c=32)
                V.reciprocal(rec_s[:, t, :], heads[:, :, D]).then_inc(rec_step, 1)
                dve.wait_ge(rec_step, batch.count(3, 1 if t == 0 else 3))
                V.tensor_tensor(y_s[:, t, :].rearrange("p (h d) -> p h d", d=D), heads[:, :, 0:D],
                                rec_s[:, t, :].unsqueeze(2).broadcast_to([P, H, D]), ALU.mult).then_inc(ys_ready, 1)

            def tail_cross(batch):
                dve.wait_ge(mixed_filled, batch.count(5, 2))
                pairs = bank_v[:, :].rearrange("p (q c) -> p q c", c=32)[:, :, 0:2 * (D + 1)].rearrange(
                    "p q (v c) -> p q v c", v=2)
                V.reciprocal(rec_c[:, :, :], pairs[:, :, :, D]).then_inc(rec_step, 1)
                dve.wait_ge(rec_step, batch.count(3, 2))
                V.tensor_tensor(y_c[:, :, :].rearrange("p q (v d) -> p q v d", v=2), pairs[:, :, :, 0:D],
                                rec_c[:, :, :].unsqueeze(3).broadcast_to([P, NT * PAIRS, 2, D]), ALU.mult).then_inc(yc_ready, 1)

            def tail_res2(batch):
                dve.wait_ge(mixed_filled, batch.count(5, 5))
                dve.wait_ge(x1res_ready, batch.count(1, 1))
                V.tensor_tensor(res2[:, :, :], bank_v[:, 0:2 * E].rearrange("p (t c) -> p t c", t=NT), x1res[:, batch.buf], ALU.add
                                ).then_inc(res_ready[1], 1)

            def tail_res3(batch):
                dve.wait_ge(tail_filled, batch.count(UNITS_T, 5))
                V.tensor_tensor(res3[:, :, :], bank_t[:, 0:2 * E].rearrange("p (t c) -> p t c", t=NT), x2[:, batch.buf], ALU.add
                                ).then_inc(res_ready[2], 1)

            def tail_up(batch, arg):
                i = int(arg)
                dve.wait_ge(tanh_ready, batch.count(3, i + 1))
                V.scalar_tensor_tensor(ga[:, i, :], th[:, i, :], 1.0, bank_t[:, 0:S], ALU.add, ALU.mult).then_inc(gate_ready, 1)
                dve.wait_ge(gate_ready, batch.count(3, i + 1))
                V.scalar_tensor_tensor(hid[:, i, :], ga[:, i, :], 0.5, bank_t[:, S:2 * S], ALU.mult, ALU.mult
                                       ).then_inc(hid_ready, 1)

            def tail_norm3(batch):
                if batch.reaches(16, 0):
                    dve.wait_ge(out_stored, batch.count(16, 0))
                normalise(batch, 2, res3, o_sb, out_ready)

            pipeline(dve, DVE_ORDER, {
                "local.products": local_products,
                "local.scores": local_scores,
                "local.max": local_max,
                "local.gate": local_gate,
                "local.sum": local_sum,
                "local.probs": local_probs,
                "spread": spread_products,
                "local.spread4": local_spread4,
                "local.spread6": local_spread6,
                "local.context": local_context,
                "local.res": local_out,
                "local.stats": lambda batch: bn(batch, 0, res1),
                "local.norm": local_norm1,
                "late": rowmax_late,
                "early": rowmax_early,
                "rowmax.shift": rowmax_shift,
                "rowmax.shift_t": rowmax_shift_t,
                "tail.self0": lambda batch: tail_self(batch, 0),
                "tail.cross": tail_cross,
                "tail.self1": lambda batch: tail_self(batch, 1),
                "tail.res2": tail_res2,
                "tail.stats2": lambda batch: bn(batch, 1, res2),
                "tail.norm2": lambda batch: normalise(batch, 1, res2, x2[:, batch.buf], x2_ready),
                "up": tail_up,
                "tail.res3": tail_res3,
                "tail.stats3": lambda batch: bn(batch, 2, res3),
                "tail.norm3": tail_norm3,
            })

        @block.gpsimd
        def _(pool):
            TT = nc.gpsimd.tensor_tensor
            pool.wait_ge(local_weights_loaded, LOCAL_WEIGHTS)
            pool.wait_ge(pads_set, 8)

            def rsqrt(batch, which):
                pool.wait_ge(mv_ready[which], batch.count(NT, NT))
                TT(veps[which][:, :], mv[which][:, :, 1], small[:, 0:2], ALU.add).then_inc(veps_ready[which], 1)
                pool.wait_ge(veps_ready[which], batch.count(1, 1))
                TT(rstd[which][:, :], veps[which][:, :], small[:, 2:4], ALU.pow).then_inc(rstd_ready[which], 1)

            def local_xb(batch):
                pool.wait_ge(x_loaded, batch.count(64, 64))
                TT(xb[:, :, :], x_sb[:, batch.buf, :, :], rows[:, 0, :].unsqueeze(1).broadcast_to([P, NT, E]), ALU.add
                   ).then_inc(xb_ready, 1)

            def local_products(batch):
                pool.wait_ge(qk1_ready, batch.count(2, 2))
                TT(prod[:, :, :], bass.AP(k1[:, :].tensor, 0, [[S + WIN - 1, P], [1, WIN], [1, S]]),
                   q1[:, :].unsqueeze(1).broadcast_to([P, WIN, S]), ALU.mult).then_inc(prod_ready, 1)

            def local_prob_rest(batch):
                pool.wait_ge(prob_hi_ready, batch.count(1, 1))
                TT(prob_rest[:, :, :, :], probs[:, :, :, :], prob_parts[:, :, 0:CAND + 1, 0, :], ALU.subtract
                   ).then_inc(prob_rest_ready, 1)

            def local_prob_lo(batch):
                pool.wait_ge(prob_mid_ready, batch.count(1, 1))
                TT(prob_parts[:, :, 0:CAND + 1, 2, :], prob_rest[:, :, :, :], prob_parts[:, :, 0:CAND + 1, 1, :], ALU.subtract
                   ).then_inc(prob_lo_ready, 1)

            def local_row0_products(batch):
                pool.wait_ge(v1_ready, batch.count(1, 1))
                pool.wait_ge(r0exp_ready, batch.count(1, 1))
                TT(r0pv[:, :], r0exp[:, :], v1[:, batch.buf, 2:2 + S], ALU.mult).then_inc(r0pv_ready, 1)

            def local_context(batch):
                pool.wait_ge(pv_ready, batch.count(2, 2))
                TT(pvsum[:, :, :], pv01[:, :, :], pv23[:, :, :], ALU.add).then_inc(pvsum_ready, 1)
                pool.wait_ge(pvsum_ready, batch.count(2, 1))
                TT(pvall[:, :], pvsum[:, 0, :], pvsum[:, 1, :], ALU.add).then_inc(pvsum_ready, 1)

            def project_rest(batch):
                pool.wait_ge(hi_ready, batch.count(1, 1))
                TT(rest[:, :], full[:, :], parts[:, 0, :], ALU.subtract).then_inc(rest_ready, 1)

            def project_lo(batch):
                pool.wait_ge(mid_ready, batch.count(1, 1))
                TT(parts[:, 2, :], rest[:, :], parts[:, 1, :], ALU.subtract).then_inc(lo_ready, 1)

            def rowmax_x1res(batch):
                if batch.loop is None and batch.offset == 0:
                    pool.wait_ge(bp_ready, 1)
                pool.wait_ge(x1_ready, batch.count(1, 1))
                if batch.reaches(1, -2):
                    pool.wait_ge(res_ready[1], batch.count(1, -2))
                TT(x1res[:, batch.buf, :, :], x1[:, batch.buf, :, :], bp_eff[:, :].unsqueeze(1).broadcast_to([P, NT, E]),
                   ALU.add).then_inc(x1res_ready, 1)

            def mask(batch, arg):
                h = int(arg)
                pool.wait_ge(exp_done, batch.count(UNITS_S, h // 4 * 5 + h % 4 + 1))
                pool.sem_inc(pool_met, 1)
                diag = p_self[:, h % RING, :].rearrange("p (a q) -> p a q", q=P)[:, 0:3:2, :]
                nc.gpsimd.affine_select(out=diag, in_=diag, compare_op=ALU.is_ge, fill=0.0, base=0,
                                        pattern=[[0, 2], [1, P]], channel_multiplier=-1).then_inc(masked, 1)

            def tail_y(batch):
                pool.wait_ge(ys_ready, batch.count(2, 2))
                pool.wait_ge(yc_ready, batch.count(1, 1))
                TT(y[:, :, :].rearrange("p t c -> p (t c)"), y_s[:, :, :].rearrange("p t c -> p (t c)"),
                   y_c[:, :, :].rearrange("p q c -> p (q c)"), ALU.add).then_inc(y_ready, 1)

            pipeline(pool, POOL_ORDER, {
                "local.xb": local_xb,
                "local.products": local_products,
                "local.prob_rest": local_prob_rest,
                "local.prob_lo": local_prob_lo,
                "local.row0_products": local_row0_products,
                "local.context": local_context,
                "local.rstd": lambda batch: rsqrt(batch, 0),
                "project.rest": project_rest,
                "project.lo": project_lo,
                "rowmax.x1res": rowmax_x1res,
                "mask": mask,
                "tail.y": tail_y,
                "tail.rstd2": lambda batch: rsqrt(batch, 1),
                "tail.rstd3": lambda batch: rsqrt(batch, 2),
            })


def constants():
    import numpy as np
    head = np.arange(P) // D
    f32c = np.concatenate([np.eye(P), head[:, None] == head[None, :], head[:, None] == np.arange(H)[None, :]],
                          1).astype(np.float32)

    def pos_bias(diff):
        diff = diff.astype(np.float32)
        return (np.exp(np.float32(-0.5) * (diff / np.float32(2.0)) ** 2)
                + np.cos(np.float32(2.0 * np.pi) * diff / np.float32(401.0))).astype(np.float32)

    tok = np.arange(NT)[None, :] * P + np.arange(P)[:, None]
    cand = np.zeros((P, CAND, NT, H), np.float32)
    for c in range(WIN):
        key = tok + c - WIN // 2
        ok = (key >= 1) & (key < S)
        cand[:, c] = np.where(ok, pos_bias(tok - key), np.float32(-1e30))[:, :, None]
    cand[:, WIN] = pos_bias(tok)[:, :, None]
    row0 = np.broadcast_to(pos_bias(-np.arange(S))[None, :], (P, S))
    bias = np.ascontiguousarray(np.concatenate([cand.reshape(P, -1), row0], 1))
    spread = np.zeros((2, 3, H, 2, P), np.float32)
    for c in range(2):
        spread[c, :, :, c, :] = head[None, :] == np.arange(H)[:, None]
    spread = spread.reshape(PROB_ROWS, 2, P)
    i, j = np.arange(P)[:, None], np.arange(P)[None, :]
    b16 = np.concatenate([np.eye(P), np.where(j <= i, 0.0, -3e38)], 1)
    rows = np.zeros((KROWS, 2 * S + 2 * SC), np.float32)
    for part in range(2):
        for par in range(2):
            r = ROWS + 2 * part + par
            rows[r, par * S:(par + 1) * S] = 1.0
            rows[r, 2 * S + par * SC:2 * S + (par + 1) * SC] = 1.0
    bits = lambda v: (np.ascontiguousarray(v, np.float32).view(np.uint32) >> 16).astype(np.uint16)
    return f32c, bias, bits(spread), bits(b16), bits(rows)


def kernel(**inputs):
    import numpy as np
    import concourse.bacc as bacc
    from concourse.bass_utils import run_bass_kernel_spmd

    a = {k: np.asarray(v) for k, v in inputs.items()}
    local = lambda n: a["L0_attn_" + n]
    cross = lambda n: a["L0_xattn_" + n]
    k_f32, k_bias, k_spread, k_bf16, k_rows = constants()
    arrays = {
        "x": a["x"],
        "xt": a["x"].transpose(0, 2, 1),
        "ctxt": a["ctx_512"].transpose(0, 2, 1),
        "w1": np.stack([local(n).T for n in ("wq", "wk", "wv", "wo")], 1),
        "w2": np.stack([cross(n) for n in ("Wq", "Wk", "Wv", "Wcq", "Wp")], 1),
        "wck": cross("Wck"),
        "wcv": cross("Wcv"),
        "bias_cols": np.stack([local("bq"), local("bk"), local("bv"), cross("bq"), cross("bk"), cross("bcq"),
                               cross("bck"), cross("bv"), cross("bcv")], 1),
        "bias_rows": np.stack([local("bo"), cross("bp")], 0),
        "wgu": np.concatenate([a["L0_ffn_w_gate"].T, a["L0_ffn_w_up"].T], 1),
        "wd": a["L0_ffn_w_down"].T.reshape(3, P, E).transpose(1, 0, 2),
        "k_f32": k_f32, "k_bias": k_bias, "k_spread": k_spread, "k_bf16": k_bf16, "k_rows": k_rows,
    }
    arrays = {k: np.ascontiguousarray(v) for k, v in arrays.items()}
    nc = bacc.Bacc("TRN2", target_bir_lowering=False, num_devices=1)
    args = {k: nc.dram_tensor(k, list(v.shape), mybir.dt.from_np(v.dtype), kind="ExternalInput").ap()
            for k, v in arrays.items()}
    out = nc.dram_tensor("out", [B, S, E], mybir.dt.float32, kind="ExternalOutput").ap()
    decoder_layer(nc, out=out, **args)
    r = run_bass_kernel_spmd(nc, [arrays], core_ids=[0])
    return r.results[0]["out"]
```
